# Optimizing a Trainium2 kernel written in Bass

```python
import numpy as np
import jax
import jax.numpy as jnp

def _softmax(x, axis=-1):
    return jax.nn.softmax(x, axis=axis)

def _gelu(x):
    return jax.nn.gelu(x, approximate=True)

def _silu(x):
    return jax.nn.silu(x)

def _sigmoid(x):
    return jax.nn.sigmoid(x)

def _layernorm(x, axis=-1, eps=1e-05):
    m = jnp.mean(x, axis=axis, keepdims=True)
    v = jnp.var(x, axis=axis, keepdims=True)
    return (x - m) / jnp.sqrt(v + eps)

def _scatter_add(tgt, idx, src, axis=0):
    return tgt.at[idx].add(src)

def _segment_sum(src, seg, n):
    return jax.ops.segment_sum(src, seg, n)
kernel_name = 'mk_gnn_ffn_d1_gnn_r8_fff848'

def setup_inputs(seed: int=0):
    np.random.seed(seed)
    _w = jnp.asarray

    def _rec_inputs():
        import jax
        import jax.numpy as jnp
        _gk = jax.random.key(seed)
        x = -0.0002117 + 1 * jax.random.normal(jax.random.fold_in(_gk, 1), (6250, 512), jnp.float32)
        _s = jax.random.randint(jax.random.fold_in(_gk, 2), (50000,), 0, 6250, jnp.int32)
        _d = jax.random.randint(jax.random.fold_in(_gk, 3), (50000,), 0, 6250, jnp.int32)
        _loop = jnp.arange(6250, dtype=jnp.int32)
        src = jnp.concatenate([_s, _d, _loop])
        dst = jnp.concatenate([_d, _s, _loop])
        _o = jnp.argsort(dst, stable=True)
        src = src[_o]
        dst = dst[_o]
        return (x, src, dst)
    x, src, dst = _rec_inputs()

    def _L0_gnn_setup():
        import jax, jax.numpy as jnp
        import numpy as np
        N = 6250
        E = 100000
        D = 512

        def _gcn_conv(x, edge_index, W, b):
            n = x.shape[0]
            xw = x @ W.T
            loop = jnp.arange(n, dtype=edge_index.dtype)
            row = jnp.concatenate([edge_index[0], loop])
            col = jnp.concatenate([edge_index[1], loop])
            deg = jax.ops.segment_sum(jnp.ones_like(row, dtype=xw.dtype), col, num_segments=n)
            dinv = jnp.where(deg > 0, jax.lax.rsqrt(deg), 0.0)
            norm = dinv[row] * dinv[col]
            msgs = norm[:, None] * xw[row]
            out = jax.ops.segment_sum(msgs, col, num_segments=n)
            return out + b

        def _batch_norm(h, gamma, beta, eps=1e-05):
            mean = jnp.mean(h, axis=0)
            var = jnp.var(h, axis=0)
            return (h - mean) * jax.lax.rsqrt(var + eps) * gamma + beta
        key = jax.random.key(seed)
        k1, k2, k3, k4, k5, k6 = jax.random.split(key, 6)
        x = jax.random.normal(k1, (N, D), dtype=jnp.float32)
        edge_index = jax.random.randint(k2, (2, E), 0, N, dtype=jnp.int64)
        W = jax.random.normal(k3, (D, D), dtype=jnp.float32) * (1.0 / np.sqrt(D))
        b = jnp.zeros((D,), dtype=jnp.float32)
        gamma = jnp.ones((D,), dtype=jnp.float32)
        beta = jnp.zeros((D,), dtype=jnp.float32)
        return {'x': x, 'edge_index': edge_index, 'W': W, 'b': b, 'gamma': gamma, 'beta': beta}
    _L0_gnn_all = _L0_gnn_setup()
    _L0_gnn_in = {k: v for k, v in _L0_gnn_all.items() if k in ('W', 'b', 'gamma', 'beta')}
    del _L0_gnn_all

    def _L0_ffn_setup():
        import jax, jax.numpy as jnp
        import numpy as np
        H = 512
        F = 256
        E = 16
        SHARED = 2
        TOP_K = 4
        B, S = (2, 256)

        def _mlp(x, w1, b1, w2, b2):
            return jax.nn.gelu(x @ w1 + b1, approximate=False) @ w2 + b2
        key = jax.random.key(seed)
        ks = jax.random.split(key, 10)
        sc = 0.02
        return {'hidden_states': jax.random.normal(ks[0], (B, S, H), dtype=jnp.float32), 'gate_w': jax.random.normal(ks[1], (E, H), dtype=jnp.float32) * sc, 're_w1': jax.random.normal(ks[2], (E, H, F), dtype=jnp.float32) * sc, 're_b1': jnp.zeros((E, F), dtype=jnp.float32), 're_w2': jax.random.normal(ks[3], (E, F, H), dtype=jnp.float32) * sc, 're_b2': jnp.zeros((E, H), dtype=jnp.float32), 'se_w1': jax.random.normal(ks[4], (SHARED, H, F), dtype=jnp.float32) * sc, 'se_b1': jnp.zeros((SHARED, F), dtype=jnp.float32), 'se_w2': jax.random.normal(ks[5], (SHARED, F, H), dtype=jnp.float32) * sc, 'se_b2': jnp.zeros((SHARED, H), dtype=jnp.float32)}
    _L0_ffn_all = _L0_ffn_setup()
    _L0_ffn_in = {k: v for k, v in _L0_ffn_all.items() if k in ('gate_w', 're_w1', 're_b1', 're_w2', 're_b2', 'se_w1', 'se_b1', 'se_w2', 'se_b2')}
    del _L0_ffn_all
    return {'x': x, 'src': src, 'dst': dst, 'L0_gnn_W': _L0_gnn_in['W'], 'L0_gnn_b': _L0_gnn_in['b'], 'L0_gnn_gamma': _L0_gnn_in['gamma'], 'L0_gnn_beta': _L0_gnn_in['beta'], 'L0_ffn_gate_w': _L0_ffn_in['gate_w'], 'L0_ffn_re_w1': _L0_ffn_in['re_w1'], 'L0_ffn_re_b1': _L0_ffn_in['re_b1'], 'L0_ffn_re_w2': _L0_ffn_in['re_w2'], 'L0_ffn_re_b2': _L0_ffn_in['re_b2'], 'L0_ffn_se_w1': _L0_ffn_in['se_w1'], 'L0_ffn_se_b1': _L0_ffn_in['se_b1'], 'L0_ffn_se_w2': _L0_ffn_in['se_w2'], 'L0_ffn_se_b2': _L0_ffn_in['se_b2']}

def reference(x, src, dst, L0_gnn_W, L0_gnn_b, L0_gnn_gamma, L0_gnn_beta, L0_ffn_gate_w, L0_ffn_re_w1, L0_ffn_re_b1, L0_ffn_re_w2, L0_ffn_re_b2, L0_ffn_se_w1, L0_ffn_se_b1, L0_ffn_se_w2, L0_ffn_se_b2):
    import jax
    import jax.numpy as jnp

    def _L0_gnn_ref(x, edge_index, W, b, gamma, beta):
        import jax, jax.numpy as jnp
        import numpy as np
        N = 6250
        E = 100000
        D = 512

        def _gcn_conv(x, edge_index, W, b):
            n = x.shape[0]
            xw = x @ W.T
            loop = jnp.arange(n, dtype=edge_index.dtype)
            row = jnp.concatenate([edge_index[0], loop])
            col = jnp.concatenate([edge_index[1], loop])
            deg = jax.ops.segment_sum(jnp.ones_like(row, dtype=xw.dtype), col, num_segments=n)
            dinv = jnp.where(deg > 0, jax.lax.rsqrt(deg), 0.0)
            norm = dinv[row] * dinv[col]
            msgs = norm[:, None] * xw[row]
            out = jax.ops.segment_sum(msgs, col, num_segments=n)
            return out + b

        def _batch_norm(h, gamma, beta, eps=1e-05):
            mean = jnp.mean(h, axis=0)
            var = jnp.var(h, axis=0)
            return (h - mean) * jax.lax.rsqrt(var + eps) * gamma + beta
        identity = x
        h = _gcn_conv(x, edge_index, W, b)
        h = _batch_norm(h, gamma, beta)
        h = jax.nn.gelu(h, approximate=False)
        return h + identity

    def _L0_ffn_ref(hidden_states, gate_w, re_w1, re_b1, re_w2, re_b2, se_w1, se_b1, se_w2, se_b2):
        import jax, jax.numpy as jnp
        import numpy as np
        H = 512
        F = 256
        E = 16
        SHARED = 2
        TOP_K = 4
        B, S = (2, 256)

        def _mlp(x, w1, b1, w2, b2):
            return jax.nn.gelu(x @ w1 + b1, approximate=False) @ w2 + b2
        b, s, h = hidden_states.shape
        x = hidden_states.reshape(-1, h)
        gate_probs = jax.nn.softmax(x @ gate_w.T, axis=-1)
        top_v, top_i = jax.lax.top_k(gate_probs, TOP_K)
        top_v = jax.nn.softmax(top_v, axis=-1)
        combine = jnp.einsum('tk,tke->te', top_v, jax.nn.one_hot(top_i, E, dtype=x.dtype))
        routed = jnp.zeros_like(x)
        for e in range(E):
            routed = routed + combine[:, e:e + 1] * _mlp(x, re_w1[e], re_b1[e], re_w2[e], re_b2[e])
        shared = jnp.zeros_like(x)
        for j in range(SHARED):
            shared = shared + _mlp(x, se_w1[j], se_b1[j], se_w2[j], se_b2[j])
        shared = shared / SHARED
        return (routed + shared).reshape(b, s, h)
    edge_index = jnp.stack([src, dst])
    x = x + _L0_gnn_ref(_layernorm(x, axis=-1), edge_index, L0_gnn_W, L0_gnn_b, L0_gnn_gamma, L0_gnn_beta)
    x = x + _L0_ffn_ref(_layernorm(x, axis=-1)[None], L0_ffn_gate_w, L0_ffn_re_w1, L0_ffn_re_b1, L0_ffn_re_w2, L0_ffn_re_b2, L0_ffn_se_w1, L0_ffn_se_b1, L0_ffn_se_w2, L0_ffn_se_b2)[0]
    return x

_drawn_inputs = setup_inputs


def setup_inputs(seed=0):
    import zlib

    import numpy as np

    out = dict(_drawn_inputs(seed))
    spreads = {'L0_gnn_b': (0.0, 0.8),
     'L0_gnn_gamma': (1.0, 0.2),
     'L0_gnn_beta': (0.0, 0.1),
     'L0_ffn_re_b1': (0.0, 0.8),
     'L0_ffn_re_b2': (0.0, 0.336),
     'L0_ffn_se_b1': (0.0, 0.8),
     'L0_ffn_se_b2': (0.0, 0.1)}
    factors = {'L0_ffn_re_w1': 3.01, 'L0_ffn_re_w2': 2.817}
    for name, (base, spread) in spreads.items():
        noise = np.random.default_rng([zlib.crc32(name.encode()), seed]).standard_normal(out[name].shape)
        drawn = base * np.exp(spread * noise) if base else spread * noise
        out[name] = jnp.asarray(drawn.astype(out[name].dtype))
    for name, factor in factors.items():
        out[name] = (out[name] * factor).astype(out[name].dtype)
    return out
```

```python
from contextlib import ExitStack

import concourse.bass as bass
from concourse import mybir

F32 = mybir.dt.float32
F16 = mybir.dt.float16
I32 = mybir.dt.int32
ALU = mybir.AluOpType
ACT = mybir.ActivationFunctionType
AX = mybir.AxisListType

P = 128
N = 6250
D = 512
KD = D // P
T = -(-N // P)
NP = T * P
LAST = N - (T - 1) * P
EDGES = 106250
CHUNKS = -(-EDGES // P)
RING = 16
PACK = 4
LAG = 2 * PACK
CPART, CBLK = 128, 7
CPAD = CPART * CBLK
OH = 28
NB = CPAD // OH
GRP = 7
BIG = 1000
YS = 1024.0
EPS = 1e-5
HID = 256
KH = HID // P
EXPERTS = 16
SHARED = 2
NE = EXPERTS + SHARED
TOP = 4
SB = 2 * P
ROUTED_SB = (NP * TOP + EXPERTS * SB) // SB
SHARED_SB = -(-NP // SB)
NSB = ROUTED_SB + SHARED * SHARED_SB
RB = 2 * ROUTED_SB
WL = KD * HID
MAX_FROM, SPLIT_FROM = 2, 29
assert NSB % 2 == 0 and KH * D == WL and 2 * (SPLIT_FROM - (MAX_FROM + NE + 1)) > LAG and SPLIT_FROM + NE <= T
assert CPAD >= CHUNKS + RING - 1 and NB % 2 == 0 and T == GRP * GRP


def gnn_ffn(nc, x, src_cols, dst_cols, dst_rows, w_t, b_cols, gamma_cols, beta_cols, gate_t, w1, b1_cols, w2, b2, out):
    ytab = nc.dram_tensor("ytab", [NP, 2 * D], F16, kind="Internal").ap()
    x1tab = nc.dram_tensor("x1tab", [NP, D], F32, kind="Internal").ap()
    xntab = nc.dram_tensor("xntab", [NP, D], F32, kind="Internal").ap()
    wtab = nc.dram_tensor("wtab", [NE, P, 4 * WL], F16, kind="Internal").ap()
    btab = nc.dram_tensor("btab", [NSB * SB, D], F32, kind="Internal").ap()

    with ExitStack() as ctx:
        def sb(name, shape, dt):
            return ctx.enter_context(nc.sbuf_tensor(name, shape, dt))

        def ps(name, shape, dt):
            return ctx.enter_context(nc.psum_tensor(name, shape, dt))

        def sem(name):
            return ctx.enter_context(nc.semaphore(name))

        big = sb("big", [P, T * D], F32)
        x_all = big[:, :].rearrange("p (t d) -> p t d", d=D)
        h_t = big[:, :].rearrange("p (k n) -> p k n", k=KD)
        src_i = sb("src_i", [P, CPAD], I32)
        dst_i = sb("dst_i", [P, CPAD], I32)
        dst_f = sb("dst_f", [P, CPAD], F32)
        wspl = sb("wspl", [P, 2, 4 * WL], F16)
        wspl_flat = wspl[:, :, :].rearrange("p b n -> p (b n)")
        dst_h = wspl_flat[:, 0:CPAD]
        dst_l = wspl_flat[:, CPAD:2 * CPAD]
        tmp_i = wspl_flat[:, 2 * CPAD:4 * CPAD].bitcast(I32)
        dr_i = wspl_flat[0:CPART, 4 * CPAD:6 * CPAD].bitcast(I32).rearrange("p (b j) -> p b j", j=P)
        arena = sb("arena", [P, RING * 2 * D], F16)
        oh_l = arena[:, 0:2 * P * OH].rearrange("p (b j c) -> p b j c", b=2, c=OH)
        iota_rep = arena[:, 2 * P * OH:3 * P * OH].rearrange("p (j c) -> p j c", c=OH)
        oh_h = arena[:, 3 * P * OH:3 * P * OH + 2 * T * OH].rearrange("p (b j c) -> p b j c", b=2, c=OH)
        z = arena[:, 0:2 * GRP * D].bitcast(F32).rearrange("p (k d) -> p k d", d=D)
        yrow = arena[:, 2 * GRP * D:4 * GRP * D].rearrange("p (k d) -> p k d", d=2 * D)
        cnd_at = (3 * P + 2 * T) * OH
        cnd = arena[0:CPART, cnd_at:cnd_at + 8 * T * CBLK].bitcast(F32).rearrange("p (a t b) -> p a t b", a=4, b=CBLK)
        iota16 = sb("iota16", [P, P], F16)
        iota_t = sb("iota_t", [P, T], F32)
        tbase = sb("tbase", [P, T], F32)
        chunk_id = sb("chunk_id", [CPART, CBLK], F32)
        mn = sb("mn", [CPART, CBLK], F32)
        mx = sb("mx", [CPART, CBLK], F32)
        rng = sb("rng", [CPART, 2, T], F32)
        rcol = sb("rcol", [T, 8], F32)
        def even_slot(slot):
            return nc.s_assert_within(slot, 0, RING - 2, skip_runtime_bounds_check_because="the count of steps is even")

        rcol_i = sb("rcol_i", [T, 2], I32)
        rrow = sb("rrow", [1, 8, T], F32)
        tab = sb("tab", [1, 3, T], I32)
        tot = sb("tot", [1, 8], F32)
        toti = sb("toti", [1, 4], I32)
        ident = sb("ident", [P, P], F32)
        upper16 = sb("upper16", [P, P], F16)
        ones16 = sb("ones16", [P, P], F16)
        ident16 = sb("ident16", [P, P], F16)
        upper = sb("upper", [T, T], F32)
        ones = sb("ones", [P, P], F32)
        zero16 = sb("zero16", [1, D], F16)
        deg = sb("deg", [P, T], F32)
        mhalf = sb("mhalf", [P, T], F32)
        dinv = sb("dinv", [P, T], F32)
        dinv_ys = sb("dinv_ys", [P, T], F32)
        wraw = sb("wraw", [P, 2, 2, WL], F32)
        st6 = wraw[:, 0, 0, 0:T * 6].rearrange("p (t s) -> p t s", s=6)
        mv = sb("mv", [P, T, 2], F32)
        veps = sb("veps", [P, T], F32)
        rstd = sb("rstd", [P, T], F32)
        ysc = sb("ysc", [P, T], F32)
        ybi = sb("ybi", [P, T], F32)
        rows = arena[:, 0:RING * 2 * D].rearrange("p (k d) -> p k d", k=RING)
        idx = sb("idx", [P, RING], I32)
        sel = sb("sel", [P, RING, P], F16)
        rows_flat = arena[:, 0:RING * 2 * D]
        sel_flat = sel[:, :, :].rearrange("p k n -> p (k n)")
        yself = sb("yself", [P, 2 * D], F16)
        agg_s = sb("agg_s", [P, D], F32)
        agg_ts = sb("agg_ts", [P, KD, P], F32)
        w_sb = sb("w_sb", [P, KD, D], F32)
        bcol = sb("bcol", [P, 3, KD], F32)
        hst = sb("hst", [P, KD, T, 6], F32)
        hmv = sb("hmv", [P, KD, 2], F32)

        wmx = sb("wmx", [P, 2, NE], F32)
        wm3 = sb("wm3", [P, 4], F32)
        wmb = sb("wmb", [P, 3, P], F32)
        wex_i = sb("wex_i", [P, 8], I32)
        wex_f = sb("wex_f", [P, 8], F32)
        wex_s = sb("wex_s", [P, 8], I32)
        scl = wex_s[:, :].bitcast(F32)
        scale_w1, scale_w2, scale_h, unscale_1, unscale_2 = (scl[:, i:i + 1] for i in range(5))
        b1c = sb("b1c", [P, NE * KH], F32)
        bn_a = sb("bn_a", [P, KD], F32)
        bn_b = sb("bn_b", [P, KD], F32)
        bn_v = sb("bn_v", [P, KD], F32)
        gate = sb("gate", [P, KD, EXPERTS], F32)
        c1 = sb("c1", [P, T], F32)
        c2 = sb("c2", [P, T], F32)
        mv2 = sb("mv2", [P, 2, 2], F32)
        st2 = sb("st2", [P, 2, 6], F32)
        ve2 = sb("ve2", [P, 2], F32)
        r2 = sb("r2", [P, 2], F32)
        nb2 = sb("nb2", [P, 2], F32)
        idx4 = sb("idx4", [P, 2, TOP], I32)
        idx2 = sb("idx2", [P, 2, 2], I32)
        start_f = sb("start_f", [1, NE + 1], F32)
        start_i = sb("start_i", [1, NE + 1], I32)
        eb_i = sb("eb_i", [1, NSB], I32)

        big16 = big[:, :].bitcast(F16)

        def views(base, specs):
            at, out_views = 0, []
            for shape, dt in specs:
                size = 1
                for q in shape:
                    size *= q
                width = size if dt == F16 else 2 * size
                v = base[:, at:at + width]
                if dt != F16:
                    v = v.bitcast(dt)
                if len(shape) > 1:
                    names = "abcd"[:len(shape)]
                    v = v.rearrange("p (" + " ".join(names) + ") -> p " + " ".join(names), **dict(zip(names, shape)))
                out_views.append(v)
                at += width
            return out_views

        logits, wk, slot_i, tok_i = views(wraw[:, :, :, :].rearrange("p a b n -> p (a b n)").bitcast(F16), [
            ((T, EXPERTS), F32), ((T, TOP), F32), ((T, TOP), I32), ((2 * NSB + 2,), I32)])
        xr, x1, xn, x_ts, g_tile = views(arena, [((2, D), F32)] * 3 + [((2, KD, P), F32)] * 2)
        G = (T, EXPERTS)
        (probs, hot, tmp_a, tmp_b, cum_a, cum_b, rank_s, mask16, rev16, top_v, vec_a, vec_b, r_f, b_f, tval,
         oh_r, oh_b, iota_b, pcol, ebt, iota_sb) = views(big16, [
            (G, F32), ((TOP,) + G, F32), (G, F32), (G, F32), (G, F32), (G, F32), (G, F32), (G, F16), (G, F32), ((TOP, T), F32),
            ((TOP, T), F32), ((TOP, T), F32), ((T, TOP), F32), ((T, TOP), F32), ((T,), F32),
            ((2, P), F16), ((2, 2, RB), F16), ((RB,), F16), ((2,), F32), ((NSB, NE), F32), ((NSB,), F32)])
        (tot_e, pre_e, pre_e2, blk_e) = views(arena[:, 10240:], [((EXPERTS,), F32), ((EXPERTS,), F32), ((EXPERTS,), F32), ((EXPERTS,), I32)])
        tok_f = views(arena[:, 11264:], [((2 * NSB + 2,), F32)])[0]
        wsb, b2r, xg, xh, xl, g_s, hh, hl, y_s = views(big16, [
            ((2, 4 * WL), F16), ((NE, D), F32), ((2, D), F32), ((2, KD, P), F16), ((2, KD, P), F16),
            ((KH, SB), F32), ((KH, SB), F16), ((KH, SB), F16), ((2, 2, D), F32)])
        yk, x1r, sh_r, acc = views(big16, [((2, TOP, D), F32), ((2, D), F32), ((2, SHARED, D), F32), ((2, D), F32)])

        bank = [ps(f"bank{i}", [P, 512], F32) for i in range(8)]
        deg_ps, rt_ps = bank[0], bank[1]
        agg_b = [bank[2], bank[3]]

        def cut(b, k, w=P):
            return bank[b][:, 0:k * w].rearrange("p (k n) -> p k n", k=k)

        at_ps, ht_ps, wm_ps = cut(4, KD), cut(5, KD), cut(6, 3)

        s_wraw0 = sem("s_wraw0")
        s_wraw1 = sem("s_wraw1")
        s_wused = sem("s_wused")
        s_wlo = sem("s_wlo")
        s_wst0 = sem("s_wst0")
        s_wst1 = sem("s_wst1")
        s_wm = sem("s_wm")
        s_wmt = sem("s_wmt")
        s_mx = sem("s_mx")
        s_b1 = sem("s_b1")
        s_gate = sem("s_gate")
        s_bnv = sem("s_bnv")
        s_bnr = sem("s_bnr")
        s_bn = sem("s_bn")
        s_gelu = sem("s_gelu")
        s_xr0 = sem("s_xr0")
        s_xr1 = sem("s_xr1")
        s_u = sem("s_u")
        s_t1 = sem("s_t1")
        s_x1 = sem("s_x1")
        s_ve2 = sem("s_ve2")
        s_r2 = sem("s_r2")
        s_nb2 = sem("s_nb2")
        s_xn = sem("s_xn")
        s_t2 = sem("s_t2")
        s_xT = sem("s_xT")
        s_lg = sem("s_lg")
        s_lgc = sem("s_lgc")
        s_x1st0 = sem("s_x1st0")
        s_x1st1 = sem("s_x1st1")
        s_xnst0 = sem("s_xnst0")
        s_xnst1 = sem("s_xnst1")
        s_atab = sem("s_atab")
        s_bc = sem("s_bc")
        s_sub = sem("s_sub")
        s_exp = sem("s_exp")
        s_topv = sem("s_topv")
        s_exp2 = sem("s_exp2")
        s_mask = sem("s_mask")
        s_rank = sem("s_rank")
        s_route = sem("s_route")
        s_ohr = sem("s_ohr")
        s_inv = sem("s_inv")
        s_tok = sem("s_tok")
        s_b2 = sem("s_b2")
        s_wl0 = sem("s_wl0")
        s_wl1 = sem("s_wl1")
        s_ig = sem("s_ig")
        s_xg = sem("s_xg")
        s_t = sem("s_t")
        s_xhi = sem("s_xhi")
        s_xlo = sem("s_xlo")
        s_l1 = sem("s_l1")
        s_g = sem("s_g")
        s_hlo = sem("s_hlo")
        s_l2 = sem("s_l2")
        s_y = sem("s_y")
        s_bst0 = sem("s_bst0")
        s_bst1 = sem("s_bst1")
        s_btab = sem("s_btab")
        s_i4 = sem("s_i4")
        s_yk0 = sem("s_yk0")
        s_yk1 = sem("s_yk1")
        s_fl0 = sem("s_fl0")
        s_fl1 = sem("s_fl1")
        s_acc = sem("s_acc")
        s_ost0 = sem("s_ost0")
        s_ost1 = sem("s_ost1")
        s_wraw, s_wst, s_xr, s_x1st, s_xnst = [s_wraw0, s_wraw1], [s_wst0, s_wst1], [s_xr0, s_xr1], [s_x1st0, s_x1st1], [s_xnst0, s_xnst1]
        s_wl, s_bst, s_yk, s_fl, s_ost = [s_wl0, s_wl1], [s_bst0, s_bst1], [s_yk0, s_yk1], [s_fl0, s_fl1], [s_ost0, s_ost1]
        s_dst = sem("s_dst")
        s_whi = sem("s_whi")
        s_st2 = sem("s_st2")
        s_mv2 = sem("s_mv2")
        s_hhi = sem("s_hhi")
        s_fd = sem("s_fd")
        s_hst = sem("s_hst")
        s_src = sem("s_src")
        s_x = sem("s_x")
        s_w = sem("s_w")
        s_const = sem("s_const")
        s_cdve = sem("s_cdve")
        s_oh = sem("s_oh")
        s_ohused = sem("s_ohused")
        s_deg = sem("s_deg")
        s_degs = sem("s_degs")
        s_dinv = sem("s_dinv")
        s_veps = sem("s_veps")
        s_rstd = sem("s_rstd")
        s_rng = sem("s_rng")
        s_rt = sem("s_rt")
        s_rcol = sem("s_rcol")
        s_rrow = sem("s_rrow")
        s_tab = sem("s_tab")
        s_ysc = sem("s_ysc")
        s_z = sem("s_z")
        s_yhi = sem("s_yhi")
        s_ylo = sem("s_ylo")
        s_yst = [sem(f"s_yst{k}") for k in range(GRP)]
        s_ytab = sem("s_ytab")
        s_idx = sem("s_idx")
        s_sel = sem("s_sel")
        s_gather = [sem(f"s_gather{k}") for k in range(RING // PACK)]
        s_landed = sem("s_landed")
        s_consumed = sem("s_consumed")
        s_yself = sem("s_yself")
        s_agg = sem("s_agg")
        s_aggs = sem("s_aggs")
        s_at = sem("s_at")
        s_ats = sem("s_ats")
        s_ht = sem("s_ht")
        s_hts = sem("s_hts")
        s_pool = sem("s_pool")
        s_hmv = sem("s_hmv")
        s_out = sem("s_out")
        s_go = sem("s_go")

        block = ctx.enter_context(nc.Block())

        @block.sync
        def _(sp):
            sp.dma_start(dst_i[:, :], dst_cols).then_inc(s_dst, 16)
            sp.dma_start(dr_i[:, :, :], dst_rows.rearrange("(b p) j -> p b j", p=CPART)).then_inc(s_dst, 16)
            sp.dma_start(src_i[:, :], src_cols).then_inc(s_src, 16)
            xv = x.rearrange("(t p) d -> p t d", p=P)
            for g in range(GRP):
                sp.dma_start(x_all[:, g * GRP:(g + 1) * GRP, :], xv[:, g * GRP:(g + 1) * GRP, :]).then_inc(s_x, 16)
            sp.dma_start(w_sb[:, :, :], w_t.rearrange("(k p) n -> p k n", p=P)).then_inc(s_w, 16)
            sp.dma_start(bcol[:, 0, :], b_cols).then_inc(s_w, 16)
            sp.dma_start(bcol[:, 1, :], gamma_cols).then_inc(s_w, 16)
            sp.dma_start(bcol[:, 2, :], beta_cols).then_inc(s_w, 16)
            yv = ytab.rearrange("(t p) d -> p t d", p=P)
            with sp.Fori(0, GRP) as g:
                for k in range(GRP):
                    sp.wait_ge(s_ylo, g * GRP + k + 1)
                    sp.dma_start(yv[:, bass.ds(g * GRP + k, 1), :], yrow[:, k:k + 1, :]).then_inc(s_yst[k], 16)
            for k in range(GRP):
                sp.wait_ge(s_yst[k], 16 * GRP)
            sp.sem_inc(s_ytab, 1)
            sp.dma_start(b1c[:, :], b1_cols).then_inc(s_b1, 16)
            sp.dma_start(gate[:, :, :], gate_t.rearrange("(k p) e -> p k e", p=P)).then_inc(s_gate, 16)

            def load_raw(e, j):
                sp.dma_start(wraw[:, j, 0, :].rearrange("p (k n) -> p k n", k=KD), w1[bass.ds(e, 1)].rearrange("e (k p) n -> p (e k) n", p=P)).then_inc(s_wraw[j], 16)
                sp.dma_start(wraw[:, j, 1, :].rearrange("p (k n) -> p k n", k=KH), w2[bass.ds(e, 1)].rearrange("e (k p) n -> p (e k) n", p=P)).then_inc(s_wraw[j], 16)

            for j in range(2):
                load_raw(j, j)
            with sp.Fori(1, NE // 2) as i:
                for j in range(2):
                    sp.wait_ge(s_wused, 2 * i + j - 1)
                    load_raw(2 * i + j, j)
            for j in range(2):
                sp.wait_ge(s_wused, NE + j - 1)
                load_raw(j, j)
            with sp.Fori(0, NE // 2 - 1) as i:
                for j in range(2):
                    sp.wait_ge(s_wlo, 2 * i + j + 1)
                    sp.dma_start(wtab[bass.ds(2 * i + j, 1)].rearrange("e p n -> p (e n)"), wspl[:, j, :]).then_inc(s_wst[j], 16)
                    load_raw(2 * i + j + 2, j)
            for j in range(2):
                sp.wait_ge(s_wlo, NE - 1 + j)
                sp.dma_start(wtab[NE - 2 + j], wspl[:, j, :]).then_inc(s_wst[j], 16)

            sp.wait_ge(s_hmv, 1)
            xt = lambda tab, t: tab[bass.ds(t * P, P), :]

            def store_rows(t, j):
                sp.wait_ge(s_x1, t + 1)
                sp.dma_start(xt(x1tab, t), x1[:, j, :]).then_inc(s_x1st[j], 16)
                sp.wait_ge(s_xn, t + 1)
                sp.dma_start(xt(xntab, t), xn[:, j, :]).then_inc(s_xnst[j], 16)

            for t in range(2):
                sp.dma_start(xr[:, t, :], xt(x, t)).then_inc(s_xr[t], 16)
            with sp.Fori(1, T // 2) as h:
                for j in range(2):
                    sp.wait_ge(s_u, 2 * h + j - 1)
                    sp.dma_start(xr[:, j, :], xt(x, 2 * h + j)).then_inc(s_xr[j], 16)
                    store_rows(2 * h + j - 2, j)
            sp.wait_ge(s_u, T - 2)
            sp.dma_start(xr[:, 0, :], xt(x, T - 1)).then_inc(s_xr[0], 16)
            for t in range(T - 3, T):
                store_rows(t, t % 2)
            for j in range(2):
                sp.wait_ge(s_x1st[j], 16 * ((T + 1 - j) // 2))
                sp.wait_ge(s_xnst[j], 16 * ((T + 1 - j) // 2))
                sp.wait_ge(s_wst[j], 16 * (NE // 2))
            sp.sem_inc(s_atab, 1)

            sp.wait_ge(s_tok, 1)
            sp.dma_start(b2r[:, :, :], b2.unsqueeze(0).to_broadcast([P, NE, D])).then_inc(s_b2, 16)
            for j in range(2):
                sp.dma_start(wsb[:, j, :], wtab[j]).then_inc(s_wl[j], 16)
            with sp.Fori(1, NE // 2) as i:
                for j in range(2):
                    done = sp.value_load(start_i[0:1, bass.ds(2 * i + j - 1, 1)], min_val=1, max_val=NSB)
                    sp.wait_ge(s_l2, done)
                    sp.dma_start(wsb[:, j, :], wtab[bass.ds(2 * i + j, 1)].rearrange("e p n -> p (e n)")).then_inc(s_wl[j], 16)

            sp.wait_ge(s_btab, 1)

            def load_f(t, j):
                sp.dma_start(x1r[:, j, :], xt(x1tab, t)).then_inc(s_fl[j], 16)
                for q in range(SHARED):
                    sp.dma_start(sh_r[:, j, q, :], btab[bass.ds((ROUTED_SB + q * SHARED_SB) * SB + t * P, P), :]).then_inc(s_fl[j], 16)

            def store_f(t, j):
                sp.wait_ge(s_acc, t + 1)
                sp.dma_start(xt(out, t), acc[:, j, :]).then_inc(s_ost[j], 16)

            for t in range(2):
                load_f(t, t)
            with sp.Fori(1, T // 2) as h:
                for j in range(2):
                    store_f(2 * h + j - 2, j)
                    load_f(2 * h + j, j)
            store_f(T - 3, 0)
            load_f(T - 1, 0)
            store_f(T - 2, 1)
            store_f(T - 1, 0)
            for j in range(2):
                sp.wait_ge(s_ost[j], 16 * ((T + 1 - j) // 2))

        @block.gpsimd
        def _(pool):
            n = [0]

            def link(ins):
                n[0] += 1
                ins.then_inc(s_pool, 1)
                pool.wait_ge(s_pool, n[0])

            pool.iota(iota_rep[:, :, :], [[1, P], [0, OH]], base=0, channel_multiplier=0,
                      allow_small_or_imprecise_dtypes=True).then_inc(s_const, 1)
            pool.iota(iota16[:, :], [[1, P]], base=0, channel_multiplier=0,
                      allow_small_or_imprecise_dtypes=True).then_inc(s_const, 1)
            pool.iota(iota_t[:, :], [[1, T]], base=0, channel_multiplier=0,
                      allow_small_or_imprecise_dtypes=True).then_inc(s_const, 1)
            pool.iota(tbase[:, :], [[P, T]], base=0, channel_multiplier=0,
                      allow_small_or_imprecise_dtypes=True).then_inc(s_const, 1)
            pool.iota(chunk_id[:, :], [[CPART, CBLK]], base=0, channel_multiplier=1,
                      allow_small_or_imprecise_dtypes=True).then_inc(s_const, 1)
            pool.memset(ones[:, :], 1.0).then_inc(s_const, 1)
            pool.memset(mhalf[:, :], -0.5).then_inc(s_const, 1)
            pool.memset(zero16[:, :], 0.0).then_inc(s_const, 1)
            pool.memset(ones16[:, :], 1.0).then_inc(s_const, 1)
            pool.wait_ge(s_const, 9)
            pool.affine_select(out=ident[:, :], in_=ones[:, :], pattern=[[-1, P]], compare_op=ALU.is_equal,
                               fill=0.0, base=0, channel_multiplier=1).then_inc(s_const, 1)
            pool.affine_select(out=upper[:, :], in_=ones[0:T, 0:T], pattern=[[1, T]], compare_op=ALU.is_gt,
                               fill=0.0, base=0, channel_multiplier=-1).then_inc(s_const, 1)
            pool.affine_select(out=upper16[:, :], in_=ones16[:, :], pattern=[[1, P]], compare_op=ALU.is_gt,
                               fill=0.0, base=0, channel_multiplier=-1).then_inc(s_const, 1)
            pool.wait_ge(s_const, 12)
            pool.tensor_copy(ident16[:, :], ident[:, :]).then_inc(s_const, 1)
            pool.wait_ge(s_degs, 1)
            pool.tensor_tensor(dinv[:, :], deg[:, :], mhalf[:, :], ALU.pow).then_inc(s_dinv, 1)
            pool.wait_ge(s_veps, 1)
            pool.tensor_tensor(rstd[:, :], veps[:, :], mhalf[:, :], ALU.pow).then_inc(s_rstd, 1)
            pool.wait_ge(s_tab, 1)
            groups = pool.value_load(toti[0:1, 0:1], min_val=1, max_val=T * CPAD // RING)
            pool.wait_ge(s_ytab, 1)
            pool.sem_inc(s_landed, CPAD)
            def gathers(g, first):
                for q in range(RING // PACK):
                    pool.wait_ge(s_sel, CPAD + g * RING + (q + 1) * PACK)
                    pool.sem_inc(s_go, 1)
                    for k in range(q * PACK, (q + 1) * PACK):
                        pool.indirect_dma_start(rows[:, k, :], None, ytab, bass.IndirectOffsetOnAxis(ap=idx[:, k:k + 1], axis=0)).then_inc(s_gather[q], 16)
                    if q or not first:
                        pool.wait_ge(s_gather[(q - 1) % (RING // PACK)], (g + 1 if q else g) * 16 * PACK)
                        pool.sem_inc(s_landed, PACK)

            gathers(0, True)
            with pool.Fori(1, groups) as g:
                gathers(g, False)
            pool.wait_ge(s_gather[RING // PACK - 1], groups * 16 * PACK)
            pool.sem_inc(s_landed, PACK)


            pool.wait_ge(s_bnv, 1)
            pool.tensor_tensor(bn_a[:, :], bn_v[:, :], mhalf[:, 0:KD], ALU.pow).then_inc(s_bnr, 1)

            def rstd2(t, j):
                pool.wait_ge(s_ve2, t + 1)
                pool.sem_inc(s_go, 1)
                pool.tensor_tensor(r2[:, j:j + 1], ve2[:, j:j + 1], mhalf[:, 0:1], ALU.pow).then_inc(s_r2, 1)

            for t in range(2):
                rstd2(t, t)
            with pool.Fori(1, T // 2) as h:
                for j in range(2):
                    pool.wait_ge(s_nb2, 2 * h + j - 1)
                    pool.sem_inc(s_go, 1)
                    pool.wait_ge(s_xn, 2 * h + j - 1)
                    pool.sem_inc(s_go, 1)
                    rstd2(2 * h + j, j)
            pool.wait_ge(s_xn, T - 2)
            rstd2(T - 1, 0)

            pool.wait_ge(s_lgc, T)
            pool.iota(rev16, [[0, T], [-1, EXPERTS]], base=EXPERTS, channel_multiplier=0, allow_small_or_imprecise_dtypes=True).then_inc(s_bc, 1)
            pool.iota(iota_b, [[1, RB]], base=0, channel_multiplier=0, allow_small_or_imprecise_dtypes=True).then_inc(s_bc, 1)
            pool.iota(pcol, [[0, 2]], base=0, channel_multiplier=1, allow_small_or_imprecise_dtypes=True).then_inc(s_bc, 1)
            pool.iota(iota_sb, [[1, NSB]], base=0, channel_multiplier=0, allow_small_or_imprecise_dtypes=True).then_inc(s_bc, 1)
            pool.iota(tok_f, [[P, 2 * NSB + 2]], base=-RB * P, channel_multiplier=1, allow_small_or_imprecise_dtypes=True).then_inc(s_bc, 1)

            pool.wait_ge(s_tok, 1)
            pool.wait_ge(s_atab, 1)

            def gather(b, j, wait):
                pool.tensor_copy(idx2[:, j, :], tok_i[:, bass.ds(2 * b, 2)]).then_inc(s_ig, 1)
                pool.wait_ge(s_ig, b + 1)
                pool.sem_inc(s_go, 1)
                if wait:
                    pool.wait_ge(s_t, b)
                    pool.sem_inc(s_go, 1)
                for q in range(2):
                    pool.indirect_dma_start(xg[:, q, :], None, xntab, bass.IndirectOffsetOnAxis(ap=idx2[:, j, q:q + 1], axis=0)).then_inc(s_xg, 16)

            def store_y(b, j):
                pool.wait_ge(s_y, 2 * b + 4)
                pool.sem_inc(s_go, 1)
                pool.dma_start(btab[bass.ds(b * SB, SB), :].rearrange("(q p) d -> p q d", q=2), y_s[:, j, :, :]).then_inc(s_bst[j], 16)

            gather(0, 0, False)
            gather(1, 1, True)
            with pool.Fori(1, NSB // 2) as h:
                for j in range(2):
                    gather(2 * h + j, j, True)
                    store_y(2 * h + j - 2, j)
            gather(NSB, 0, True)
            store_y(NSB - 2, 0)
            store_y(NSB - 1, 1)
            for j in range(2):
                pool.wait_ge(s_bst[j], 16 * (NSB // 2))
            pool.sem_inc(s_btab, 1)

            def gather4(t, j, wait):
                if wait:
                    pool.wait_ge(s_acc, t - 1)
                    pool.sem_inc(s_go, 1)
                pool.tensor_copy(idx4[:, j, :], slot_i[:, bass.ds(t, 1), :].rearrange("p a k -> p (a k)")).then_inc(s_i4, 1)
                pool.wait_ge(s_i4, t + 1)
                pool.sem_inc(s_go, 1)
                for k in range(TOP):
                    pool.indirect_dma_start(yk[:, j, k, :], None, btab, bass.IndirectOffsetOnAxis(ap=idx4[:, j, k:k + 1], axis=0)).then_inc(s_yk[j], 16)

            for t in range(2):
                gather4(t, t, False)
            with pool.Fori(1, T // 2) as h:
                for j in range(2):
                    gather4(2 * h + j, j, True)
            gather4(T - 1, 0, True)

        @block.vector
        def _(dve):
            n = [0]

            def link(ins):
                n[0] += 1
                ins.then_inc(s_cdve, 1)
                dve.wait_ge(s_cdve, n[0])

            dve.wait_ge(s_dst, 32)
            link(nc.vector.tensor_copy(dst_f[:, :], dst_i[:, :]))
            link(nc.vector.tensor_scalar(tmp_i[:, :], dst_i[:, :], 7, None, ALU.logical_shift_right))
            link(nc.vector.tensor_copy(dst_h[:, :], tmp_i[:, :]))
            link(nc.vector.tensor_scalar(tmp_i[:, :], dst_i[:, :], P - 1, None, ALU.bitwise_and))
            link(nc.vector.tensor_copy(dst_l[:, :], tmp_i[:, :]))
            dve.wait_ge(s_const, 9)

            def onehots(i, k):
                c = bass.ds(i * 2 * OH + k * OH, OH)
                nc.vector.tensor_tensor(oh_l[:, k, :, :], iota_rep[:, :, :],
                                        dst_l[:, c].unsqueeze(1).to_broadcast([P, P, OH]), ALU.is_equal).then_inc(s_oh, 1)
                nc.vector.tensor_tensor(oh_h[:, k, :, :], iota_rep[:, 0:T, :],
                                        dst_h[:, c].unsqueeze(1).to_broadcast([P, T, OH]), ALU.is_equal).then_inc(s_oh, 1)

            for k in range(2):
                onehots(0, k)
            with dve.Fori(1, NB // 2) as i:
                for k in range(2):
                    dve.wait_ge(s_ohused, 2 * i + k - 1)
                    onehots(i, k)
            link(nc.vector.tensor_scalar(dr_i[:, :, :], dr_i[:, :, :], 7, None, ALU.logical_shift_right))
            link(nc.vector.tensor_reduce(mn[:, :], dr_i[:, :, :], AX.X, ALU.min))
            link(nc.vector.tensor_reduce(mx[:, :], dr_i[:, :, :], AX.X, ALU.max))
            tt = iota_t[0:CPART, :].unsqueeze(2).to_broadcast([CPART, T, CBLK])
            bc = lambda a: a[:, :].unsqueeze(1).to_broadcast([CPART, T, CBLK])
            link(nc.vector.tensor_tensor(cnd[:, 0], tt, bc(mn), ALU.is_ge))
            link(nc.vector.tensor_tensor(cnd[:, 1], bc(mx), tt, ALU.is_ge))
            link(nc.vector.tensor_tensor(cnd[:, 0], cnd[:, 0], cnd[:, 1], ALU.mult))
            link(nc.vector.tensor_scalar(mn[:, :], chunk_id[:, :], -1.0, float(BIG), ALU.mult, ALU.add))
            link(nc.vector.tensor_scalar(mx[:, :], chunk_id[:, :], 1.0, None, ALU.add))
            link(nc.vector.tensor_tensor(cnd[:, 2], cnd[:, 0], bc(mn), ALU.mult))
            link(nc.vector.tensor_tensor(cnd[:, 3], cnd[:, 0], bc(mx), ALU.mult))
            link(nc.vector.tensor_reduce(rng[:, 0, :], cnd[:, 2], AX.X, ALU.max))
            nc.vector.tensor_reduce(rng[:, 1, :], cnd[:, 3], AX.X, ALU.max).then_inc(s_rng, 1)
            dve.wait_ge(s_rt, 1)
            rt = rt_ps[0:T, 0:2 * CPART].rearrange("t (a c) -> t a c", a=2)
            link(nc.vector.tensor_reduce(rcol[:, 0:2], rt, AX.X, ALU.max))
            link(nc.vector.tensor_scalar(rcol[:, 2:3], rcol[:, 0:1], -1.0, float(BIG), ALU.mult, ALU.add))
            link(nc.vector.tensor_scalar(rcol[:, 2:3], rcol[:, 2:3], float(CHUNKS - 1), None, ALU.min))
            link(nc.vector.tensor_scalar(rcol[:, 3:4], rcol[:, 2:3], 1.0, None, ALU.add))
            link(nc.vector.tensor_tensor(rcol[:, 3:4], rcol[:, 3:4], rcol[:, 1:2], ALU.max))
            link(nc.vector.scalar_tensor_tensor(rcol[:, 4:5], rcol[:, 3:4], 1.0, rcol[:, 2:3], ALU.add, ALU.subtract))
            link(nc.vector.tensor_copy(rcol_i[:, 0:1], rcol[:, 4:5]))
            link(nc.vector.tensor_scalar(rcol_i[:, 1:2], rcol_i[:, 0:1], 1, 1, ALU.logical_shift_right, ALU.logical_shift_left))
            link(nc.vector.tensor_copy(rcol[:, 4:5], rcol_i[:, 1:2]))
            nc.vector.tensor_tensor(rcol[:, 3:4], rcol[:, 2:3], rcol[:, 4:5], ALU.add).then_inc(s_rcol, 1)
            dve.wait_ge(s_rrow, 1)
            link(nc.vector.tensor_copy(rrow[:, 0:3, :], rt_ps[0:1, 256:256 + 3 * T].rearrange("o (a t) -> o a t", a=3)))
            link(nc.vector.tensor_copy(tot[:, 0:1], rt_ps[0:1, 256 + 3 * T:257 + 3 * T]))
            link(nc.vector.tensor_tensor(rrow[:, 2, :], rrow[:, 2, :], rrow[:, 0, :], ALU.subtract))
            link(nc.vector.tensor_scalar(rrow[:, 2, :], rrow[:, 2, :], float(CPAD), None, ALU.add))
            link(nc.vector.tensor_scalar(tot[:, 1:2], tot[:, 0:1], float(RING - 1), None, ALU.add))
            link(nc.vector.tensor_copy(toti[:, 1:2], tot[:, 1:2]))
            link(nc.vector.tensor_scalar(toti[:, 0:1], toti[:, 1:2], RING.bit_length() - 1, None, ALU.logical_shift_right))
            link(nc.vector.tensor_copy(tot[:, 2:3], toti[:, 0:1]))
            link(nc.vector.tensor_scalar(tot[:, 3:4], tot[:, 2:3], float(RING), tot[:, 0:1], ALU.mult, ALU.subtract))
            link(nc.vector.tensor_tensor(rrow[:, 1, T - 1:T], rrow[:, 1, T - 1:T], tot[:, 3:4], ALU.add))
            link(nc.vector.tensor_copy(tab[:, :, :], rrow[:, 0:3, :]))
            dve.sem_inc(s_tab, 1)
            dve.wait_ge(s_x, 16 * GRP)
            with dve.Fori(0, T) as t:
                nc.vector.bn_stats(st6[:, bass.ds(t, 1), :], x_all[:, bass.ds(t, 1), :]).then_inc(s_cdve, 1)
            dve.wait_ge(s_cdve, n[0] + T)
            n[0] += T
            link(nc.vector.tensor_tensor(mv[:, :, 0], st6[:, :, 1], st6[:, :, 4], ALU.add))
            link(nc.vector.tensor_scalar(mv[:, :, 0], mv[:, :, 0], 0.5, None, ALU.mult))
            link(nc.vector.tensor_tensor(mv[:, :, 1], st6[:, :, 1], st6[:, :, 4], ALU.subtract))
            link(nc.vector.scalar_tensor_tensor(mv[:, :, 1], mv[:, :, 1], 0.25, mv[:, :, 1], ALU.mult, ALU.mult))
            link(nc.vector.tensor_tensor(veps[:, :], st6[:, :, 2], st6[:, :, 5], ALU.add))
            link(nc.vector.scalar_tensor_tensor(veps[:, :], veps[:, :], 1.0 / D, mv[:, :, 1], ALU.mult, ALU.add))
            nc.vector.tensor_scalar(veps[:, :], veps[:, :], EPS, None, ALU.add).then_inc(s_veps, 1)
            dve.wait_ge(s_deg, 1)
            nc.vector.tensor_copy(deg[:, :], deg_ps[:, 0:T]).then_inc(s_degs, 1)
            dve.wait_ge(s_dinv, 1)
            dve.wait_ge(s_rstd, 1)
            link(nc.vector.tensor_scalar(dinv_ys[:, :], dinv[:, :], 1.0 / YS, None, ALU.mult))
            link(nc.vector.scalar_tensor_tensor(ysc[:, :], rstd[:, :], YS, dinv[:, :], ALU.mult, ALU.mult))
            nc.vector.scalar_tensor_tensor(ybi[:, :], mv[:, :, 0], -1.0, ysc[:, :], ALU.mult, ALU.mult).then_inc(s_ysc, 1)
            with dve.Fori(0, GRP) as g:
                for k in range(GRP):
                    dve.wait_ge(s_yhi, g * GRP + k + 1)
                    nc.vector.tensor_tensor(yrow[:, k, D:2 * D], z[:, k, :], yrow[:, k, 0:D], ALU.subtract).then_inc(s_ylo, 1)

            dve.wait_ge(s_src, 16)
            dve.sem_inc(s_sel, CPAD)

            def tile(t, stats):
                lo = dve.value_load(tab[0:1, 0, bass.ds(t, 1)], min_val=0, max_val=CPAD - 2)
                hi = dve.value_load(tab[0:1, 1, bass.ds(t, 1)], min_val=0, max_val=CPAD - 2)
                off = dve.value_load(tab[0:1, 2, bass.ds(t, 1)], min_val=0, max_val=T * CPAD + CPAD)
                with dve.Fori(lo, hi, 2) as c:
                    s = dve.snap(c + off)
                    slot = even_slot(dve.snap(s % RING))
                    dve.wait_ge(s_consumed, s + 2)
                    nc.vector.tensor_copy(idx[:, bass.ds(slot, 2)], src_i[:, bass.ds(c, 2)])
                    for q in range(2):
                        nc.vector.tensor_scalar(sel[:, bass.ds(slot + q, 1), :], iota16[:, :].unsqueeze(1), tbase[:, bass.ds(t, 1)],
                                                dst_f[:, bass.ds(c + q, 1)], ALU.add, ALU.is_equal).then_inc(s_sel, 1)
                if stats:
                    dve.wait_ge(s_hts, t - 1)
                    for m in range(KD):
                        nc.vector.bn_stats(hst[:, m, bass.ds(t - 2, 1), :], h_t[:, m, bass.ds((t - 2) * P, P)].unsqueeze(1)).then_inc(s_hst, 1)

            def weight_max(e, j):
                dve.wait_ge(s_wraw[j], 16 * (e - j) + 32)
                nc.vector.tensor_reduce(wmx[:, 0, bass.ds(e, 1)], wraw[:, j, 0, :], AX.X, ALU.max, apply_absolute_value=True)
                nc.vector.tensor_reduce(wmx[:, 1, bass.ds(e, 1)], wraw[:, j, 1, :], AX.X, ALU.max, apply_absolute_value=True).then_inc(s_wused, 1)

            def weight_split(e, j, wait):
                dve.wait_ge(s_wraw[j], 16 * (e - j) + 32 + 16 * NE)
                if wait:
                    dve.wait_ge(s_wst[j], 8 * (e - j))
                for w in range(2):
                    hi = wspl[:, j, 2 * w * WL:(2 * w + 1) * WL]
                    lo = wspl[:, j, (2 * w + 1) * WL:(2 * w + 2) * WL]
                    nc.vector.tensor_scalar(hi, wraw[:, j, w, :], scl[:, w:w + 1], None, ALU.mult).then_inc(s_whi, 1)
                    dve.wait_ge(s_whi, 2 * e + w + 1)
                    last = nc.vector.scalar_tensor_tensor(lo, wraw[:, j, w, :], scl[:, w:w + 1], hi, ALU.mult, ALU.subtract)
                last.then_inc(s_wlo, 1)

            MAX_TO = MAX_FROM + NE
            tile(0, False)
            tile(1, False)
            with dve.Fori(0, NE // 2) as i:
                for j in range(2):
                    tile(2 * i + j + MAX_FROM, True)
                    weight_max(2 * i + j, j)
            dve.wait_ge(s_wused, NE)
            dve.wait_ge(s_b1, 16)
            link(nc.vector.tensor_reduce(wm3[:, 0:2], wmx[:, :, :], AX.X, ALU.max))
            link(nc.vector.tensor_reduce(wm3[:, 2:3], b1c[:, :], AX.X, ALU.max, apply_absolute_value=True))
            nc.vector.tensor_copy(wmb[:, :, :], wm3[:, 0:3].unsqueeze(2).to_broadcast([P, 3, P])).then_inc(s_wm, 1)
            with dve.Fori(MAX_TO, SPLIT_FROM) as t:
                tile(t, True)
            dve.wait_ge(s_wmt, 1)
            link(nc.vector.tensor_reduce(wm3[:, 0:3], wm_ps, AX.X, ALU.max))
            link(nc.vector.scalar_tensor_tensor(wm3[:, 2:3], wm3[:, 0:1], float(D), wm3[:, 2:3], ALU.mult, ALU.add))
            link(nc.vector.tensor_scalar(wex_i[:, 0:3], wm3[:, 0:3].bitcast(I32), 23, None, ALU.logical_shift_right))
            link(nc.vector.tensor_copy(wex_f[:, 0:3], wex_i[:, 0:3]))
            link(nc.vector.tensor_scalar(wex_f[:, 0:3], wex_f[:, 0:3], 97.0, None, ALU.max))
            link(nc.vector.tensor_scalar(wex_f[:, 0:3], wex_f[:, 0:3], -1.0, 268.0, ALU.mult, ALU.add))
            link(nc.vector.tensor_scalar(wex_f[:, 3:4], wex_f[:, 0:1], -1.0, 244.0, ALU.mult, ALU.add))
            link(nc.vector.tensor_tensor(wex_f[:, 4:5], wex_f[:, 1:2], wex_f[:, 2:3], ALU.add))
            link(nc.vector.tensor_scalar(wex_f[:, 4:5], wex_f[:, 4:5], -1.0, 381.0, ALU.mult, ALU.add))
            link(nc.vector.tensor_copy(wex_i[:, 0:5], wex_f[:, 0:5]))
            link(nc.vector.tensor_scalar(wex_s[:, 0:5], wex_i[:, 0:5], 23, None, ALU.logical_shift_left))
            for j in range(2):
                tile(j + SPLIT_FROM, True)
                weight_split(j, j, False)
            with dve.Fori(1, NE // 2) as i:
                for j in range(2):
                    tile(2 * i + j + SPLIT_FROM, True)
                    weight_split(2 * i + j, j, True)
            for t in range(SPLIT_FROM + NE, T):
                tile(t, True)
            dve.wait_ge(s_hts, T)
            for m in range(KD):
                nc.vector.bn_stats(hst[:, m, T - 2, :], h_t[:, m, (T - 2) * P:(T - 1) * P]).then_inc(s_hst, 1)
            for m in range(KD):
                nc.vector.bn_stats(hst[:, m, T - 1, :], h_t[:, m, (T - 1) * P:(T - 1) * P + LAST]).then_inc(s_hst, 1)
            dve.wait_ge(s_hst, KD * T)
            for m in range(KD):
                link(nc.vector.bn_aggr(hmv[:, m, :], hst[:, m, :, :].rearrange("p t s -> p (t s)")))
            nc.vector.tensor_scalar(bn_v[:, :], hmv[:, :, 1], EPS, None, ALU.add).then_inc(s_bnv, 1)
            dve.wait_ge(s_bnr, 1)
            link(nc.vector.tensor_tensor(bn_a[:, :], bn_a[:, :], bcol[:, 1, :], ALU.mult))
            link(nc.vector.tensor_tensor(bn_b[:, :], hmv[:, :, 0], bn_a[:, :], ALU.mult))
            link(nc.vector.tensor_tensor(bn_b[:, :], bcol[:, 2, :], bn_b[:, :], ALU.subtract))
            link(nc.vector.tensor_scalar(c1[:, :], rstd[:, :], 1.0, None, ALU.add))
            link(nc.vector.scalar_tensor_tensor(c2[:, :], mv[:, :, 0], -1.0, rstd[:, :], ALU.mult, ALU.mult))
            dve.sem_inc(s_bn, 1)
            dve.sem_inc(s_hmv, 1)

            def residual(t, j, steady):
                dve.wait_ge(s_xr[j], 8 * (t - j) + 16)
                if steady:
                    dve.wait_ge(s_xn, t - 1)
                    dve.wait_ge(s_x1st[j], 8 * (t - j))
                nc.vector.tensor_scalar(x1[:, j, :], xr[:, j, :], c1[:, bass.ds(t, 1)], c2[:, bass.ds(t, 1)], ALU.mult, ALU.add).then_inc(s_u, 1)
                dve.wait_ge(s_u, t + 1)
                dve.wait_ge(s_t1, t + 1)
                nc.vector.tensor_tensor(x1[:, j, :], bank[j][:, :], x1[:, j, :], ALU.add).then_inc(s_x1, 1)
                dve.wait_ge(s_x1, t + 1)
                nc.vector.bn_stats(st2[:, j, :], x1[:, j, :]).then_inc(s_st2, 1)
                dve.wait_ge(s_st2, t + 1)
                dve.sem_inc(s_go, 1)
                nc.vector.bn_aggr(mv2[:, j, :], st2[:, j, :]).then_inc(s_mv2, 1)
                dve.wait_ge(s_mv2, t + 1)
                nc.vector.tensor_scalar(ve2[:, j:j + 1], mv2[:, j, 1:2], EPS, None, ALU.add).then_inc(s_ve2, 1)

            def shift(t, j):
                dve.wait_ge(s_r2, t + 1)
                nc.vector.scalar_tensor_tensor(nb2[:, j:j + 1], mv2[:, j, 0:1], -1.0, r2[:, j:j + 1], ALU.mult, ALU.mult).then_inc(s_nb2, 1)

            def keep_logits(t, j):
                dve.wait_ge(s_lg, t + 1)
                nc.vector.tensor_copy(logits[:, bass.ds(t, 1), :], bank[4 + j][:, 0:EXPERTS].unsqueeze(1)).then_inc(s_lgc, 1)

            residual(0, 0, False)
            shift(0, 0)
            residual(1, 1, False)
            shift(1, 1)
            residual(2, 0, True)
            shift(2, 0)
            residual(3, 1, True)
            shift(3, 1)
            keep_logits(0, 0)
            with dve.Fori(2, T // 2) as h:
                for j in range(2):
                    residual(2 * h + j, j, True)
                    keep_logits(2 * h + j - 3, 1 - j)
                    shift(2 * h + j, j)
            residual(T - 1, 0, True)
            shift(T - 1, 0)
            for t in range(T - 4, T):
                keep_logits(t, t % 2)

            V = nc.vector
            full = [P, T, EXPERTS]
            over = lambda a: a.unsqueeze(2).to_broadcast(full)
            dve.wait_ge(s_lgc, T)
            dve.wait_ge(s_bc, 5)
            link(V.tensor_reduce(vec_a[:, 0, :], logits, AX.X, ALU.max))
            V.tensor_tensor(probs, logits, over(vec_a[:, 0, :]), ALU.subtract).then_inc(s_sub, 1)
            dve.wait_ge(s_exp, 1)
            link(V.tensor_reduce(vec_a[:, 0, :], probs, AX.X, ALU.add))
            link(V.reciprocal(vec_a[:, 0, :], vec_a[:, 0, :]))
            link(V.tensor_tensor(probs, probs, over(vec_a[:, 0, :]), ALU.mult))
            for k in range(TOP):
                link(V.tensor_reduce(top_v[:, k, :], probs, AX.X, ALU.max))
                link(V.tensor_tensor(tmp_a, probs, over(top_v[:, k, :]), ALU.is_equal))
                link(V.tensor_tensor(tmp_a, tmp_a, rev16, ALU.mult))
                link(V.tensor_reduce(vec_b[:, 0, :], tmp_a, AX.X, ALU.max))
                link(V.tensor_tensor(hot[:, k], rev16, over(vec_b[:, 0, :]), ALU.is_equal))
                link(V.scalar_tensor_tensor(probs, hot[:, k], -2.0, probs, ALU.mult, ALU.add))
            link(V.tensor_tensor(tmp_a, hot[:, 0], hot[:, 1], ALU.add))
            link(V.tensor_tensor(tmp_b, hot[:, 2], hot[:, 3], ALU.add))
            V.tensor_tensor(mask16, tmp_a, tmp_b, ALU.add).then_inc(s_mask, 1)
            V.tensor_tensor(vec_a, top_v, top_v[:, 0:1, :].to_broadcast([P, TOP, T]), ALU.subtract).then_inc(s_topv, 1)
            dve.wait_ge(s_rank, 1)
            HG = T * EXPERTS // 2
            flat = lambda a: a.rearrange("p t e -> p (t e)")
            for h in range(2):
                link(V.tensor_copy(flat(rank_s)[:, h * HG:(h + 1) * HG], bank[h][:, 0:HG]))
                link(V.tensor_copy(flat(cum_a)[:, h * HG:(h + 1) * HG], bank[2 + h][:, 0:HG]))
            src_c, dst_c, step = cum_a, cum_b, 1
            while step < T:
                link(V.tensor_copy(dst_c[:, 0:step, :], src_c[:, 0:step, :]))
                link(V.tensor_tensor(dst_c[:, step:T, :], src_c[:, step:T, :], src_c[:, 0:T - step, :], ALU.add))
                src_c, dst_c, step = dst_c, src_c, 2 * step
            link(V.tensor_tensor(flat(rank_s)[:, EXPERTS:], flat(rank_s)[:, EXPERTS:], flat(src_c)[:, 0:(T - 1) * EXPERTS], ALU.add))
            link(V.tensor_scalar(tot_e, src_c[:, T - 1, :], float(SB - 1), None, ALU.add))
            link(V.tensor_copy(blk_e, tot_e))
            link(V.tensor_scalar(blk_e, blk_e, 8, None, ALU.logical_shift_right))
            link(V.tensor_copy(tot_e, blk_e))
            link(V.tensor_scalar(pre_e, tot_e, 1.0, None, ALU.max))
            link(V.tensor_copy(tot_e, pre_e))
            a_e, b_e, step = pre_e, pre_e2, 1
            while step < EXPERTS:
                link(V.tensor_copy(b_e[:, 0:step], a_e[:, 0:step]))
                link(V.tensor_tensor(b_e[:, step:], a_e[:, step:], a_e[:, 0:EXPERTS - step], ALU.add))
                a_e, b_e, step = b_e, a_e, 2 * step
            link(V.tensor_tensor(b_e, a_e, tot_e, ALU.subtract))
            link(V.tensor_copy(start_f[:, 0:EXPERTS], b_e[0:1, :]))
            for q in range(SHARED + 1):
                link(V.memset(start_f[:, EXPERTS + q:EXPERTS + q + 1], float(ROUTED_SB + q * SHARED_SB)))
            link(V.tensor_copy(start_i[:, :], start_f[:, :]))
            link(V.tensor_tensor(ebt[0:1], iota_sb[0:1, :].unsqueeze(2).to_broadcast([1, NSB, NE]),
                                 start_f[:, 0:NE].unsqueeze(1).to_broadcast([1, NSB, NE]), ALU.is_ge))
            link(V.tensor_reduce(iota_sb[0:1, :], ebt[0:1], AX.X, ALU.add))
            link(V.tensor_scalar(eb_i[:, :], iota_sb[0:1, :], 1.0, None, ALU.subtract))
            link(V.scalar_tensor_tensor(rank_s, b_e.unsqueeze(1).to_broadcast(full), float(SB), rank_s, ALU.mult, ALU.add))
            for k in range(TOP):
                link(V.tensor_tensor(tmp_a, hot[:, k], rank_s, ALU.mult))
                link(V.tensor_reduce(r_f[:, :, k], tmp_a, AX.X, ALU.add))
            link(V.tensor_copy(slot_i, r_f))
            ti = tmp_b.rearrange("p t e -> p (t e)")[:, 0:T * TOP].bitcast(I32).rearrange("p (t k) -> p t k", k=TOP)
            link(V.tensor_scalar(ti, slot_i, 7, None, ALU.logical_shift_right))
            link(V.tensor_copy(b_f, ti))
            link(V.tensor_scalar(ti, slot_i, P - 1, None, ALU.bitwise_and))
            link(V.tensor_copy(r_f, ti))
            dve.wait_ge(s_exp2, 1)
            link(V.tensor_tensor(vec_b[:, 0, :], vec_a[:, 0, :], vec_a[:, 1, :], ALU.add))
            link(V.tensor_tensor(vec_b[:, 1, :], vec_a[:, 2, :], vec_a[:, 3, :], ALU.add))
            link(V.tensor_tensor(vec_b[:, 0, :], vec_b[:, 0, :], vec_b[:, 1, :], ALU.add))
            link(V.reciprocal(vec_b[:, 0, :], vec_b[:, 0, :]))
            link(V.tensor_tensor(wk, vec_a.rearrange("p k t -> p t k"), vec_b[:, 0, :].unsqueeze(2).to_broadcast([P, T, TOP]), ALU.mult))

            def places(t, wait):
                for k in range(TOP):
                    j = k % 2
                    if wait or k >= 2:
                        dve.wait_ge(s_inv, t * TOP + k - 1)
                    nc.vector.tensor_scalar(oh_r[:, j, :], iota16[:, :], r_f[:, bass.ds(t, 1), k:k + 1].rearrange("p a k -> p (a k)"), None, ALU.is_equal)
                    bcol_tk = b_f[:, bass.ds(t, 1), k:k + 1].rearrange("p a k -> p (a k)")
                    nc.vector.tensor_scalar(oh_b[:, j, 0, :], iota_b, bcol_tk, pcol[:, 0:1], ALU.is_equal, ALU.mult)
                    nc.vector.tensor_scalar(oh_b[:, j, 1, :], iota_b, bcol_tk, iota_t[:, bass.ds(t, 1)], ALU.is_equal, ALU.mult).then_inc(s_ohr, 1)

            places(0, False)
            with dve.Fori(1, T) as t:
                places(t, True)
            dve.wait_ge(s_inv, T * TOP + 1)
            for q in range(SHARED):
                a0 = 2 * (ROUTED_SB + q * SHARED_SB)
                if q:
                    link(V.tensor_scalar(tok_f[:, a0:a0 + 2 * SHARED_SB + 2], tok_f[:, a0:a0 + 2 * SHARED_SB + 2], -2.0 * SHARED_SB * P, None, ALU.add))
            link(V.tensor_scalar(tok_f, tok_f, 0.0, float(NP - 1), ALU.max, ALU.min))
            link(V.tensor_copy(tok_f[:, 0:RB], bank[4][:, 0:RB]))
            link(V.scalar_tensor_tensor(tok_f[:, 0:RB], bank[4][:, RB:2 * RB], float(P), tok_f[:, 0:RB], ALU.mult, ALU.add))
            link(V.tensor_copy(tok_i, tok_f))
            dve.sem_inc(s_tok, 1)

            def low_x(b):
                dve.wait_ge(s_xhi, 2 * b + 2)
                for q in range(2):
                    last = nc.vector.scalar_tensor_tensor(xl[:, q], cut(q, KD), YS, xh[:, q], ALU.mult, ALU.subtract)
                last.then_inc(s_xlo, 1)

            def hidden(b, wait):
                for m in range(KH):
                    dve.wait_ge(s_g, 2 * b + m + 3)
                    if m == 0 and wait:
                        dve.wait_ge(s_l2, b)
                    nc.vector.tensor_scalar(hh[:, m, :], g_s[:, m, :], scale_h, None, ALU.mult).then_inc(s_hhi, 1)
                    dve.wait_ge(s_hhi, 2 * b + m + 1)
                    nc.vector.scalar_tensor_tensor(hl[:, m, :], g_s[:, m, :], scale_h, hh[:, m, :], ALU.mult, ALU.subtract).then_inc(s_hlo, 1)

            def results(b, j, wait):
                e = dve.value_load(eb_i[0:1, bass.ds(b, 1)], min_val=0, max_val=NE - 1)
                dve.wait_ge(s_l2, b + 1)
                if wait:
                    dve.wait_ge(s_bst[j], 8 * (b - j))
                for q in range(2):
                    nc.vector.scalar_tensor_tensor(y_s[:, j, q, :].unsqueeze(1), bank[4 + q][:, :].unsqueeze(1), unscale_2, b2r[:, bass.ds(e, 1), :], ALU.mult, ALU.add).then_inc(s_y, 1)

            dve.wait_ge(s_b2, 16)
            low_x(0)
            for b in range(2):
                hidden(b, b > 0)
                low_x(b + 1)
                results(b, b, False)
            with dve.Fori(1, NSB // 2) as h:
                for j in range(2):
                    hidden(2 * h + j, True)
                    low_x(2 * h + j + 1)
                    results(2 * h + j, j, True)

            def combine(t, j, wait):
                dve.wait_ge(s_fl[j], 24 * (t - j) + 48)
                if wait:
                    dve.wait_ge(s_ost[j], 8 * (t - j))
                V.tensor_tensor(acc[:, j, :], sh_r[:, j, 0, :], sh_r[:, j, 1, :], ALU.add).then_inc(s_fd, 1)
                dve.wait_ge(s_fd, 5 * t + 1)
                V.scalar_tensor_tensor(acc[:, j, :], acc[:, j, :], 1.0 / SHARED, x1r[:, j, :], ALU.mult, ALU.add).then_inc(s_fd, 1)
                dve.wait_ge(s_yk[j], 32 * (t - j) + 64)
                for k in range(TOP):
                    dve.wait_ge(s_fd, 5 * t + k + 2)
                    V.scalar_tensor_tensor(acc[:, j, :], yk[:, j, k, :], wk[:, bass.ds(t, 1), k:k + 1].rearrange("p a k -> p (a k)"), acc[:, j, :],
                                           ALU.mult, ALU.add).then_inc(s_fd if k < TOP - 1 else s_acc, 1)

            for t in range(2):
                combine(t, t, False)
            with dve.Fori(1, T // 2) as h:
                for j in range(2):
                    combine(2 * h + j, j, True)
            combine(T - 1, 0, True)

        @block.scalar
        def _(act):
            act.wait_ge(s_ysc, 1)

            def rows_hi(g, k):
                t = g * GRP + k
                nc.scalar.activation(z[:, k, :], x_all[:, bass.ds(t, 1), :].rearrange("p a d -> p (a d)"), ACT.Identity, bias=ybi[:, bass.ds(t, 1)],
                                     scale=ysc[:, bass.ds(t, 1)]).then_inc(s_z, 1)
                act.wait_ge(s_z, t + 1)
                nc.scalar.activation(yrow[:, k, 0:D], z[:, k, :], ACT.Copy).then_inc(s_yhi, 1)

            for k in range(GRP):
                rows_hi(0, k)
            with act.Fori(1, GRP) as g:
                for k in range(GRP):
                    act.wait_ge(s_yst[k], g * 16)
                    act.wait_ge(s_ylo, g * GRP + k + 1 - GRP)
                    rows_hi(g, k)
            act.wait_ge(s_w, 64)

            yv = ytab.rearrange("(t p) d -> p t d", p=P)
            act.wait_ge(s_ytab, 1)
            act.dma_start(yself[:, :], yv[:, 0:1, :]).then_inc(s_yself, 16)

            def finish_tile(t, par, more=True):
                act.wait_ge(s_agg, t + 2)
                act.dma_start(yself[:, :], yv[:, bass.ds(t + 1, 1), :]).then_inc(s_yself, 16) if more else None
                act.wait_ge(s_at, t + 1)
                nc.scalar.activation(agg_s[:, :], agg_b[par][:, :], ACT.Copy, scale=dinv_ys[:, bass.ds(t, 1)]).then_inc(s_aggs, 1)
                act.wait_ge(s_at, t + 2)
                nc.scalar.activation(agg_ts[:, :, :], at_ps[:, :, :], ACT.Copy).then_inc(s_ats, 1)
                act.wait_ge(s_ht, t + 1)
                for m in range(KD):
                    ins = nc.scalar.activation(h_t[:, m, bass.ds(t * P, P)], ht_ps[:, m, :], ACT.Identity, bias=bcol[:, 0, m:m + 1])
                ins.then_inc(s_hts, 1)

            finish_tile(0, 0)
            with act.Fori(0, T // 2 - 1) as h:
                finish_tile(2 * h + 1, 1)
                finish_tile(2 * h + 2, 0)
            finish_tile(T - 2, 1)
            finish_tile(T - 1, 0, more=False)

            act.wait_ge(s_bn, 1)
            def gelu_tile(t, j, steady):
                if steady:
                    act.wait_ge(s_t1, t - 1)
                for m in range(KD):
                    last = nc.scalar.activation(g_tile[:, j, m, :], h_t[:, m, bass.ds(t * P, P)], ACT.Gelu, bias=bn_b[:, m:m + 1], scale=bn_a[:, m:m + 1])
                last.then_inc(s_gelu, 1)

            def norm_row(t, j, steady):
                act.wait_ge(s_nb2, t + 1)
                if steady:
                    act.wait_ge(s_t2, t - 1)
                    act.wait_ge(s_xnst[j], 8 * (t - j))
                nc.scalar.activation(xn[:, j, :], x1[:, j, :], ACT.Identity, bias=nb2[:, j:j + 1], scale=r2[:, j:j + 1]).then_inc(s_xn, 1)

            def keep_turned(t, j, steady):
                act.wait_ge(s_t2, t + 1)
                if steady:
                    act.wait_ge(s_lg, t - 1)
                nc.scalar.activation(x_ts[:, j], cut(2 + j, KD), ACT.Copy).then_inc(s_xT, 1)

            gelu_tile(0, 0, False)
            gelu_tile(1, 1, False)
            norm_row(0, 0, False)
            gelu_tile(2, 0, True)
            norm_row(1, 1, False)
            keep_turned(0, 0, False)
            gelu_tile(3, 1, True)
            norm_row(2, 0, True)
            keep_turned(1, 1, False)
            with act.Fori(2, T // 2) as h:
                for j in range(2):
                    gelu_tile(2 * h + j, j, True)
                    norm_row(2 * h + j - 1, 1 - j, True)
                    keep_turned(2 * h + j - 2, j, True)
            gelu_tile(T - 1, 0, True)
            norm_row(T - 2, 1, True)
            keep_turned(T - 3, 0, True)
            norm_row(T - 1, 0, True)
            keep_turned(T - 2, 1, True)
            keep_turned(T - 1, 0, True)

            act.wait_ge(s_sub, 1)
            nc.scalar.activation(probs, probs, ACT.Exp).then_inc(s_exp, 1)
            act.wait_ge(s_topv, 1)
            nc.scalar.activation(vec_a, vec_a, ACT.Exp).then_inc(s_exp2, 1)

            def high_x(b, wait):
                act.wait_ge(s_t, b + 1)
                if wait:
                    act.wait_ge(s_l1, 2 * b)
                for q in range(2):
                    nc.scalar.activation(xh[:, q], cut(q, KD), ACT.Copy, scale=YS).then_inc(s_xhi, 1)

            def gelu(b, wait):
                e = act.value_load(eb_i[0:1, bass.ds(b, 1)], min_val=0, max_val=NE - 1)
                for m in range(KH):
                    act.wait_ge(s_l1, 2 * b + m + 1)
                    if wait:
                        act.wait_ge(s_hlo, 2 * b + m - 1)
                    nc.scalar.activation(g_s[:, m, :], bank[2 + m][:, 0:SB], ACT.Gelu, bias=b1c[:, bass.ds(e * KH + m, 1)], scale=unscale_1).then_inc(s_g, 1)

            act.sem_inc(s_g, 2)
            act.wait_ge(s_tok, 1)
            high_x(0, False)
            gelu(0, False)
            high_x(1, True)
            with act.Fori(1, NSB) as b:
                gelu(b, True)
                high_x(b + 1, True)

        @block.tensor
        def _(pe):
            pe.wait_ge(s_const, 13)
            nc.tensor.matmul(deg_ps[:, 0:T], ones[0:1, 0:P], ones[0:1, 0:T], start=True, stop=False)
            with pe.Fori(0, NB // 2) as i:
                for k in range(2):
                    pe.wait_ge(s_oh, 4 * i + 2 * k + 2)
                    for c in range(OH):
                        mm = nc.tensor.matmul(deg_ps[:, 0:T], oh_l[:, k, :, c], oh_h[:, k, :, c], start=False, stop=False)
                    mm.then_inc(s_ohused, 1)
            nc.tensor.matmul(deg_ps[:, 0:T], zero16[:, 0:P], zero16[:, 0:T], start=False, stop=True).then_inc(s_deg, 1)
            pe.wait_ge(s_rng, 1)
            for a in range(2):
                mm = nc.tensor.transpose(rt_ps[0:T, a * CPART:(a + 1) * CPART], rng[:, a, :], ident[0:CPART, 0:CPART])
            mm.then_inc(s_rt, 1)
            pe.wait_ge(s_rcol, 1)
            nc.tensor.matmul(rt_ps[0:1, 256:256 + T], rcol[:, 2:3], ident[0:T, 0:T], start=True, stop=True)
            nc.tensor.matmul(rt_ps[0:1, 256 + T:256 + 2 * T], rcol[:, 3:4], ident[0:T, 0:T], start=True, stop=True)
            nc.tensor.matmul(rt_ps[0:1, 256 + 2 * T:256 + 3 * T], rcol[:, 4:5], upper[:, :], start=True, stop=True)
            nc.tensor.matmul(rt_ps[0:1, 256 + 3 * T:257 + 3 * T], rcol[:, 4:5], ones[0:T, 0:1], start=True, stop=True).then_inc(s_rrow, 1)

            pe.wait_ge(s_tab, 1)
            pe.wait_ge(s_ytab, 1)
            pe.wait_ge(s_w, 64)
            pe.sem_inc(s_agg, 1)
            pe.sem_inc(s_consumed, RING + CPAD)

            def gather_sum(t, par):
                lo = pe.value_load(tab[0:1, 0, bass.ds(t, 1)], min_val=0, max_val=CPAD - 2)
                hi = pe.value_load(tab[0:1, 1, bass.ds(t, 1)], min_val=0, max_val=CPAD - 2)
                off = pe.value_load(tab[0:1, 2, bass.ds(t, 1)], min_val=0, max_val=T * CPAD + CPAD)
                pe.wait_ge(s_aggs, t + 1)
                nc.tensor.matmul(agg_b[par][:, :], zero16[:, 0:P], zero16[:, 0:D], start=True, stop=False)
                with pe.Fori(lo, hi, 2) as c:
                    s = pe.snap(c + off)
                    pe.wait_ge(s_landed, s + 2)
                    slot = even_slot(pe.snap(s % RING))
                    for q in range(2):
                        w = sel_flat[:, bass.ds(slot * P + q * P, P)]
                        for part in range(2):
                            mm = nc.tensor.matmul(agg_b[par][:, :], w, rows_flat[:, bass.ds(slot * (2 * D) + (2 * q + part) * D, D)], start=False, stop=False)
                        mm.then_inc(s_consumed, 1)
                pe.wait_ge(s_yself, 16 * t + 16)
                nc.tensor.matmul(agg_b[par][:, :], ident16[:, :], yself[:, 0:D], start=False, stop=False)
                nc.tensor.matmul(agg_b[par][:, :], ident16[:, :], yself[:, D:2 * D], start=False, stop=True).then_inc(s_agg, 1)

            def turn(t):
                pe.wait_ge(s_aggs, t + 3)
                for k in range(KD):
                    mm = nc.tensor.transpose(at_ps[:, k, :], agg_s[:, k * P:(k + 1) * P], ident[:, :])
                mm.then_inc(s_at, 1)

            def project(t):
                pe.wait_ge(s_ats, t + 1)
                for m in range(KD):
                    for k in range(KD):
                        mm = nc.tensor.matmul(ht_ps[:, m, :], w_sb[:, k, m * P:(m + 1) * P], agg_ts[:, k, :], start=(k == 0), stop=(k == KD - 1))
                mm.then_inc(s_ht, 1)

            pe.sem_inc(s_aggs, 2)
            pe.sem_inc(s_at, 1)
            gather_sum(0, 0)
            def pair(h):
                for j in range(2):
                    gather_sum(2 * h + j + 1, (j + 1) % 2)
                    turn(2 * h + j)
                    project(2 * h + j)

            with pe.Fori(0, (MAX_FROM + NE) // 2) as h:
                pair(h)
            pe.wait_ge(s_wm, 1)
            for q in range(3):
                mm = nc.tensor.transpose(wm_ps[:, q, :], wmb[:, q, :], ident[:, :])
            mm.then_inc(s_wmt, 1)
            with pe.Fori((MAX_FROM + NE) // 2, T // 2) as h:
                pair(h)
            turn(T - 1)
            project(T - 1)

            pe.wait_ge(s_gate, 16)

            def turn_gelu(t, j, steady):
                pe.wait_ge(s_gelu, t + 1)
                if steady:
                    pe.wait_ge(s_x1, t - 1)
                for m in range(KD):
                    mm = nc.tensor.transpose(bank[j][:, m * P:(m + 1) * P], g_tile[:, j, m, :], ident[:, :])
                mm.then_inc(s_t1, 1)

            def turn_norm(t, j, steady):
                pe.wait_ge(s_xn, t + 1)
                if steady:
                    pe.wait_ge(s_xT, t - 1)
                for m in range(KD):
                    mm = nc.tensor.transpose(bank[2 + j][:, m * P:(m + 1) * P], xn[:, j, m * P:(m + 1) * P], ident[:, :])
                mm.then_inc(s_t2, 1)

            def gate_logits(t, j, steady):
                pe.wait_ge(s_xT, t + 1)
                if steady:
                    pe.wait_ge(s_lgc, t - 1)
                for m in range(KD):
                    mm = nc.tensor.matmul(bank[4 + j][:, 0:EXPERTS], x_ts[:, j, m, :], gate[:, m, :], start=(m == 0), stop=(m == KD - 1))
                mm.then_inc(s_lg, 1)

            turn_gelu(0, 0, False)
            turn_gelu(1, 1, False)
            turn_norm(0, 0, False)
            turn_gelu(2, 0, True)
            turn_norm(1, 1, False)
            gate_logits(0, 0, False)
            turn_gelu(3, 1, True)
            turn_norm(2, 0, True)
            gate_logits(1, 1, False)
            with pe.Fori(2, T // 2) as h:
                for j in range(2):
                    turn_gelu(2 * h + j, j, True)
                    turn_norm(2 * h + j - 1, 1 - j, True)
                    gate_logits(2 * h + j - 2, j, True)
            turn_gelu(T - 1, 0, True)
            turn_norm(T - 2, 1, True)
            gate_logits(T - 3, 0, True)
            turn_norm(T - 1, 0, True)
            gate_logits(T - 2, 1, True)
            gate_logits(T - 1, 0, True)

            pe.wait_ge(s_mask, 1)
            mflat = mask16.rearrange("p t e -> p (t e)")
            HG = T * EXPERTS // 2
            for h in range(2):
                nc.tensor.matmul(bank[h][:, 0:HG], upper16[:, :], mflat[:, h * HG:(h + 1) * HG], start=True, stop=True)
                mm = nc.tensor.matmul(bank[2 + h][:, 0:HG], ones16[:, :], mflat[:, h * HG:(h + 1) * HG], start=True, stop=True)
            mm.then_inc(s_rank, 1)
            nc.tensor.matmul(bank[4][:, 0:2 * RB], zero16[:, 0:P], zero16[:, 0:2 * RB], start=True, stop=False)
            with pe.Fori(0, T) as t:
                for k in range(TOP):
                    pe.wait_ge(s_ohr, t * TOP + k + 1)
                    nc.tensor.matmul(bank[4][:, 0:2 * RB], oh_r[:, k % 2, :], oh_b[:, k % 2].rearrange("p a b -> p (a b)"), start=False, stop=False).then_inc(s_inv, 1)
            nc.tensor.matmul(bank[4][:, 0:2 * RB], zero16[:, 0:P], zero16[:, 0:2 * RB], start=False, stop=True).then_inc(s_inv, 1)

            def turn_rows(b):
                pe.wait_ge(s_xg, 32 * b + 32)
                for q in range(2):
                    for m in range(KD):
                        mm = nc.tensor.transpose(bank[q][:, m * P:(m + 1) * P], xg[:, q, m * P:(m + 1) * P], ident[:, :])
                mm.then_inc(s_t, 1)

            def superblock(b, w):
                W1 = wsb[:, w, 0:2 * WL].rearrange("p (s k n) -> p s k n", s=2, k=KD)
                W2 = wsb[:, w, 2 * WL:4 * WL].rearrange("p (s k n) -> p s k n", s=2, k=KH)
                pe.wait_ge(s_xlo, b + 1)
                for m in range(KH):
                    pe.wait_ge(s_g, 2 * b + m + 1)
                    o = bank[2 + m][:, 0:SB].rearrange("p (q n) -> p q n", q=2)
                    for k in range(KD):
                        for u, v in ((0, xh), (0, xl), (1, xh)):
                            mm = nc.tensor.matmul(o, W1[:, u, k, m * P:(m + 1) * P], v[:, :, k, :], start=(k == 0 and u == 0 and v is xh),
                                                  stop=(k == KD - 1 and u == 1))
                    mm.then_inc(s_l1, 1)
                turn_rows(b + 1)
                pe.wait_ge(s_y, 2 * b + 2)
                for m in range(KH):
                    pe.wait_ge(s_hlo, 2 * b + m + 1)
                    for q in range(2):
                        for u, v in ((0, hh), (0, hl), (1, hh)):
                            mm = nc.tensor.matmul(bank[4 + q][:, :], v[:, m, q * P:(q + 1) * P], W2[:, u, m, :], start=(m == 0 and u == 0 and v is hh),
                                                  stop=(m == KH - 1 and u == 1))
                mm.then_inc(s_l2, 1)

            pe.wait_ge(s_tok, 1)
            pe.sem_inc(s_y, 2)
            turn_rows(0)
            with pe.Fori(0, NE // 2) as i:
                for w in range(2):
                    pe.wait_ge(s_wl[w], 16 * i + 16)
                    pe.sem_inc(s_go, 1)
                    b_from = pe.value_load(start_i[0:1, bass.ds(2 * i + w, 1)], min_val=0, max_val=NSB)
                    b_to = pe.value_load(start_i[0:1, bass.ds(2 * i + w + 1, 1)], min_val=1, max_val=NSB)
                    with pe.Fori(b_from, b_to) as b:
                        superblock(b, w)


def kernel(x, src, dst, L0_gnn_W, L0_gnn_b, L0_gnn_gamma, L0_gnn_beta, L0_ffn_gate_w, L0_ffn_re_w1, L0_ffn_re_b1, L0_ffn_re_w2, L0_ffn_re_b2, L0_ffn_se_w1, L0_ffn_se_b1, L0_ffn_se_w2, L0_ffn_se_b2):
    import numpy as np
    import concourse.bacc as bacc
    from concourse.bass_utils import run_bass_kernel_spmd

    nc = bacc.Bacc("TRN2", target_bir_lowering=False, num_devices=1)
    edges = CPAD * P - EDGES
    dst_rows = np.pad(np.asarray(dst), (0, edges), constant_values=NP).reshape(CPAD, P)
    src_rows = np.pad(np.asarray(src), (0, edges)).reshape(CPAD, P)
    laid = {
        "x": np.pad(np.asarray(x), ((0, NP - N), (0, 0))),
        "src_cols": src_rows.T, "dst_cols": dst_rows.T, "dst_rows": dst_rows,
        "w_t": np.asarray(L0_gnn_W).T,
        "b_cols": np.asarray(L0_gnn_b).reshape(KD, P).T,
        "gamma_cols": np.asarray(L0_gnn_gamma).reshape(KD, P).T,
        "beta_cols": np.asarray(L0_gnn_beta).reshape(KD, P).T,
        "gate_t": np.asarray(L0_ffn_gate_w).T,
        "w1": np.concatenate([np.asarray(L0_ffn_re_w1), np.asarray(L0_ffn_se_w1)]),
        "b1_cols": np.concatenate([np.asarray(L0_ffn_re_b1), np.asarray(L0_ffn_se_b1)]).reshape(NE * KH, P).T,
        "w2": np.concatenate([np.asarray(L0_ffn_re_w2), np.asarray(L0_ffn_se_w2)]),
        "b2": np.concatenate([np.asarray(L0_ffn_re_b2), np.asarray(L0_ffn_se_b2)]),
    }
    arrays, args = {}, []
    for name, a in laid.items():
        a = np.ascontiguousarray(a)
        arrays[f"in_{name}"] = a
        args.append(nc.dram_tensor(f"in_{name}", a.shape, mybir.dt.from_np(a.dtype), kind="ExternalInput").ap())
    args.append(nc.dram_tensor("out_x", (NP, D), F32, kind="ExternalOutput").ap())
    gnn_ffn(nc, *args)
    r = run_bass_kernel_spmd(nc, [arrays], core_ids=[0])
    return r.results[0]["out_x"][:N]
```

```python
from contextlib import ExitStack

import concourse.bass as bass
from concourse import mybir

F32 = mybir.dt.float32
F16 = mybir.dt.float16
I32 = mybir.dt.int32
ALU = mybir.AluOpType
ACT = mybir.ActivationFunctionType
AX = mybir.AxisListType

P = 128
N = 6250
D = 512
KD = D // P
T = -(-N // P)
NP = T * P
LAST = N - (T - 1) * P
EDGES = 106250
CHUNKS = -(-EDGES // P)
RING = 16
PACK = 2
LAG_PACKS = 3
LAG = (LAG_PACKS + 1) * PACK
CPART, CBLK = 128, 7
CPAD = CPART * CBLK
OH = 28
NB = CPAD // OH
GRP = 7
BIG = 1000
YS = 1024.0
EPS = 1e-5
HID = 256
KH = HID // P
EXPERTS = 16
SHARED = 2
NE = EXPERTS + SHARED
TOP = 4
SB = 2 * P
ROUTED_SB = (NP * TOP + EXPERTS * SB) // SB
SHARED_SB = -(-NP // SB)
RB = 2 * ROUTED_SB
UNITS = SHARED * KH
WL = KD * HID
MAX_FROM, SPLIT_FROM = 2, 29
assert ROUTED_SB % 2 == 0 and SHARED == 2 and EXPERTS % 2 == 0 and T == 2 * SHARED_SB - 1 and SHARED_SB % 2 == 1 and KH * D == WL and 2 * (SPLIT_FROM - (MAX_FROM + NE + 1)) > LAG and SPLIT_FROM + NE <= T
assert CPAD >= CHUNKS + RING - 1 and NB % 2 == 0 and T == GRP * GRP


def gnn_ffn(nc, x, src_cols, dst_cols, dst_rows, w_t, b_cols, gamma_cols, beta_cols, gate_t, w1, b1_cols, w2, b2, out):
    ytab = nc.dram_tensor("ytab", [NP, 2 * D], F16, kind="Internal").ap()
    x1tab = nc.dram_tensor("x1tab", [NP, D], F32, kind="Internal").ap()
    xntab = nc.dram_tensor("xntab", [NP, 2 * D], F16, kind="Internal").ap()
    wtab = nc.dram_tensor("wtab", [NE, P, 4 * WL], F16, kind="Internal").ap()
    btab = nc.dram_tensor("btab", [ROUTED_SB * SB, D], F32, kind="Internal").ap()

    with ExitStack() as ctx:
        def sb(name, shape, dt):
            return ctx.enter_context(nc.sbuf_tensor(name, shape, dt))

        def ps(name, shape, dt):
            return ctx.enter_context(nc.psum_tensor(name, shape, dt))

        def sem(name):
            return ctx.enter_context(nc.semaphore(name))

        big = sb("big", [P, T * D], F32)
        x_all = big[:, :].rearrange("p (t d) -> p t d", d=D)
        h_t = big[:, :].rearrange("p (k n) -> p k n", k=KD)
        src_i = sb("src_i", [P, CPAD], I32)
        dst_i = sb("dst_i", [P, CPAD], I32)
        dst_f = sb("dst_f", [P, CPAD], F32)
        wspl = sb("wspl", [P, 2, 4 * WL], F16)
        wspl_flat = wspl[:, :, :].rearrange("p b n -> p (b n)")
        dst_h = wspl_flat[:, 0:CPAD]
        dst_l = wspl_flat[:, CPAD:2 * CPAD]
        tmp_i = wspl_flat[:, 2 * CPAD:4 * CPAD].bitcast(I32)
        dr_i = wspl_flat[0:CPART, 4 * CPAD:6 * CPAD].bitcast(I32).rearrange("p (b j) -> p b j", j=P)
        arena = sb("arena", [P, RING * 2 * D], F16)
        oh_l = arena[:, 0:2 * P * OH].rearrange("p (b j c) -> p b j c", b=2, c=OH)
        iota_rep = arena[:, 2 * P * OH:3 * P * OH].rearrange("p (j c) -> p j c", c=OH)
        oh_h = arena[:, 3 * P * OH:3 * P * OH + 2 * T * OH].rearrange("p (b j c) -> p b j c", b=2, c=OH)
        z = arena[:, 0:2 * GRP * D].bitcast(F32).rearrange("p (k d) -> p k d", d=D)
        yrow = arena[:, 2 * GRP * D:4 * GRP * D].rearrange("p (k d) -> p k d", d=2 * D)
        cnd_at = (3 * P + 2 * T) * OH
        cnd = arena[0:CPART, cnd_at:cnd_at + 8 * T * CBLK].bitcast(F32).rearrange("p (a t b) -> p a t b", a=4, b=CBLK)
        iota16 = sb("iota16", [P, P], F16)
        iota_t = sb("iota_t", [P, T], F32)
        tbase = sb("tbase", [P, T], F32)
        chunk_id = sb("chunk_id", [CPART, CBLK], F32)
        mn = sb("mn", [CPART, CBLK], F32)
        mx = sb("mx", [CPART, CBLK], F32)
        rng = sb("rng", [CPART, 2, T], F32)
        rcol = sb("rcol", [T, 8], F32)
        def even_slot(slot):
            return nc.s_assert_within(slot, 0, RING - 2, skip_runtime_bounds_check_because="the count of steps is even")

        rcol_i = sb("rcol_i", [T, 2], I32)
        rrow = sb("rrow", [1, 8, T], F32)
        tab = sb("tab", [1, 3, T], I32)
        tot = sb("tot", [1, 8], F32)
        toti = sb("toti", [1, 4], I32)
        ident = sb("ident", [P, P], F32)
        upper16 = sb("upper16", [P, P], F16)
        ones16 = sb("ones16", [P, P], F16)
        ident16 = sb("ident16", [P, P], F16)
        upper = sb("upper", [T, T], F32)
        ones = sb("ones", [P, P], F32)
        zero16 = sb("zero16", [1, D], F16)
        deg = sb("deg", [P, T], F32)
        mhalf = sb("mhalf", [P, T], F32)
        dinv = sb("dinv", [P, T], F32)
        dinv_ys = sb("dinv_ys", [P, T], F32)
        wraw = sb("wraw", [P, 2, 2, WL], F32)
        st6 = wraw[:, 0, 0, 0:T * 6].rearrange("p (t s) -> p t s", s=6)
        mv = sb("mv", [P, T, 2], F32)
        veps = sb("veps", [P, T], F32)
        rstd = sb("rstd", [P, T], F32)
        ysc = sb("ysc", [P, T], F32)
        ybi = sb("ybi", [P, T], F32)
        rows = arena[:, 0:RING * 2 * D].rearrange("p (k d) -> p k d", k=RING)
        idx = sb("idx", [P, RING], I32)
        sel = sb("sel", [P, RING, P], F16)
        rows_flat = arena[:, 0:RING * 2 * D]
        sel_flat = sel[:, :, :].rearrange("p k n -> p (k n)")
        yself = sb("yself", [P, 2 * D], F16)
        agg_s = sb("agg_s", [P, D], F32)
        agg_ts = sb("agg_ts", [P, KD, P], F32)
        w_sb = sb("w_sb", [P, KD, D], F32)
        bcol = sb("bcol", [P, 3, KD], F32)
        hst = sb("hst", [P, KD, T, 6], F32)
        hmv = sb("hmv", [P, KD, 2], F32)

        wmx = sb("wmx", [P, 2, NE], F32)
        wm3 = sb("wm3", [P, 4], F32)
        wmb = sb("wmb", [P, 3, P], F32)
        wex_i = sb("wex_i", [P, 8], I32)
        wex_f = sb("wex_f", [P, 8], F32)
        wex_s = sb("wex_s", [P, 8], I32)
        scl = wex_s[:, :].bitcast(F32)
        scale_w1, scale_w2, scale_h, unscale_1, unscale_2 = (scl[:, i:i + 1] for i in range(5))
        b1c = sb("b1c", [P, NE * KH], F32)
        bn_a = sb("bn_a", [P, KD], F32)
        bn_b = sb("bn_b", [P, KD], F32)
        bn_v = sb("bn_v", [P, KD], F32)
        gate = sb("gate", [P, KD, EXPERTS], F32)
        c1 = sb("c1", [P, T], F32)
        c2 = sb("c2", [P, T], F32)
        mv2 = sb("mv2", [P, 2, 2], F32)
        st2 = sb("st2", [P, 2, 6], F32)
        ve2 = sb("ve2", [P, 2], F32)
        r2 = sb("r2", [P, 2], F32)
        nb2 = sb("nb2", [P, 2], F32)
        idx4 = sb("idx4", [P, 2, TOP], I32)
        idx2 = sb("idx2", [P, 2, 2], I32)
        start_f = sb("start_f", [1, EXPERTS + 1], F32)
        start_i = sb("start_i", [1, EXPERTS + 1], I32)
        eb_i = sb("eb_i", [1, ROUTED_SB], I32)

        big16 = big[:, :].bitcast(F16)

        def views(base, specs):
            at, out_views = 0, []
            for shape, dt in specs:
                size = 1
                for q in shape:
                    size *= q
                width = size if dt == F16 else 2 * size
                v = base[:, at:at + width]
                if dt != F16:
                    v = v.bitcast(dt)
                if len(shape) > 1:
                    names = "abcd"[:len(shape)]
                    v = v.rearrange("p (" + " ".join(names) + ") -> p " + " ".join(names), **dict(zip(names, shape)))
                out_views.append(v)
                at += width
            return out_views

        logits, wk, slot_i, tok_i = views(wraw[:, :, :, :].rearrange("p a b n -> p (a b n)").bitcast(F16), [
            ((T, EXPERTS), F32), ((T, TOP), F32), ((T, TOP), I32), ((2 * ROUTED_SB + 2,), I32)])
        xr, x1, xn, x_ts, g_tile = views(arena, [((2, D), F32)] * 3 + [((2, KD, P), F32)] * 2)
        xn_row, b2s = views(arena[:, 12288:], [((2, 2 * D), F16), ((SHARED, D), F32)])
        x1b = sel_flat.bitcast(F32).rearrange("p (a d) -> p a d", a=2)
        G = (T, EXPERTS)
        (probs, hot, tmp_a, tmp_b, cum_a, cum_b, rank_s, mask16, rev16, top_v, vec_a, vec_b, r_f, b_f, tval,
         oh_r, oh_b, iota_b, pcol, ebt, iota_sb) = views(big16, [
            (G, F32), ((TOP,) + G, F32), (G, F32), (G, F32), (G, F32), (G, F32), (G, F32), (G, F16), (G, F32), ((TOP, T), F32),
            ((TOP, T), F32), ((TOP, T), F32), ((T, TOP), F32), ((T, TOP), F32), ((T,), F32),
            ((2, P), F16), ((2, 2, RB), F16), ((RB,), F16), ((2,), F32), ((ROUTED_SB, EXPERTS), F32), ((ROUTED_SB,), F32)])
        (tot_e, pre_e, pre_e2, blk_e) = views(arena[:, 10240:], [((EXPERTS,), F32), ((EXPERTS,), F32), ((EXPERTS,), F32), ((EXPERTS,), I32)])
        tok_f = views(arena[:, 11264:], [((2 * ROUTED_SB + 2,), F32)])[0]
        wsb, b2r, xg, x_hl, g_s, hh, hl, y_s, xs = views(big16, [
            ((2, 4 * WL), F16), ((EXPERTS, D), F32), ((2, 2 * D), F16), ((2, 2, KD, P), F16),
            ((KH, SB), F32), ((KH, SB), F16), ((KH, SB), F16), ((2, 2, D), F32), ((2, 2, 2 * D), F16)])
        yk, x1r, acc, gs_s, hhs, hls = views(arena, [
            ((2, TOP, D), F32), ((2, D), F32), ((2, D), F32), ((UNITS, SB), F32), ((UNITS, SB), F16), ((UNITS, SB), F16)])
        half_unscale = wex_f[:, 5:6]

        bank = [ps(f"bank{i}", [P, 512], F32) for i in range(8)]
        deg_ps, rt_ps = bank[0], bank[1]
        agg_b = [bank[2], bank[3]]

        def cut(b, k, w=P):
            return bank[b][:, 0:k * w].rearrange("p (k n) -> p k n", k=k)

        turned = [[bank[q + 6 * u][:, :].bitcast(F16)[:, 0:D].rearrange("p (k n) -> p k n", k=KD) for u in range(2)] for q in range(2)]
        at_ps, ht_ps, wm_ps = cut(4, KD), cut(5, KD), cut(6, 3)

        s_wraw0 = sem("s_wraw0")
        s_wraw1 = sem("s_wraw1")
        s_wused = sem("s_wused")
        s_wlo = sem("s_wlo")
        s_wst0 = sem("s_wst0")
        s_wst1 = sem("s_wst1")
        s_wm = sem("s_wm")
        s_wmt = sem("s_wmt")
        s_mx = sem("s_mx")
        s_b1 = sem("s_b1")
        s_gate = sem("s_gate")
        s_bnv = sem("s_bnv")
        s_bnr = sem("s_bnr")
        s_bn = sem("s_bn")
        s_gelu = sem("s_gelu")
        s_xr0 = sem("s_xr0")
        s_xr1 = sem("s_xr1")
        s_u = sem("s_u")
        s_t1 = sem("s_t1")
        s_x1 = sem("s_x1")
        s_ve2 = sem("s_ve2")
        s_r2 = sem("s_r2")
        s_nb2 = sem("s_nb2")
        s_xn = sem("s_xn")
        s_t2 = sem("s_t2")
        s_xT = sem("s_xT")
        s_lg = sem("s_lg")
        s_lgc = sem("s_lgc")
        s_x1st0 = sem("s_x1st0")
        s_x1st1 = sem("s_x1st1")
        s_xnst0 = sem("s_xnst0")
        s_xnst1 = sem("s_xnst1")
        s_atab = sem("s_atab")
        s_bc = sem("s_bc")
        s_sub = sem("s_sub")
        s_exp = sem("s_exp")
        s_topv = sem("s_topv")
        s_exp2 = sem("s_exp2")
        s_mask = sem("s_mask")
        s_rank = sem("s_rank")
        s_route = sem("s_route")
        s_ohr = sem("s_ohr")
        s_inv = sem("s_inv")
        s_tok = sem("s_tok")
        s_b2 = sem("s_b2")
        s_wl0 = sem("s_wl0")
        s_wl1 = sem("s_wl1")
        s_ig = sem("s_ig")
        s_xg = [sem(f"s_xg{q}") for q in range(2)]
        s_b2s = sem("s_b2s")
        s_x1b = sem("s_x1b")
        s_xnh = sem("s_xnh")
        s_xnl = sem("s_xnl")
        s_xs = [sem(f"s_xs{w}") for w in range(2)]
        s_st = sem("s_st")
        s_sxh = sem("s_sxh")
        s_sxl = sem("s_sxl")
        s_sl1 = sem("s_sl1")
        s_sg = sem("s_sg")
        s_shh = sem("s_shh")
        s_shl = sem("s_shl")
        s_sl2 = sem("s_sl2")
        s_base = sem("s_base")
        s_t = sem("s_t")
        s_xhi = sem("s_xhi")
        s_xlo = sem("s_xlo")
        s_l1 = sem("s_l1")
        s_g = sem("s_g")
        s_hlo = sem("s_hlo")
        s_l2 = sem("s_l2")
        s_y = sem("s_y")
        s_bst0 = sem("s_bst0")
        s_bst1 = sem("s_bst1")
        s_btab = sem("s_btab")
        s_i4 = sem("s_i4")
        s_yk0 = sem("s_yk0")
        s_yk1 = sem("s_yk1")
        s_fl0 = sem("s_fl0")
        s_fl1 = sem("s_fl1")
        s_acc = sem("s_acc")
        s_ost0 = sem("s_ost0")
        s_ost1 = sem("s_ost1")
        s_wraw, s_wst, s_xr, s_x1st, s_xnst = [s_wraw0, s_wraw1], [s_wst0, s_wst1], [s_xr0, s_xr1], [s_x1st0, s_x1st1], [s_xnst0, s_xnst1]
        s_wl, s_bst, s_yk, s_fl, s_ost = [s_wl0, s_wl1], [s_bst0, s_bst1], [s_yk0, s_yk1], [s_fl0, s_fl1], [s_ost0, s_ost1]
        s_dst = sem("s_dst")
        s_whi = sem("s_whi")
        s_st2 = sem("s_st2")
        s_mv2 = sem("s_mv2")
        s_hhi = sem("s_hhi")
        s_fd = sem("s_fd")
        s_hst = sem("s_hst")
        s_src = sem("s_src")
        s_x = sem("s_x")
        s_w = sem("s_w")
        s_const = sem("s_const")
        s_cdve = sem("s_cdve")
        s_oh = sem("s_oh")
        s_ohused = sem("s_ohused")
        s_deg = sem("s_deg")
        s_degs = sem("s_degs")
        s_dinv = sem("s_dinv")
        s_veps = sem("s_veps")
        s_rstd = sem("s_rstd")
        s_rng = sem("s_rng")
        s_rt = sem("s_rt")
        s_rcol = sem("s_rcol")
        s_rrow = sem("s_rrow")
        s_tab = sem("s_tab")
        s_ysc = sem("s_ysc")
        s_z = sem("s_z")
        s_yhi = sem("s_yhi")
        s_ylo = sem("s_ylo")
        s_yst = [sem(f"s_yst{k}") for k in range(GRP)]
        s_ytab = sem("s_ytab")
        s_idx = sem("s_idx")
        s_sel = sem("s_sel")
        s_gather = [sem(f"s_gather{k}") for k in range(RING // PACK)]
        s_landed = sem("s_landed")
        s_consumed = sem("s_consumed")
        s_yself = sem("s_yself")
        s_agg = sem("s_agg")
        s_aggs = sem("s_aggs")
        s_at = sem("s_at")
        s_ats = sem("s_ats")
        s_ht = sem("s_ht")
        s_hts = sem("s_hts")
        s_pool = sem("s_pool")
        s_hmv = sem("s_hmv")
        s_out = sem("s_out")
        s_go = sem("s_go")

        block = ctx.enter_context(nc.Block())

        @block.sync
        def _(sp):
            sp.dma_start(dst_i[:, :], dst_cols).then_inc(s_dst, 16)
            sp.dma_start(dr_i[:, :, :], dst_rows.rearrange("(b p) j -> p b j", p=CPART)).then_inc(s_dst, 16)
            sp.dma_start(src_i[:, :], src_cols).then_inc(s_src, 16)
            xv = x.rearrange("(t p) d -> p t d", p=P)
            for g in range(GRP):
                sp.dma_start(x_all[:, g * GRP:(g + 1) * GRP, :], xv[:, g * GRP:(g + 1) * GRP, :]).then_inc(s_x, 16)
            sp.dma_start(w_sb[:, :, :], w_t.rearrange("(k p) n -> p k n", p=P)).then_inc(s_w, 16)
            sp.dma_start(bcol[:, 0, :], b_cols).then_inc(s_w, 16)
            sp.dma_start(bcol[:, 1, :], gamma_cols).then_inc(s_w, 16)
            sp.dma_start(bcol[:, 2, :], beta_cols).then_inc(s_w, 16)
            yv = ytab.rearrange("(t p) d -> p t d", p=P)
            with sp.Fori(0, GRP) as g:
                for k in range(GRP):
                    sp.wait_ge(s_ylo, g * GRP + k + 1)
                    sp.dma_start(yv[:, bass.ds(g * GRP + k, 1), :], yrow[:, k:k + 1, :]).then_inc(s_yst[k], 16)
            for k in range(GRP):
                sp.wait_ge(s_yst[k], 16 * GRP)
            sp.sem_inc(s_ytab, 1)
            sp.dma_start(b1c[:, :], b1_cols).then_inc(s_b1, 16)
            sp.dma_start(gate[:, :, :], gate_t.rearrange("(k p) e -> p k e", p=P)).then_inc(s_gate, 16)

            def load_raw(e, j):
                sp.dma_start(wraw[:, j, 0, :].rearrange("p (k n) -> p k n", k=KD), w1[bass.ds(e, 1)].rearrange("e (k p) n -> p (e k) n", p=P)).then_inc(s_wraw[j], 16)
                sp.dma_start(wraw[:, j, 1, :].rearrange("p (k n) -> p k n", k=KH), w2[bass.ds(e, 1)].rearrange("e (k p) n -> p (e k) n", p=P)).then_inc(s_wraw[j], 16)

            for j in range(2):
                load_raw(j, j)
            with sp.Fori(1, NE // 2) as i:
                for j in range(2):
                    sp.wait_ge(s_wused, 2 * i + j - 1)
                    load_raw(2 * i + j, j)
            for j in range(2):
                sp.wait_ge(s_wused, NE + j - 1)
                load_raw(j, j)
            with sp.Fori(0, NE // 2 - 1) as i:
                for j in range(2):
                    sp.wait_ge(s_wlo, 2 * i + j + 1)
                    sp.dma_start(wtab[bass.ds(2 * i + j, 1)].rearrange("e p n -> p (e n)"), wspl[:, j, :]).then_inc(s_wst[j], 16)
                    load_raw(2 * i + j + 2, j)
            for j in range(2):
                sp.wait_ge(s_wlo, NE - 1 + j)
                sp.dma_start(wtab[NE - 2 + j], wspl[:, j, :]).then_inc(s_wst[j], 16)

            sp.wait_ge(s_hmv, 1)
            xt = lambda tab, t: tab[bass.ds(t * P, P), :]
            sp.dma_start(b2s, b2[EXPERTS:NE].unsqueeze(0).to_broadcast([P, SHARED, D])).then_inc(s_b2s, 16)

            def store_rows(t, j):
                sp.wait_ge(s_x1b, t + 1)
                sp.dma_start(xt(x1tab, t), x1b[:, j, :]).then_inc(s_x1st[j], 16)
                sp.wait_ge(s_xnl, t + 1)
                sp.dma_start(xt(xntab, t), xn_row[:, j, :]).then_inc(s_xnst[j], 16)

            for t in range(2):
                sp.dma_start(xr[:, t, :], xt(x, t)).then_inc(s_xr[t], 16)
            with sp.Fori(1, T // 2) as h:
                for j in range(2):
                    sp.wait_ge(s_u, 2 * h + j - 1)
                    sp.dma_start(xr[:, j, :], xt(x, 2 * h + j)).then_inc(s_xr[j], 16)
                    store_rows(2 * h + j - 2, j)
            sp.wait_ge(s_u, T - 2)
            sp.dma_start(xr[:, 0, :], xt(x, T - 1)).then_inc(s_xr[0], 16)
            for t in range(T - 3, T):
                store_rows(t, t % 2)
            for j in range(2):
                sp.wait_ge(s_x1st[j], 16 * ((T + 1 - j) // 2))
                sp.wait_ge(s_xnst[j], 16 * ((T + 1 - j) // 2))
                sp.wait_ge(s_wst[j], 16 * (NE // 2))
            sp.sem_inc(s_atab, 1)

            sp.wait_ge(s_tok, 1)
            sp.dma_start(b2r[:, :, :], b2[0:EXPERTS].unsqueeze(0).to_broadcast([P, EXPERTS, D])).then_inc(s_b2, 16)
            for j in range(2):
                sp.dma_start(wsb[:, j, :], wtab[j]).then_inc(s_wl[j], 16)

            def load_xs(s, w, nq):
                sp.dma_start(xs[:, w, 0:nq, :], xntab[bass.ds(s * SB, nq * P), :].rearrange("(q p) d -> p q d", q=nq)).then_inc(s_xs[w], 16)

            def load_x1(t, q):
                sp.dma_start(x1r[:, q, :], xt(x1tab, t)).then_inc(s_fl[q], 16)

            for w in range(2):
                load_xs(w, w, 2)
                load_x1(w, w)
            with sp.Fori(1, NE // 2) as i:
                for j in range(2):
                    done = sp.value_load(start_i[0:1, bass.ds(2 * i + j - 1, 1)], min_val=1, max_val=ROUTED_SB)
                    sp.wait_ge(s_l2, done)
                    sp.dma_start(wsb[:, j, :], wtab[bass.ds(2 * i + j, 1)].rearrange("e p n -> p (e n)")).then_inc(s_wl[j], 16)

            def store_out(t, q):
                sp.wait_ge(s_acc, t + 1)
                sp.dma_start(xt(out, t), acc[:, q, :]).then_inc(s_ost[q], 16)

            def refill(s, w, xs_nq, x1_nq):
                if xs_nq:
                    sp.wait_ge(s_st, 2 * s)
                    load_xs(s + 1, w, xs_nq)
                for q in range(x1_nq):
                    sp.wait_ge(s_base, 2 * s + q + 1)
                    load_x1(2 * s + q, q)
                for q in range(2):
                    store_out(2 * s - 2 + q, q)

            with sp.Fori(1, SHARED_SB // 2) as h:
                for j in range(2):
                    refill(2 * h + j - 1, j, 2, 2)
            refill(SHARED_SB - 2, 0, 1, 2)
            refill(SHARED_SB - 1, 1, 0, 1)
            store_out(T - 1, 0)
            for j in range(2):
                sp.wait_ge(s_ost[j], 16 * ((T + 1 - j) // 2))

        @block.gpsimd
        def _(pool):
            n = [0]

            def link(ins):
                n[0] += 1
                ins.then_inc(s_pool, 1)
                pool.wait_ge(s_pool, n[0])

            pool.iota(iota_rep[:, :, :], [[1, P], [0, OH]], base=0, channel_multiplier=0,
                      allow_small_or_imprecise_dtypes=True).then_inc(s_const, 1)
            pool.iota(iota16[:, :], [[1, P]], base=0, channel_multiplier=0,
                      allow_small_or_imprecise_dtypes=True).then_inc(s_const, 1)
            pool.iota(iota_t[:, :], [[1, T]], base=0, channel_multiplier=0,
                      allow_small_or_imprecise_dtypes=True).then_inc(s_const, 1)
            pool.iota(tbase[:, :], [[P, T]], base=0, channel_multiplier=0,
                      allow_small_or_imprecise_dtypes=True).then_inc(s_const, 1)
            pool.iota(chunk_id[:, :], [[CPART, CBLK]], base=0, channel_multiplier=1,
                      allow_small_or_imprecise_dtypes=True).then_inc(s_const, 1)
            pool.memset(ones[:, :], 1.0).then_inc(s_const, 1)
            pool.memset(mhalf[:, :], -0.5).then_inc(s_const, 1)
            pool.memset(zero16[:, :], 0.0).then_inc(s_const, 1)
            pool.memset(ones16[:, :], 1.0).then_inc(s_const, 1)
            pool.wait_ge(s_const, 9)
            pool.affine_select(out=ident[:, :], in_=ones[:, :], pattern=[[-1, P]], compare_op=ALU.is_equal,
                               fill=0.0, base=0, channel_multiplier=1).then_inc(s_const, 1)
            pool.affine_select(out=upper[:, :], in_=ones[0:T, 0:T], pattern=[[1, T]], compare_op=ALU.is_gt,
                               fill=0.0, base=0, channel_multiplier=-1).then_inc(s_const, 1)
            pool.affine_select(out=upper16[:, :], in_=ones16[:, :], pattern=[[1, P]], compare_op=ALU.is_gt,
                               fill=0.0, base=0, channel_multiplier=-1).then_inc(s_const, 1)
            pool.wait_ge(s_const, 12)
            pool.tensor_copy(ident16[:, :], ident[:, :]).then_inc(s_const, 1)
            pool.wait_ge(s_degs, 1)
            pool.tensor_tensor(dinv[:, :], deg[:, :], mhalf[:, :], ALU.pow).then_inc(s_dinv, 1)
            pool.wait_ge(s_veps, 1)
            pool.tensor_tensor(rstd[:, :], veps[:, :], mhalf[:, :], ALU.pow).then_inc(s_rstd, 1)
            pool.wait_ge(s_tab, 1)
            groups = pool.value_load(toti[0:1, 0:1], min_val=1, max_val=T * CPAD // RING)
            pool.wait_ge(s_ytab, 1)
            pool.sem_inc(s_landed, CPAD)
            def gathers(g, first):
                for q in range(RING // PACK):
                    pool.wait_ge(s_sel, CPAD + g * RING + (q + 1) * PACK)
                    pool.sem_inc(s_go, 1)
                    for k in range(q * PACK, (q + 1) * PACK):
                        pool.indirect_dma_start(rows[:, k, :], None, ytab, bass.IndirectOffsetOnAxis(ap=idx[:, k:k + 1], axis=0)).then_inc(s_gather[q], 16)
                    if q >= LAG_PACKS or not first:
                        pool.wait_ge(s_gather[(q - LAG_PACKS) % (RING // PACK)], (g + 1 if q >= LAG_PACKS else g) * 16 * PACK)
                        pool.sem_inc(s_landed, PACK)

            gathers(0, True)
            with pool.Fori(1, groups) as g:
                gathers(g, False)
            for q in range(RING // PACK - LAG_PACKS, RING // PACK):
                pool.wait_ge(s_gather[q], groups * 16 * PACK)
                pool.sem_inc(s_landed, PACK)


            pool.wait_ge(s_bnv, 1)
            pool.tensor_tensor(bn_a[:, :], bn_v[:, :], mhalf[:, 0:KD], ALU.pow).then_inc(s_bnr, 1)

            def rstd2(t, j, steady):
                pool.wait_ge(s_ve2, t + 1)
                pool.sem_inc(s_go, 1)
                pool.tensor_tensor(r2[:, j:j + 1], ve2[:, j:j + 1], mhalf[:, 0:1], ALU.pow).then_inc(s_r2, 1)
                if steady:
                    pool.wait_ge(s_x1st[j], 8 * (t - j))
                    pool.sem_inc(s_go, 1)
                pool.tensor_tensor(x1b[:, j, :], x1[:, j, :], b2s[:, 0, :], ALU.add).then_inc(s_x1b, 1)

            pool.wait_ge(s_b2s, 16)
            link(pool.tensor_tensor(b2s[:, 0, :], b2s[:, 0, :], b2s[:, 1, :], ALU.add))
            link(pool.tensor_scalar(b2s[:, 0, :], b2s[:, 0, :], 1.0 / SHARED, None, ALU.mult))
            for t in range(2):
                rstd2(t, t, False)
            with pool.Fori(1, T // 2) as h:
                for j in range(2):
                    pool.wait_ge(s_nb2, 2 * h + j - 1)
                    pool.sem_inc(s_go, 1)
                    pool.wait_ge(s_xn, 2 * h + j - 1)
                    pool.sem_inc(s_go, 1)
                    rstd2(2 * h + j, j, True)
            pool.wait_ge(s_xn, T - 2)
            rstd2(T - 1, 0, True)

            pool.wait_ge(s_lgc, T)
            pool.iota(rev16, [[0, T], [-1, EXPERTS]], base=EXPERTS, channel_multiplier=0, allow_small_or_imprecise_dtypes=True).then_inc(s_bc, 1)
            pool.iota(iota_b, [[1, RB]], base=0, channel_multiplier=0, allow_small_or_imprecise_dtypes=True).then_inc(s_bc, 1)
            pool.iota(pcol, [[0, 2]], base=0, channel_multiplier=1, allow_small_or_imprecise_dtypes=True).then_inc(s_bc, 1)
            pool.iota(iota_sb, [[1, ROUTED_SB]], base=0, channel_multiplier=0, allow_small_or_imprecise_dtypes=True).then_inc(s_bc, 1)
            pool.iota(tok_f, [[P, RB + 2]], base=-RB * P, channel_multiplier=1, allow_small_or_imprecise_dtypes=True).then_inc(s_bc, 1)

            pool.wait_ge(s_tok, 1)
            pool.wait_ge(s_atab, 1)

            def gather(b, j, wait):
                pool.tensor_copy(idx2[:, j, :], tok_i[:, bass.ds(2 * b, 2)]).then_inc(s_ig, 1)
                pool.wait_ge(s_ig, b + 1)
                pool.sem_inc(s_go, 1)
                for q in range(2):
                    if wait:
                        pool.wait_ge(s_t, 2 * b + q - 1)
                        pool.sem_inc(s_go, 1)
                    pool.indirect_dma_start(xg[:, q, :], None, xntab, bass.IndirectOffsetOnAxis(ap=idx2[:, j, q:q + 1], axis=0)).then_inc(s_xg[q], 16)

            def store_y(b, j):
                pool.wait_ge(s_y, 2 * b + 4)
                pool.sem_inc(s_go, 1)
                pool.dma_start(btab[bass.ds(b * SB, SB), :].rearrange("(q p) d -> p q d", q=2), y_s[:, j, :, :]).then_inc(s_bst[j], 16)

            gather(0, 0, False)
            gather(1, 1, True)
            with pool.Fori(1, ROUTED_SB // 2) as h:
                for j in range(2):
                    gather(2 * h + j, j, True)
                    store_y(2 * h + j - 2, j)
            gather(ROUTED_SB, 0, True)
            store_y(ROUTED_SB - 2, 0)
            store_y(ROUTED_SB - 1, 1)
            for j in range(2):
                pool.wait_ge(s_bst[j], 16 * (ROUTED_SB // 2))
            pool.sem_inc(s_go, 1)

            def gather4(t, j, wait):
                if wait:
                    pool.wait_ge(s_acc, t - 1)
                    pool.sem_inc(s_go, 1)
                pool.tensor_copy(idx4[:, j, :], slot_i[:, bass.ds(t, 1), :].rearrange("p a k -> p (a k)")).then_inc(s_i4, 1)
                pool.wait_ge(s_i4, t + 1)
                pool.sem_inc(s_go, 1)
                for k in range(TOP):
                    pool.indirect_dma_start(yk[:, j, k, :], None, btab, bass.IndirectOffsetOnAxis(ap=idx4[:, j, k:k + 1], axis=0)).then_inc(s_yk[j], 16)

            for t in range(2):
                gather4(t, t, False)
            with pool.Fori(1, T // 2) as h:
                for j in range(2):
                    gather4(2 * h + j, j, True)
            gather4(T - 1, 0, True)

        @block.vector
        def _(dve):
            n = [0]

            def link(ins):
                n[0] += 1
                ins.then_inc(s_cdve, 1)
                dve.wait_ge(s_cdve, n[0])

            dve.wait_ge(s_dst, 32)
            link(nc.vector.tensor_copy(dst_f[:, :], dst_i[:, :]))
            link(nc.vector.tensor_scalar(tmp_i[:, :], dst_i[:, :], 7, None, ALU.logical_shift_right))
            link(nc.vector.tensor_copy(dst_h[:, :], tmp_i[:, :]))
            link(nc.vector.tensor_scalar(tmp_i[:, :], dst_i[:, :], P - 1, None, ALU.bitwise_and))
            link(nc.vector.tensor_copy(dst_l[:, :], tmp_i[:, :]))
            dve.wait_ge(s_const, 9)

            def onehots(i, k):
                c = bass.ds(i * 2 * OH + k * OH, OH)
                nc.vector.tensor_tensor(oh_l[:, k, :, :], iota_rep[:, :, :],
                                        dst_l[:, c].unsqueeze(1).to_broadcast([P, P, OH]), ALU.is_equal).then_inc(s_oh, 1)
                nc.vector.tensor_tensor(oh_h[:, k, :, :], iota_rep[:, 0:T, :],
                                        dst_h[:, c].unsqueeze(1).to_broadcast([P, T, OH]), ALU.is_equal).then_inc(s_oh, 1)

            for k in range(2):
                onehots(0, k)
            with dve.Fori(1, NB // 2) as i:
                for k in range(2):
                    dve.wait_ge(s_ohused, 2 * i + k - 1)
                    onehots(i, k)
            link(nc.vector.tensor_scalar(dr_i[:, :, :], dr_i[:, :, :], 7, None, ALU.logical_shift_right))
            link(nc.vector.tensor_reduce(mn[:, :], dr_i[:, :, :], AX.X, ALU.min))
            link(nc.vector.tensor_reduce(mx[:, :], dr_i[:, :, :], AX.X, ALU.max))
            tt = iota_t[0:CPART, :].unsqueeze(2).to_broadcast([CPART, T, CBLK])
            bc = lambda a: a[:, :].unsqueeze(1).to_broadcast([CPART, T, CBLK])
            link(nc.vector.tensor_tensor(cnd[:, 0], tt, bc(mn), ALU.is_ge))
            link(nc.vector.tensor_tensor(cnd[:, 1], bc(mx), tt, ALU.is_ge))
            link(nc.vector.tensor_tensor(cnd[:, 0], cnd[:, 0], cnd[:, 1], ALU.mult))
            link(nc.vector.tensor_scalar(mn[:, :], chunk_id[:, :], -1.0, float(BIG), ALU.mult, ALU.add))
            link(nc.vector.tensor_scalar(mx[:, :], chunk_id[:, :], 1.0, None, ALU.add))
            link(nc.vector.tensor_tensor(cnd[:, 2], cnd[:, 0], bc(mn), ALU.mult))
            link(nc.vector.tensor_tensor(cnd[:, 3], cnd[:, 0], bc(mx), ALU.mult))
            link(nc.vector.tensor_reduce(rng[:, 0, :], cnd[:, 2], AX.X, ALU.max))
            nc.vector.tensor_reduce(rng[:, 1, :], cnd[:, 3], AX.X, ALU.max).then_inc(s_rng, 1)
            dve.wait_ge(s_rt, 1)
            rt = rt_ps[0:T, 0:2 * CPART].rearrange("t (a c) -> t a c", a=2)
            link(nc.vector.tensor_reduce(rcol[:, 0:2], rt, AX.X, ALU.max))
            link(nc.vector.tensor_scalar(rcol[:, 2:3], rcol[:, 0:1], -1.0, float(BIG), ALU.mult, ALU.add))
            link(nc.vector.tensor_scalar(rcol[:, 2:3], rcol[:, 2:3], float(CHUNKS - 1), None, ALU.min))
            link(nc.vector.tensor_scalar(rcol[:, 3:4], rcol[:, 2:3], 1.0, None, ALU.add))
            link(nc.vector.tensor_tensor(rcol[:, 3:4], rcol[:, 3:4], rcol[:, 1:2], ALU.max))
            link(nc.vector.scalar_tensor_tensor(rcol[:, 4:5], rcol[:, 3:4], 1.0, rcol[:, 2:3], ALU.add, ALU.subtract))
            link(nc.vector.tensor_copy(rcol_i[:, 0:1], rcol[:, 4:5]))
            link(nc.vector.tensor_scalar(rcol_i[:, 1:2], rcol_i[:, 0:1], 1, 1, ALU.logical_shift_right, ALU.logical_shift_left))
            link(nc.vector.tensor_copy(rcol[:, 4:5], rcol_i[:, 1:2]))
            nc.vector.tensor_tensor(rcol[:, 3:4], rcol[:, 2:3], rcol[:, 4:5], ALU.add).then_inc(s_rcol, 1)
            dve.wait_ge(s_rrow, 1)
            link(nc.vector.tensor_copy(rrow[:, 0:3, :], rt_ps[0:1, 256:256 + 3 * T].rearrange("o (a t) -> o a t", a=3)))
            link(nc.vector.tensor_copy(tot[:, 0:1], rt_ps[0:1, 256 + 3 * T:257 + 3 * T]))
            link(nc.vector.tensor_tensor(rrow[:, 2, :], rrow[:, 2, :], rrow[:, 0, :], ALU.subtract))
            link(nc.vector.tensor_scalar(rrow[:, 2, :], rrow[:, 2, :], float(CPAD), None, ALU.add))
            link(nc.vector.tensor_scalar(tot[:, 1:2], tot[:, 0:1], float(RING - 1), None, ALU.add))
            link(nc.vector.tensor_copy(toti[:, 1:2], tot[:, 1:2]))
            link(nc.vector.tensor_scalar(toti[:, 0:1], toti[:, 1:2], RING.bit_length() - 1, None, ALU.logical_shift_right))
            link(nc.vector.tensor_copy(tot[:, 2:3], toti[:, 0:1]))
            link(nc.vector.tensor_scalar(tot[:, 3:4], tot[:, 2:3], float(RING), tot[:, 0:1], ALU.mult, ALU.subtract))
            link(nc.vector.tensor_tensor(rrow[:, 1, T - 1:T], rrow[:, 1, T - 1:T], tot[:, 3:4], ALU.add))
            link(nc.vector.tensor_copy(tab[:, :, :], rrow[:, 0:3, :]))
            dve.sem_inc(s_tab, 1)
            dve.wait_ge(s_x, 16 * GRP)
            with dve.Fori(0, T) as t:
                nc.vector.bn_stats(st6[:, bass.ds(t, 1), :], x_all[:, bass.ds(t, 1), :]).then_inc(s_cdve, 1)
            dve.wait_ge(s_cdve, n[0] + T)
            n[0] += T
            link(nc.vector.tensor_tensor(mv[:, :, 0], st6[:, :, 1], st6[:, :, 4], ALU.add))
            link(nc.vector.tensor_scalar(mv[:, :, 0], mv[:, :, 0], 0.5, None, ALU.mult))
            link(nc.vector.tensor_tensor(mv[:, :, 1], st6[:, :, 1], st6[:, :, 4], ALU.subtract))
            link(nc.vector.scalar_tensor_tensor(mv[:, :, 1], mv[:, :, 1], 0.25, mv[:, :, 1], ALU.mult, ALU.mult))
            link(nc.vector.tensor_tensor(veps[:, :], st6[:, :, 2], st6[:, :, 5], ALU.add))
            link(nc.vector.scalar_tensor_tensor(veps[:, :], veps[:, :], 1.0 / D, mv[:, :, 1], ALU.mult, ALU.add))
            nc.vector.tensor_scalar(veps[:, :], veps[:, :], EPS, None, ALU.add).then_inc(s_veps, 1)
            dve.wait_ge(s_deg, 1)
            nc.vector.tensor_copy(deg[:, :], deg_ps[:, 0:T]).then_inc(s_degs, 1)
            dve.wait_ge(s_dinv, 1)
            dve.wait_ge(s_rstd, 1)
            link(nc.vector.tensor_scalar(dinv_ys[:, :], dinv[:, :], 1.0 / YS, None, ALU.mult))
            link(nc.vector.scalar_tensor_tensor(ysc[:, :], rstd[:, :], YS, dinv[:, :], ALU.mult, ALU.mult))
            nc.vector.scalar_tensor_tensor(ybi[:, :], mv[:, :, 0], -1.0, ysc[:, :], ALU.mult, ALU.mult).then_inc(s_ysc, 1)
            with dve.Fori(0, GRP) as g:
                for k in range(GRP):
                    dve.wait_ge(s_yhi, g * GRP + k + 1)
                    nc.vector.tensor_tensor(yrow[:, k, D:2 * D], z[:, k, :], yrow[:, k, 0:D], ALU.subtract).then_inc(s_ylo, 1)

            dve.wait_ge(s_src, 16)
            dve.sem_inc(s_sel, CPAD)

            def tile(t, stats):
                lo = dve.value_load(tab[0:1, 0, bass.ds(t, 1)], min_val=0, max_val=CPAD - 2)
                hi = dve.value_load(tab[0:1, 1, bass.ds(t, 1)], min_val=0, max_val=CPAD - 2)
                off = dve.value_load(tab[0:1, 2, bass.ds(t, 1)], min_val=0, max_val=T * CPAD + CPAD)
                with dve.Fori(lo, hi, 2) as c:
                    s = dve.snap(c + off)
                    slot = even_slot(dve.snap(s % RING))
                    dve.wait_ge(s_consumed, s + 2)
                    nc.vector.tensor_copy(idx[:, bass.ds(slot, 2)], src_i[:, bass.ds(c, 2)])
                    for q in range(2):
                        nc.vector.tensor_scalar(sel[:, bass.ds(slot + q, 1), :], iota16[:, :].unsqueeze(1), tbase[:, bass.ds(t, 1)],
                                                dst_f[:, bass.ds(c + q, 1)], ALU.add, ALU.is_equal).then_inc(s_sel, 1)
                if stats:
                    dve.wait_ge(s_hts, t - 1)
                    for m in range(KD):
                        nc.vector.bn_stats(hst[:, m, bass.ds(t - 2, 1), :], h_t[:, m, bass.ds((t - 2) * P, P)].unsqueeze(1)).then_inc(s_hst, 1)

            def weight_max(e, j):
                dve.wait_ge(s_wraw[j], 16 * (e - j) + 32)
                nc.vector.tensor_reduce(wmx[:, 0, bass.ds(e, 1)], wraw[:, j, 0, :], AX.X, ALU.max, apply_absolute_value=True)
                nc.vector.tensor_reduce(wmx[:, 1, bass.ds(e, 1)], wraw[:, j, 1, :], AX.X, ALU.max, apply_absolute_value=True).then_inc(s_wused, 1)

            def weight_split(e, j, wait):
                dve.wait_ge(s_wraw[j], 16 * (e - j) + 32 + 16 * NE)
                if wait:
                    dve.wait_ge(s_wst[j], 8 * (e - j))
                for w in range(2):
                    hi = wspl[:, j, 2 * w * WL:(2 * w + 1) * WL]
                    lo = wspl[:, j, (2 * w + 1) * WL:(2 * w + 2) * WL]
                    nc.vector.tensor_scalar(hi, wraw[:, j, w, :], scl[:, w:w + 1], None, ALU.mult).then_inc(s_whi, 1)
                    dve.wait_ge(s_whi, 2 * e + w + 1)
                    last = nc.vector.scalar_tensor_tensor(lo, wraw[:, j, w, :], scl[:, w:w + 1], hi, ALU.mult, ALU.subtract)
                last.then_inc(s_wlo, 1)

            MAX_TO = MAX_FROM + NE
            tile(0, False)
            tile(1, False)
            with dve.Fori(0, NE // 2) as i:
                for j in range(2):
                    tile(2 * i + j + MAX_FROM, True)
                    weight_max(2 * i + j, j)
            dve.wait_ge(s_wused, NE)
            dve.wait_ge(s_b1, 16)
            link(nc.vector.tensor_reduce(wm3[:, 0:2], wmx[:, :, :], AX.X, ALU.max))
            link(nc.vector.tensor_reduce(wm3[:, 2:3], b1c[:, :], AX.X, ALU.max, apply_absolute_value=True))
            nc.vector.tensor_copy(wmb[:, :, :], wm3[:, 0:3].unsqueeze(2).to_broadcast([P, 3, P])).then_inc(s_wm, 1)
            with dve.Fori(MAX_TO, SPLIT_FROM) as t:
                tile(t, True)
            dve.wait_ge(s_wmt, 1)
            link(nc.vector.tensor_reduce(wm3[:, 0:3], wm_ps, AX.X, ALU.max))
            link(nc.vector.scalar_tensor_tensor(wm3[:, 2:3], wm3[:, 0:1], float(D), wm3[:, 2:3], ALU.mult, ALU.add))
            link(nc.vector.tensor_scalar(wex_i[:, 0:3], wm3[:, 0:3].bitcast(I32), 23, None, ALU.logical_shift_right))
            link(nc.vector.tensor_copy(wex_f[:, 0:3], wex_i[:, 0:3]))
            link(nc.vector.tensor_scalar(wex_f[:, 0:3], wex_f[:, 0:3], 97.0, None, ALU.max))
            link(nc.vector.tensor_scalar(wex_f[:, 0:3], wex_f[:, 0:3], -1.0, 268.0, ALU.mult, ALU.add))
            link(nc.vector.tensor_scalar(wex_f[:, 3:4], wex_f[:, 0:1], -1.0, 244.0, ALU.mult, ALU.add))
            link(nc.vector.tensor_tensor(wex_f[:, 4:5], wex_f[:, 1:2], wex_f[:, 2:3], ALU.add))
            link(nc.vector.tensor_scalar(wex_f[:, 4:5], wex_f[:, 4:5], -1.0, 381.0, ALU.mult, ALU.add))
            link(nc.vector.tensor_copy(wex_i[:, 0:5], wex_f[:, 0:5]))
            link(nc.vector.tensor_scalar(wex_s[:, 0:5], wex_i[:, 0:5], 23, None, ALU.logical_shift_left))
            for j in range(2):
                tile(j + SPLIT_FROM, True)
                weight_split(j, j, False)
            with dve.Fori(1, NE // 2) as i:
                for j in range(2):
                    tile(2 * i + j + SPLIT_FROM, True)
                    weight_split(2 * i + j, j, True)
            for t in range(SPLIT_FROM + NE, T):
                tile(t, True)
            dve.wait_ge(s_hts, T)
            for m in range(KD):
                nc.vector.bn_stats(hst[:, m, T - 2, :], h_t[:, m, (T - 2) * P:(T - 1) * P]).then_inc(s_hst, 1)
            for m in range(KD):
                nc.vector.bn_stats(hst[:, m, T - 1, :], h_t[:, m, (T - 1) * P:(T - 1) * P + LAST]).then_inc(s_hst, 1)
            dve.wait_ge(s_hst, KD * T)
            for m in range(KD):
                link(nc.vector.bn_aggr(hmv[:, m, :], hst[:, m, :, :].rearrange("p t s -> p (t s)")))
            nc.vector.tensor_scalar(bn_v[:, :], hmv[:, :, 1], EPS, None, ALU.add).then_inc(s_bnv, 1)
            dve.wait_ge(s_bnr, 1)
            link(nc.vector.tensor_tensor(bn_a[:, :], bn_a[:, :], bcol[:, 1, :], ALU.mult))
            link(nc.vector.tensor_tensor(bn_b[:, :], hmv[:, :, 0], bn_a[:, :], ALU.mult))
            link(nc.vector.tensor_tensor(bn_b[:, :], bcol[:, 2, :], bn_b[:, :], ALU.subtract))
            link(nc.vector.tensor_scalar(c1[:, :], rstd[:, :], 1.0, None, ALU.add))
            link(nc.vector.scalar_tensor_tensor(c2[:, :], mv[:, :, 0], -1.0, rstd[:, :], ALU.mult, ALU.mult))
            dve.sem_inc(s_bn, 1)
            dve.sem_inc(s_hmv, 1)

            def residual(t, j, steady):
                dve.wait_ge(s_xr[j], 8 * (t - j) + 16)
                if steady:
                    dve.wait_ge(s_xn, t - 1)
                    dve.wait_ge(s_x1b, t - 1)
                nc.vector.tensor_scalar(x1[:, j, :], xr[:, j, :], c1[:, bass.ds(t, 1)], c2[:, bass.ds(t, 1)], ALU.mult, ALU.add).then_inc(s_u, 1)
                dve.wait_ge(s_u, t + 1)
                dve.wait_ge(s_t1, t + 1)
                nc.vector.tensor_tensor(x1[:, j, :], bank[j][:, :], x1[:, j, :], ALU.add).then_inc(s_x1, 1)
                dve.wait_ge(s_x1, t + 1)
                nc.vector.bn_stats(st2[:, j, :], x1[:, j, :]).then_inc(s_st2, 1)
                dve.wait_ge(s_st2, t + 1)
                dve.sem_inc(s_go, 1)
                nc.vector.bn_aggr(mv2[:, j, :], st2[:, j, :]).then_inc(s_mv2, 1)
                dve.wait_ge(s_mv2, t + 1)
                nc.vector.tensor_scalar(ve2[:, j:j + 1], mv2[:, j, 1:2], EPS, None, ALU.add).then_inc(s_ve2, 1)

            def shift(t, j):
                dve.wait_ge(s_r2, t + 1)
                nc.vector.scalar_tensor_tensor(nb2[:, j:j + 1], mv2[:, j, 0:1], -1.0, r2[:, j:j + 1], ALU.mult, ALU.mult).then_inc(s_nb2, 1)

            def low_row(t, j):
                dve.wait_ge(s_xnh, t + 1)
                nc.vector.scalar_tensor_tensor(xn_row[:, j, D:2 * D], xn[:, j, :], YS, xn_row[:, j, 0:D], ALU.mult, ALU.subtract).then_inc(s_xnl, 1)

            def keep_logits(t, j):
                dve.wait_ge(s_lg, t + 1)
                nc.vector.tensor_copy(logits[:, bass.ds(t, 1), :], bank[4 + j][:, 0:EXPERTS].unsqueeze(1)).then_inc(s_lgc, 1)

            residual(0, 0, False)
            shift(0, 0)
            residual(1, 1, False)
            low_row(0, 0)
            shift(1, 1)
            residual(2, 0, True)
            low_row(1, 1)
            shift(2, 0)
            residual(3, 1, True)
            keep_logits(0, 0)
            low_row(2, 0)
            shift(3, 1)
            with dve.Fori(2, T // 2) as h:
                for j in range(2):
                    residual(2 * h + j, j, True)
                    keep_logits(2 * h + j - 3, 1 - j)
                    low_row(2 * h + j - 1, 1 - j)
                    shift(2 * h + j, j)
            residual(T - 1, 0, True)
            low_row(T - 2, 1)
            shift(T - 1, 0)
            low_row(T - 1, 0)
            for t in range(T - 4, T):
                keep_logits(t, t % 2)

            V = nc.vector
            full = [P, T, EXPERTS]
            over = lambda a: a.unsqueeze(2).to_broadcast(full)
            dve.wait_ge(s_lgc, T)
            dve.wait_ge(s_bc, 5)
            link(V.tensor_reduce(vec_a[:, 0, :], logits, AX.X, ALU.max))
            V.tensor_tensor(probs, logits, over(vec_a[:, 0, :]), ALU.subtract).then_inc(s_sub, 1)
            dve.wait_ge(s_exp, 1)
            link(V.tensor_reduce(vec_a[:, 0, :], probs, AX.X, ALU.add))
            link(V.reciprocal(vec_a[:, 0, :], vec_a[:, 0, :]))
            link(V.tensor_tensor(probs, probs, over(vec_a[:, 0, :]), ALU.mult))
            for k in range(TOP):
                link(V.tensor_reduce(top_v[:, k, :], probs, AX.X, ALU.max))
                link(V.tensor_tensor(tmp_a, probs, over(top_v[:, k, :]), ALU.is_equal))
                link(V.tensor_tensor(tmp_a, tmp_a, rev16, ALU.mult))
                link(V.tensor_reduce(vec_b[:, 0, :], tmp_a, AX.X, ALU.max))
                link(V.tensor_tensor(hot[:, k], rev16, over(vec_b[:, 0, :]), ALU.is_equal))
                link(V.scalar_tensor_tensor(probs, hot[:, k], -2.0, probs, ALU.mult, ALU.add))
            link(V.tensor_tensor(tmp_a, hot[:, 0], hot[:, 1], ALU.add))
            link(V.tensor_tensor(tmp_b, hot[:, 2], hot[:, 3], ALU.add))
            V.tensor_tensor(mask16, tmp_a, tmp_b, ALU.add).then_inc(s_mask, 1)
            V.tensor_tensor(vec_a, top_v, top_v[:, 0:1, :].to_broadcast([P, TOP, T]), ALU.subtract).then_inc(s_topv, 1)
            dve.wait_ge(s_rank, 1)
            HG = T * EXPERTS // 2
            flat = lambda a: a.rearrange("p t e -> p (t e)")
            for h in range(2):
                link(V.tensor_copy(flat(rank_s)[:, h * HG:(h + 1) * HG], bank[h][:, 0:HG]))
                link(V.tensor_copy(flat(cum_a)[:, h * HG:(h + 1) * HG], bank[2 + h][:, 0:HG]))
            src_c, dst_c, step = cum_a, cum_b, 1
            while step < T:
                link(V.tensor_copy(dst_c[:, 0:step, :], src_c[:, 0:step, :]))
                link(V.tensor_tensor(dst_c[:, step:T, :], src_c[:, step:T, :], src_c[:, 0:T - step, :], ALU.add))
                src_c, dst_c, step = dst_c, src_c, 2 * step
            link(V.tensor_tensor(flat(rank_s)[:, EXPERTS:], flat(rank_s)[:, EXPERTS:], flat(src_c)[:, 0:(T - 1) * EXPERTS], ALU.add))
            link(V.tensor_scalar(tot_e, src_c[:, T - 1, :], float(SB - 1), None, ALU.add))
            link(V.tensor_copy(blk_e, tot_e))
            link(V.tensor_scalar(blk_e, blk_e, 8, None, ALU.logical_shift_right))
            link(V.tensor_copy(tot_e, blk_e))
            link(V.tensor_scalar(pre_e, tot_e, 1.0, None, ALU.max))
            link(V.tensor_copy(tot_e, pre_e))
            a_e, b_e, step = pre_e, pre_e2, 1
            while step < EXPERTS:
                link(V.tensor_copy(b_e[:, 0:step], a_e[:, 0:step]))
                link(V.tensor_tensor(b_e[:, step:], a_e[:, step:], a_e[:, 0:EXPERTS - step], ALU.add))
                a_e, b_e, step = b_e, a_e, 2 * step
            link(V.tensor_tensor(b_e, a_e, tot_e, ALU.subtract))
            link(V.tensor_copy(start_f[:, 0:EXPERTS], b_e[0:1, :]))
            link(V.memset(start_f[:, EXPERTS:EXPERTS + 1], float(ROUTED_SB)))
            link(V.tensor_copy(start_i[:, :], start_f[:, :]))
            link(V.tensor_tensor(ebt[0:1], iota_sb[0:1, :].unsqueeze(2).to_broadcast([1, ROUTED_SB, EXPERTS]),
                                 start_f[:, 0:EXPERTS].unsqueeze(1).to_broadcast([1, ROUTED_SB, EXPERTS]), ALU.is_ge))
            link(V.tensor_reduce(iota_sb[0:1, :], ebt[0:1], AX.X, ALU.add))
            link(V.tensor_scalar(eb_i[:, :], iota_sb[0:1, :], 1.0, None, ALU.subtract))
            link(V.scalar_tensor_tensor(rank_s, b_e.unsqueeze(1).to_broadcast(full), float(SB), rank_s, ALU.mult, ALU.add))
            for k in range(TOP):
                link(V.tensor_tensor(tmp_a, hot[:, k], rank_s, ALU.mult))
                link(V.tensor_reduce(r_f[:, :, k], tmp_a, AX.X, ALU.add))
            link(V.tensor_copy(slot_i, r_f))
            ti = tmp_b.rearrange("p t e -> p (t e)")[:, 0:T * TOP].bitcast(I32).rearrange("p (t k) -> p t k", k=TOP)
            link(V.tensor_scalar(ti, slot_i, 7, None, ALU.logical_shift_right))
            link(V.tensor_copy(b_f, ti))
            link(V.tensor_scalar(ti, slot_i, P - 1, None, ALU.bitwise_and))
            link(V.tensor_copy(r_f, ti))
            dve.wait_ge(s_exp2, 1)
            link(V.tensor_tensor(vec_b[:, 0, :], vec_a[:, 0, :], vec_a[:, 1, :], ALU.add))
            link(V.tensor_tensor(vec_b[:, 1, :], vec_a[:, 2, :], vec_a[:, 3, :], ALU.add))
            link(V.tensor_tensor(vec_b[:, 0, :], vec_b[:, 0, :], vec_b[:, 1, :], ALU.add))
            link(V.reciprocal(vec_b[:, 0, :], vec_b[:, 0, :]))
            link(V.tensor_tensor(wk, vec_a.rearrange("p k t -> p t k"), vec_b[:, 0, :].unsqueeze(2).to_broadcast([P, T, TOP]), ALU.mult))

            def places(t, wait):
                for k in range(TOP):
                    j = k % 2
                    if wait or k >= 2:
                        dve.wait_ge(s_inv, t * TOP + k - 1)
                    nc.vector.tensor_scalar(oh_r[:, j, :], iota16[:, :], r_f[:, bass.ds(t, 1), k:k + 1].rearrange("p a k -> p (a k)"), None, ALU.is_equal)
                    bcol_tk = b_f[:, bass.ds(t, 1), k:k + 1].rearrange("p a k -> p (a k)")
                    nc.vector.tensor_scalar(oh_b[:, j, 0, :], iota_b, bcol_tk, pcol[:, 0:1], ALU.is_equal, ALU.mult)
                    nc.vector.tensor_scalar(oh_b[:, j, 1, :], iota_b, bcol_tk, iota_t[:, bass.ds(t, 1)], ALU.is_equal, ALU.mult).then_inc(s_ohr, 1)

            places(0, False)
            with dve.Fori(1, T) as t:
                places(t, True)
            dve.wait_ge(s_inv, T * TOP + 1)
            link(V.tensor_scalar(tok_f, tok_f, 0.0, float(NP - 1), ALU.max, ALU.min))
            link(V.tensor_copy(tok_f[:, 0:RB], bank[4][:, 0:RB]))
            link(V.scalar_tensor_tensor(tok_f[:, 0:RB], bank[4][:, RB:2 * RB], float(P), tok_f[:, 0:RB], ALU.mult, ALU.add))
            link(V.tensor_copy(tok_i, tok_f))
            dve.sem_inc(s_tok, 1)

            def low_x(b):
                for q in range(2):
                    dve.wait_ge(s_t, 2 * b + q + 1)
                    if q == 0:
                        dve.wait_ge(s_l1, KH * b + 1)
                    nc.vector.tensor_copy(x_hl[:, q, 1], turned[q][1]).then_inc(s_xlo, 1)

            def hidden(b, wait):
                for m in range(KH):
                    dve.wait_ge(s_g, 2 * b + m + 3)
                    if m == 0 and wait:
                        dve.wait_ge(s_l2, b)
                    nc.vector.tensor_scalar(hh[:, m, :], g_s[:, m, :], scale_h, None, ALU.mult).then_inc(s_hhi, 1)
                    dve.wait_ge(s_hhi, 2 * b + m + 1)
                    nc.vector.scalar_tensor_tensor(hl[:, m, :], g_s[:, m, :], scale_h, hh[:, m, :], ALU.mult, ALU.subtract).then_inc(s_hlo, 1)

            def results(b, j, wait):
                e = dve.value_load(eb_i[0:1, bass.ds(b, 1)], min_val=0, max_val=EXPERTS - 1)
                dve.wait_ge(s_l2, b + 1)
                if wait:
                    dve.wait_ge(s_bst[j], 8 * (b - j))
                for q in range(2):
                    nc.vector.scalar_tensor_tensor(y_s[:, j, q, :].unsqueeze(1), bank[4 + q][:, :].unsqueeze(1), unscale_2, b2r[:, bass.ds(e, 1), :], ALU.mult, ALU.add).then_inc(s_y, 1)

            dve.wait_ge(s_b2, 16)
            dve.sem_inc(s_l1, 1)
            link(V.tensor_scalar(half_unscale, unscale_2, 1.0 / SHARED, None, ALU.mult))
            low_x(0)
            for b in range(2):
                hidden(b, b > 0)
                low_x(b + 1)
                results(b, b, False)
            with dve.Fori(1, ROUTED_SB // 2) as h:
                for j in range(2):
                    hidden(2 * h + j, True)
                    low_x(2 * h + j + 1)
                    results(2 * h + j, j, True)

            def low_s(s, nq):
                for q in range(nq):
                    dve.wait_ge(s_st, 2 * s + q + 1)
                    nc.vector.tensor_copy(x_hl[:, q, 1], turned[q][1]).then_inc(s_sxl, 1)

            def hidden_s(s, units, nq):
                for u in units:
                    dve.wait_ge(s_sg, UNITS * s + u + 3)
                    nc.vector.tensor_scalar(hhs[:, u, 0:nq * P], gs_s[:, u, 0:nq * P], scale_h, None, ALU.mult).then_inc(s_shh, 1)
                    dve.wait_ge(s_shh, UNITS * s + u + 1)
                    nc.vector.scalar_tensor_tensor(hls[:, u, 0:nq * P], gs_s[:, u, 0:nq * P], scale_h, hhs[:, u, 0:nq * P], ALU.mult, ALU.subtract).then_inc(s_shl, 1)

            def base(s, nq, wait):
                dve.wait_ge(s_sl2, s + 1)
                for q in range(nq):
                    dve.wait_ge(s_fl[q], 16 * s + 16)
                    if wait:
                        dve.wait_ge(s_ost[q], 16 * s)
                    V.scalar_tensor_tensor(acc[:, q, :], bank[4 + q][:, :], half_unscale, x1r[:, q, :], ALU.mult, ALU.add).then_inc(s_base, 1)

            def choices(s, q):
                t = 2 * s + q
                dve.wait_ge(s_yk[q], 64 * s + 64)
                dve.wait_ge(s_base, t + 3)
                for k in range(TOP):
                    if k:
                        dve.wait_ge(s_fd, (TOP - 1) * t + k)
                    V.scalar_tensor_tensor(acc[:, q, :], yk[:, q, k, :], wk[:, bass.ds(t, 1), k:k + 1].rearrange("p a k -> p (a k)"), acc[:, q, :],
                                           ALU.mult, ALU.add).then_inc(s_fd if k < TOP - 1 else s_acc, 1)

            def step_s(s, nq, next_nq, wait):
                base(s - 1, 2, wait)
                choices(s - 1, 0)
                hidden_s(s, range(0, KH), nq)
                choices(s - 1, 1)
                hidden_s(s, range(KH, UNITS), nq)
                low_s(s + 1, next_nq)

            low_s(0, 2)
            hidden_s(0, range(UNITS), 2)
            low_s(1, 2)
            step_s(1, 2, 2, False)
            with dve.Fori(2, SHARED_SB - 2) as s:
                step_s(s, 2, 2, True)
            step_s(SHARED_SB - 2, 2, 1, True)
            step_s(SHARED_SB - 1, 1, 0, True)
            base(SHARED_SB - 1, 1, True)
            choices(SHARED_SB - 1, 0)

        @block.scalar
        def _(act):
            act.wait_ge(s_ysc, 1)

            def rows_hi(g, k):
                t = g * GRP + k
                nc.scalar.activation(z[:, k, :], x_all[:, bass.ds(t, 1), :].rearrange("p a d -> p (a d)"), ACT.Identity, bias=ybi[:, bass.ds(t, 1)],
                                     scale=ysc[:, bass.ds(t, 1)]).then_inc(s_z, 1)
                act.wait_ge(s_z, t + 1)
                nc.scalar.activation(yrow[:, k, 0:D], z[:, k, :], ACT.Copy).then_inc(s_yhi, 1)

            for k in range(GRP):
                rows_hi(0, k)
            with act.Fori(1, GRP) as g:
                for k in range(GRP):
                    act.wait_ge(s_yst[k], g * 16)
                    act.wait_ge(s_ylo, g * GRP + k + 1 - GRP)
                    rows_hi(g, k)
            act.wait_ge(s_w, 64)

            yv = ytab.rearrange("(t p) d -> p t d", p=P)
            act.wait_ge(s_ytab, 1)
            act.dma_start(yself[:, :], yv[:, 0:1, :]).then_inc(s_yself, 16)

            def finish_tile(t, par, more=True):
                act.wait_ge(s_agg, t + 2)
                act.dma_start(yself[:, :], yv[:, bass.ds(t + 1, 1), :]).then_inc(s_yself, 16) if more else None
                act.wait_ge(s_at, t + 1)
                nc.scalar.activation(agg_s[:, :], agg_b[par][:, :], ACT.Copy, scale=dinv_ys[:, bass.ds(t, 1)]).then_inc(s_aggs, 1)
                act.wait_ge(s_at, t + 2)
                nc.scalar.activation(agg_ts[:, :, :], at_ps[:, :, :], ACT.Copy).then_inc(s_ats, 1)
                act.wait_ge(s_ht, t + 1)
                for m in range(KD):
                    ins = nc.scalar.activation(h_t[:, m, bass.ds(t * P, P)], ht_ps[:, m, :], ACT.Identity, bias=bcol[:, 0, m:m + 1])
                ins.then_inc(s_hts, 1)

            finish_tile(0, 0)
            with act.Fori(0, T // 2 - 1) as h:
                finish_tile(2 * h + 1, 1)
                finish_tile(2 * h + 2, 0)
            finish_tile(T - 2, 1)
            finish_tile(T - 1, 0, more=False)

            act.wait_ge(s_bn, 1)
            def gelu_tile(t, j, steady):
                if steady:
                    act.wait_ge(s_t1, t - 1)
                for m in range(KD):
                    last = nc.scalar.activation(g_tile[:, j, m, :], h_t[:, m, bass.ds(t * P, P)], ACT.Gelu, bias=bn_b[:, m:m + 1], scale=bn_a[:, m:m + 1])
                last.then_inc(s_gelu, 1)

            def norm_row(t, j, steady):
                act.wait_ge(s_nb2, t + 1)
                if steady:
                    act.wait_ge(s_t2, t - 1)
                    act.wait_ge(s_xnl, t - 1)
                nc.scalar.activation(xn[:, j, :], x1[:, j, :], ACT.Identity, bias=nb2[:, j:j + 1], scale=r2[:, j:j + 1]).then_inc(s_xn, 1)
                if steady:
                    act.wait_ge(s_xnst[j], 8 * (t - j))
                act.wait_ge(s_xn, t + 1)
                nc.scalar.activation(xn_row[:, j, 0:D], xn[:, j, :], ACT.Copy, scale=YS).then_inc(s_xnh, 1)

            def keep_turned(t, j, steady):
                act.wait_ge(s_t2, t + 1)
                if steady:
                    act.wait_ge(s_lg, t - 1)
                nc.scalar.activation(x_ts[:, j], cut(2 + j, KD), ACT.Copy).then_inc(s_xT, 1)

            gelu_tile(0, 0, False)
            gelu_tile(1, 1, False)
            norm_row(0, 0, False)
            gelu_tile(2, 0, True)
            norm_row(1, 1, False)
            keep_turned(0, 0, False)
            gelu_tile(3, 1, True)
            norm_row(2, 0, True)
            keep_turned(1, 1, False)
            with act.Fori(2, T // 2) as h:
                for j in range(2):
                    gelu_tile(2 * h + j, j, True)
                    norm_row(2 * h + j - 1, 1 - j, True)
                    keep_turned(2 * h + j - 2, j, True)
            gelu_tile(T - 1, 0, True)
            norm_row(T - 2, 1, True)
            keep_turned(T - 3, 0, True)
            norm_row(T - 1, 0, True)
            keep_turned(T - 2, 1, True)
            keep_turned(T - 1, 0, True)

            act.wait_ge(s_sub, 1)
            nc.scalar.activation(probs, probs, ACT.Exp).then_inc(s_exp, 1)
            act.wait_ge(s_topv, 1)
            nc.scalar.activation(vec_a, vec_a, ACT.Exp).then_inc(s_exp2, 1)

            def high_x(b):
                for q in range(2):
                    act.wait_ge(s_t, 2 * b + q + 1)
                    if q == 0:
                        act.wait_ge(s_l1, KH * b + 1)
                    nc.scalar.activation(x_hl[:, q, 0], turned[q][0], ACT.Copy).then_inc(s_xhi, 1)

            def gelu(b, wait):
                e = act.value_load(eb_i[0:1, bass.ds(b, 1)], min_val=0, max_val=EXPERTS - 1)
                for m in range(KH):
                    act.wait_ge(s_l1, 2 * b + m + 2)
                    if wait:
                        act.wait_ge(s_hlo, 2 * b + m - 1)
                    nc.scalar.activation(g_s[:, m, :], bank[2 + m][:, 0:SB], ACT.Gelu, bias=b1c[:, bass.ds(e * KH + m, 1)], scale=unscale_1).then_inc(s_g, 1)

            act.sem_inc(s_g, 2)
            act.wait_ge(s_tok, 1)
            high_x(0)
            gelu(0, False)
            high_x(1)
            with act.Fori(1, ROUTED_SB) as b:
                gelu(b, True)
                high_x(b + 1)

            def high_s(s, nq):
                for q in range(nq):
                    act.wait_ge(s_st, 2 * s + q + 1)
                    nc.scalar.activation(x_hl[:, q, 0], turned[q][0], ACT.Copy).then_inc(s_sxh, 1)

            def gelu_s(s, nq):
                for u in range(UNITS):
                    act.wait_ge(s_sl1, UNITS * s + u + 1)
                    nc.scalar.activation(gs_s[:, u, 0:nq * P], bank[2 + u % 2][:, 0:nq * P], ACT.Gelu,
                                         bias=b1c[:, EXPERTS * KH + u:EXPERTS * KH + u + 1], scale=unscale_1).then_inc(s_sg, 1)

            act.sem_inc(s_sg, 2)
            high_s(0, 2)
            with act.Fori(0, SHARED_SB - 2) as s:
                gelu_s(s, 2)
                high_s(s + 1, 2)
            gelu_s(SHARED_SB - 2, 2)
            high_s(SHARED_SB - 1, 1)
            gelu_s(SHARED_SB - 1, 1)

        @block.tensor
        def _(pe):
            pe.wait_ge(s_const, 13)
            nc.tensor.matmul(deg_ps[:, 0:T], ones[0:1, 0:P], ones[0:1, 0:T], start=True, stop=False)
            with pe.Fori(0, NB // 2) as i:
                for k in range(2):
                    pe.wait_ge(s_oh, 4 * i + 2 * k + 2)
                    for c in range(OH):
                        mm = nc.tensor.matmul(deg_ps[:, 0:T], oh_l[:, k, :, c], oh_h[:, k, :, c], start=False, stop=False)
                    mm.then_inc(s_ohused, 1)
            nc.tensor.matmul(deg_ps[:, 0:T], zero16[:, 0:P], zero16[:, 0:T], start=False, stop=True).then_inc(s_deg, 1)
            pe.wait_ge(s_rng, 1)
            for a in range(2):
                mm = nc.tensor.transpose(rt_ps[0:T, a * CPART:(a + 1) * CPART], rng[:, a, :], ident[0:CPART, 0:CPART])
            mm.then_inc(s_rt, 1)
            pe.wait_ge(s_rcol, 1)
            nc.tensor.matmul(rt_ps[0:1, 256:256 + T], rcol[:, 2:3], ident[0:T, 0:T], start=True, stop=True)
            nc.tensor.matmul(rt_ps[0:1, 256 + T:256 + 2 * T], rcol[:, 3:4], ident[0:T, 0:T], start=True, stop=True)
            nc.tensor.matmul(rt_ps[0:1, 256 + 2 * T:256 + 3 * T], rcol[:, 4:5], upper[:, :], start=True, stop=True)
            nc.tensor.matmul(rt_ps[0:1, 256 + 3 * T:257 + 3 * T], rcol[:, 4:5], ones[0:T, 0:1], start=True, stop=True).then_inc(s_rrow, 1)

            pe.wait_ge(s_tab, 1)
            pe.wait_ge(s_ytab, 1)
            pe.wait_ge(s_w, 64)
            pe.sem_inc(s_agg, 1)
            pe.sem_inc(s_consumed, RING + CPAD)

            def gather_sum(t, par):
                lo = pe.value_load(tab[0:1, 0, bass.ds(t, 1)], min_val=0, max_val=CPAD - 2)
                hi = pe.value_load(tab[0:1, 1, bass.ds(t, 1)], min_val=0, max_val=CPAD - 2)
                off = pe.value_load(tab[0:1, 2, bass.ds(t, 1)], min_val=0, max_val=T * CPAD + CPAD)
                pe.wait_ge(s_aggs, t + 1)
                nc.tensor.matmul(agg_b[par][:, :], zero16[:, 0:P], zero16[:, 0:D], start=True, stop=False)
                with pe.Fori(lo, hi, 2) as c:
                    s = pe.snap(c + off)
                    pe.wait_ge(s_landed, s + 2)
                    slot = even_slot(pe.snap(s % RING))
                    for q in range(2):
                        w = sel_flat[:, bass.ds(slot * P + q * P, P)]
                        for part in range(2):
                            mm = nc.tensor.matmul(agg_b[par][:, :], w, rows_flat[:, bass.ds(slot * (2 * D) + (2 * q + part) * D, D)], start=False, stop=False)
                        mm.then_inc(s_consumed, 1)
                pe.wait_ge(s_yself, 16 * t + 16)
                nc.tensor.matmul(agg_b[par][:, :], ident16[:, :], yself[:, 0:D], start=False, stop=False)
                nc.tensor.matmul(agg_b[par][:, :], ident16[:, :], yself[:, D:2 * D], start=False, stop=True).then_inc(s_agg, 1)

            def turn(t):
                pe.wait_ge(s_aggs, t + 3)
                for k in range(KD):
                    mm = nc.tensor.transpose(at_ps[:, k, :], agg_s[:, k * P:(k + 1) * P], ident[:, :])
                mm.then_inc(s_at, 1)

            def project(t):
                pe.wait_ge(s_ats, t + 1)
                for m in range(KD):
                    for k in range(KD):
                        mm = nc.tensor.matmul(ht_ps[:, m, :], w_sb[:, k, m * P:(m + 1) * P], agg_ts[:, k, :], start=(k == 0), stop=(k == KD - 1))
                mm.then_inc(s_ht, 1)

            pe.sem_inc(s_aggs, 2)
            pe.sem_inc(s_at, 1)
            gather_sum(0, 0)
            def pair(h):
                for j in range(2):
                    gather_sum(2 * h + j + 1, (j + 1) % 2)
                    turn(2 * h + j)
                    project(2 * h + j)

            with pe.Fori(0, (MAX_FROM + NE) // 2) as h:
                pair(h)
            pe.wait_ge(s_wm, 1)
            for q in range(3):
                mm = nc.tensor.transpose(wm_ps[:, q, :], wmb[:, q, :], ident[:, :])
            mm.then_inc(s_wmt, 1)
            with pe.Fori((MAX_FROM + NE) // 2, T // 2) as h:
                pair(h)
            turn(T - 1)
            project(T - 1)

            pe.wait_ge(s_gate, 16)

            def turn_gelu(t, j, steady):
                pe.wait_ge(s_gelu, t + 1)
                if steady:
                    pe.wait_ge(s_x1, t - 1)
                for m in range(KD):
                    mm = nc.tensor.transpose(bank[j][:, m * P:(m + 1) * P], g_tile[:, j, m, :], ident[:, :])
                mm.then_inc(s_t1, 1)

            def turn_norm(t, j, steady):
                pe.wait_ge(s_xn, t + 1)
                if steady:
                    pe.wait_ge(s_xT, t - 1)
                for m in range(KD):
                    mm = nc.tensor.transpose(bank[2 + j][:, m * P:(m + 1) * P], xn[:, j, m * P:(m + 1) * P], ident[:, :])
                mm.then_inc(s_t2, 1)

            def gate_logits(t, j, steady):
                pe.wait_ge(s_xT, t + 1)
                if steady:
                    pe.wait_ge(s_lgc, t - 1)
                for m in range(KD):
                    mm = nc.tensor.matmul(bank[4 + j][:, 0:EXPERTS], x_ts[:, j, m, :], gate[:, m, :], start=(m == 0), stop=(m == KD - 1))
                mm.then_inc(s_lg, 1)

            turn_gelu(0, 0, False)
            turn_gelu(1, 1, False)
            turn_norm(0, 0, False)
            turn_gelu(2, 0, True)
            turn_norm(1, 1, False)
            gate_logits(0, 0, False)
            turn_gelu(3, 1, True)
            turn_norm(2, 0, True)
            gate_logits(1, 1, False)
            with pe.Fori(2, T // 2) as h:
                for j in range(2):
                    turn_gelu(2 * h + j, j, True)
                    turn_norm(2 * h + j - 1, 1 - j, True)
                    gate_logits(2 * h + j - 2, j, True)
            turn_gelu(T - 1, 0, True)
            turn_norm(T - 2, 1, True)
            gate_logits(T - 3, 0, True)
            turn_norm(T - 1, 0, True)
            gate_logits(T - 2, 1, True)
            gate_logits(T - 1, 0, True)

            pe.wait_ge(s_mask, 1)
            mflat = mask16.rearrange("p t e -> p (t e)")
            HG = T * EXPERTS // 2
            for h in range(2):
                nc.tensor.matmul(bank[h][:, 0:HG], upper16[:, :], mflat[:, h * HG:(h + 1) * HG], start=True, stop=True)
                mm = nc.tensor.matmul(bank[2 + h][:, 0:HG], ones16[:, :], mflat[:, h * HG:(h + 1) * HG], start=True, stop=True)
            mm.then_inc(s_rank, 1)
            nc.tensor.matmul(bank[4][:, 0:2 * RB], zero16[:, 0:P], zero16[:, 0:2 * RB], start=True, stop=False)
            with pe.Fori(0, T) as t:
                for k in range(TOP):
                    pe.wait_ge(s_ohr, t * TOP + k + 1)
                    nc.tensor.matmul(bank[4][:, 0:2 * RB], oh_r[:, k % 2, :], oh_b[:, k % 2].rearrange("p a b -> p (a b)"), start=False, stop=False).then_inc(s_inv, 1)
            nc.tensor.matmul(bank[4][:, 0:2 * RB], zero16[:, 0:P], zero16[:, 0:2 * RB], start=False, stop=True).then_inc(s_inv, 1)

            def turn(dst, src):
                for u in range(2):
                    for m in range(KD):
                        mm = nc.tensor.transpose(dst[u][:, m, :], src[:, u * D + m * P:u * D + (m + 1) * P], ident16[:, :])
                return mm

            def turn_rows(b, q):
                pe.wait_ge(s_xg[q], 16 * b + 16)
                turn(turned[q], xg[:, q, :]).then_inc(s_t, 1)

            def halves(w):
                return (wsb[:, w, 0:2 * WL].rearrange("p (s k n) -> p s k n", s=2, k=KD),
                        wsb[:, w, 2 * WL:4 * WL].rearrange("p (s k n) -> p s k n", s=2, k=KH))

            def first_layer(o, w1_parts, m, nq):
                for k in range(KD):
                    for u, v in ((0, 0), (0, 1), (1, 0)):
                        mm = nc.tensor.matmul(o, w1_parts[:, u, k, m * P:(m + 1) * P], x_hl[:, 0:nq, v, k, :], start=(k == 0 and u == 0 and v == 0),
                                              stop=(k == KD - 1 and u == 1))
                return mm

            def superblock(b, w):
                W1, W2 = halves(w)
                pe.wait_ge(s_xhi, 2 * b + 2)
                pe.wait_ge(s_xlo, 2 * b + 2)
                for m in range(KH):
                    pe.wait_ge(s_g, 2 * b + m + 1)
                    first_layer(bank[2 + m][:, 0:SB].rearrange("p (q n) -> p q n", q=2), W1, m, 2).then_inc(s_l1, 1)
                turn_rows(b + 1, 0)
                pe.wait_ge(s_y, 2 * b + 2)
                for m in range(KH):
                    pe.wait_ge(s_hlo, 2 * b + m + 1)
                    for q in range(2):
                        for u, v in ((0, hh), (0, hl), (1, hh)):
                            mm = nc.tensor.matmul(bank[4 + q][:, :], v[:, m, q * P:(q + 1) * P], W2[:, u, m, :], start=(m == 0 and u == 0 and v is hh),
                                                  stop=(m == KH - 1 and u == 1))
                    if m == 0:
                        turn_rows(b + 1, 1)
                mm.then_inc(s_l2, 1)

            pe.wait_ge(s_tok, 1)
            pe.sem_inc(s_y, 2)
            for q in range(2):
                turn_rows(0, q)
            with pe.Fori(0, EXPERTS // 2) as i:
                for w in range(2):
                    pe.wait_ge(s_wl[w], 16 * i + 16)
                    pe.sem_inc(s_go, 1)
                    b_from = pe.value_load(start_i[0:1, bass.ds(2 * i + w, 1)], min_val=0, max_val=ROUTED_SB)
                    b_to = pe.value_load(start_i[0:1, bass.ds(2 * i + w + 1, 1)], min_val=1, max_val=ROUTED_SB)
                    with pe.Fori(b_from, b_to) as b:
                        superblock(b, w)

            def turn_s(s, w, q):
                pe.wait_ge(s_xs[w], 8 * (s - w) + 16)
                turn(turned[q], xs[:, w, q, :]).then_inc(s_st, 1)

            def shared_block(s, w, nq, next_nq):
                pe.wait_ge(s_sxh, 2 * s + nq)
                pe.wait_ge(s_sxl, 2 * s + nq)
                for u in range(UNITS):
                    pe.wait_ge(s_sg, UNITS * s + u + 1)
                    o = bank[2 + u % 2][:, 0:nq * P].rearrange("p (q n) -> p q n", q=nq)
                    first_layer(o, halves(u // KH)[0], u % KH, nq).then_inc(s_sl1, 1)
                if next_nq:
                    turn_s(s + 1, 1 - w, 0)
                pe.wait_ge(s_base, 2 * s + 2)
                for u in range(UNITS):
                    W2 = halves(u // KH)[1]
                    pe.wait_ge(s_shl, UNITS * s + u + 1)
                    for q in range(nq):
                        for part, v in ((0, hhs), (0, hls), (1, hhs)):
                            mm = nc.tensor.matmul(bank[4 + q][:, :], v[:, u, q * P:(q + 1) * P], W2[:, part, u % KH, :], start=(u == 0 and part == 0 and v is hhs),
                                                  stop=(u == UNITS - 1 and part == 1))
                    if u == 1 and next_nq == 2:
                        turn_s(s + 1, 1 - w, 1)
                mm.then_inc(s_sl2, 1)

            pe.wait_ge(s_xhi, 2 * ROUTED_SB + 2)
            pe.wait_ge(s_xlo, 2 * ROUTED_SB + 2)
            pe.wait_ge(s_g, KH * ROUTED_SB + 2)
            pe.wait_ge(s_y, 2 * ROUTED_SB + 2)
            for w in range(2):
                pe.wait_ge(s_wl[w], 16 * (NE // 2))
            pe.sem_inc(s_base, 2)
            for q in range(2):
                turn_s(0, 0, q)
            with pe.Fori(0, SHARED_SB // 2 - 1) as h:
                for w in range(2):
                    shared_block(2 * h + w, w, 2, 2)
            shared_block(SHARED_SB - 3, 0, 2, 2)
            shared_block(SHARED_SB - 2, 1, 2, 1)
            shared_block(SHARED_SB - 1, 0, 1, 0)


def kernel(x, src, dst, L0_gnn_W, L0_gnn_b, L0_gnn_gamma, L0_gnn_beta, L0_ffn_gate_w, L0_ffn_re_w1, L0_ffn_re_b1, L0_ffn_re_w2, L0_ffn_re_b2, L0_ffn_se_w1, L0_ffn_se_b1, L0_ffn_se_w2, L0_ffn_se_b2):
    import numpy as np
    import concourse.bacc as bacc
    from concourse.bass_utils import run_bass_kernel_spmd

    nc = bacc.Bacc("TRN2", target_bir_lowering=False, num_devices=1)
    edges = CPAD * P - EDGES
    dst_rows = np.pad(np.asarray(dst), (0, edges), constant_values=NP).reshape(CPAD, P)
    src_rows = np.pad(np.asarray(src), (0, edges)).reshape(CPAD, P)
    laid = {
        "x": np.pad(np.asarray(x), ((0, NP - N), (0, 0))),
        "src_cols": src_rows.T, "dst_cols": dst_rows.T, "dst_rows": dst_rows,
        "w_t": np.asarray(L0_gnn_W).T,
        "b_cols": np.asarray(L0_gnn_b).reshape(KD, P).T,
        "gamma_cols": np.asarray(L0_gnn_gamma).reshape(KD, P).T,
        "beta_cols": np.asarray(L0_gnn_beta).reshape(KD, P).T,
        "gate_t": np.asarray(L0_ffn_gate_w).T,
        "w1": np.concatenate([np.asarray(L0_ffn_re_w1), np.asarray(L0_ffn_se_w1)]),
        "b1_cols": np.concatenate([np.asarray(L0_ffn_re_b1), np.asarray(L0_ffn_se_b1)]).reshape(NE * KH, P).T,
        "w2": np.concatenate([np.asarray(L0_ffn_re_w2), np.asarray(L0_ffn_se_w2)]),
        "b2": np.concatenate([np.asarray(L0_ffn_re_b2), np.asarray(L0_ffn_se_b2)]),
    }
    arrays, args = {}, []
    for name, a in laid.items():
        a = np.ascontiguousarray(a)
        arrays[f"in_{name}"] = a
        args.append(nc.dram_tensor(f"in_{name}", a.shape, mybir.dt.from_np(a.dtype), kind="ExternalInput").ap())
    args.append(nc.dram_tensor("out_x", (NP, D), F32, kind="ExternalOutput").ap())
    gnn_ffn(nc, *args)
    r = run_bass_kernel_spmd(nc, [arrays], core_ids=[0])
    return r.results[0]["out_x"][:N]
```

```python
from contextlib import ExitStack

import concourse.bass as bass
from concourse import mybir

F32 = mybir.dt.float32
F16 = mybir.dt.float16
I32 = mybir.dt.int32
ALU = mybir.AluOpType
ACT = mybir.ActivationFunctionType
AX = mybir.AxisListType

P = 128
N = 6250
D = 512
KD = D // P
T = -(-N // P)
NP = T * P
LAST = N - (T - 1) * P
EDGES = 106250
CHUNKS = -(-EDGES // P)
RING = 16
PACK = 2
LAG_PACKS = 3
LAG = (LAG_PACKS + 1) * PACK
CPART, CBLK = 128, 7
CPAD = CPART * CBLK
OH = 28
NB = CPAD // OH
GRP = 7
Z_ACT = 4
BIG = 1000
YS = 1024.0
TG = 16
GROUPS = -(-T // TG)
EPS = 1e-5
HID = 256
KH = HID // P
EXPERTS = 16
SHARED = 2
NE = EXPERTS + SHARED
TOP = 4
SB = 2 * P
ROUTED_SB = (NP * TOP + EXPERTS * SB) // SB
SHARED_SB = -(-NP // SB)
RB = 2 * ROUTED_SB
UNITS = SHARED * KH
WL = KD * HID
MAX_FROM, SPLIT_FROM = 2, 29
assert KH == 2 and ROUTED_SB % 2 == 0 and SHARED == 2 and EXPERTS % 2 == 0 and T == 2 * SHARED_SB - 1 and SHARED_SB % 2 == 1 and KH * D == WL and 2 * (SPLIT_FROM - (MAX_FROM + NE + 1)) > LAG and SPLIT_FROM + NE <= T
assert GROUPS == 4 and 2 * RB <= 512
assert CPAD >= CHUNKS + RING - 1 and NB % 2 == 0 and T == GRP * GRP


def gnn_ffn(nc, x, src_cols, dst_cols, dst_rows, w_t, b_cols, gamma_cols, beta_cols, gate_t, w1, b1_cols, w2, b2, out):
    ytab = nc.dram_tensor("ytab", [NP, 2 * D], F16, kind="Internal").ap()
    x1tab = nc.dram_tensor("x1tab", [NP, D], F32, kind="Internal").ap()
    xntab = nc.dram_tensor("xntab", [NP, 2 * D], F16, kind="Internal").ap()
    wtab = nc.dram_tensor("wtab", [NE, P, 4 * WL], F16, kind="Internal").ap()
    btab = nc.dram_tensor("btab", [ROUTED_SB * SB, D], F32, kind="Internal").ap()

    with ExitStack() as ctx:
        def sb(name, shape, dt):
            return ctx.enter_context(nc.sbuf_tensor(name, shape, dt))

        def ps(name, shape, dt):
            return ctx.enter_context(nc.psum_tensor(name, shape, dt))

        def sem(name):
            return ctx.enter_context(nc.semaphore(name))

        big = sb("big", [P, T * D], F32)
        x_all = big[:, :].rearrange("p (t d) -> p t d", d=D)
        h_t = big[:, :].rearrange("p (k n) -> p k n", k=KD)
        src_i = sb("src_i", [P, CPAD], I32)
        dst_i = sb("dst_i", [P, CPAD], I32)
        dst_f = sb("dst_f", [P, CPAD], F32)
        weight_parts = sb("weight_parts", [P, 2, 4 * WL], F16)
        wspl_flat = weight_parts[:, :, :].rearrange("p b n -> p (b n)")
        dst_h = wspl_flat[:, 0:CPAD]
        dst_l = wspl_flat[:, CPAD:2 * CPAD]
        tmp_i = wspl_flat[:, 2 * CPAD:4 * CPAD].bitcast(I32)
        dr_i = wspl_flat[0:CPART, 4 * CPAD:6 * CPAD].bitcast(I32).rearrange("p (b j) -> p b j", j=P)
        arena = sb("arena", [P, RING * 2 * D], F16)
        oh_l = arena[:, 0:2 * P * OH].rearrange("p (b j c) -> p b j c", b=2, c=OH)
        iota_rep = arena[:, 2 * P * OH:3 * P * OH].rearrange("p (j c) -> p j c", c=OH)
        oh_h = arena[:, 3 * P * OH:3 * P * OH + 2 * T * OH].rearrange("p (b j c) -> p b j c", b=2, c=OH)
        z = arena[:, 0:2 * GRP * D].bitcast(F32).rearrange("p (k d) -> p k d", d=D)
        yrow = arena[:, 2 * GRP * D:4 * GRP * D].rearrange("p (k d) -> p k d", d=2 * D)
        reach = wspl_flat[0:CPART, 6 * CPAD:6 * CPAD + 8 * T * CBLK].bitcast(F32).rearrange("p (a t b) -> p a t b", a=4, b=CBLK)
        iota16 = sb("iota16", [P, P], F16)
        iota_t = sb("iota_t", [P, T], F32)
        tbase = sb("tbase", [P, T], F32)
        chunk_id = sb("chunk_id", [CPART, CBLK], F32)
        chunk_first = sb("chunk_first", [CPART, CBLK], F32)
        chunk_last = sb("chunk_last", [CPART, CBLK], F32)
        bounds = sb("bounds", [CPART, 2, T], F32)
        range_col = sb("range_col", [T, 8], F32)
        range_col_i = sb("range_col_i", [T, 2], I32)
        range_row = sb("range_row", [1, 8, T], F32)
        tab = sb("tab", [1, 3, T], I32)
        step_count = sb("step_count", [1, 8], F32)
        group_count_i = sb("group_count_i", [1, 4], I32)
        ident = sb("ident", [P, P], F32)
        upper16 = sb("upper16", [P, P], F16)
        ones16 = sb("ones16", [P, P], F16)
        ident16 = sb("ident16", [P, P], F16)
        upper = sb("upper", [T, T], F32)
        ones = sb("ones", [P, P], F32)
        zero16 = sb("zero16", [1, D], F16)
        deg = sb("deg", [P, T], F32)
        mhalf = sb("mhalf", [P, T], F32)
        dinv = sb("dinv", [P, T], F32)
        dinv_ys = sb("dinv_ys", [P, T], F32)
        raw_weights = sb("raw_weights", [P, 2, 2, WL], F32)
        sum_x = sb("sum_x", [P, T], F32)
        nmean = sb("nmean", [P, T], F32)
        ssq = sb("ssq", [P, T], F32)
        spare_rows = raw_weights[:, :, :, :].rearrange("p a b n -> p (a b n)").bitcast(F16).rearrange("p (r d) -> p r d", d=D)
        x_var = sb("x_var", [P, T], F32)
        rstd = sb("rstd", [P, T], F32)
        row_scale = sb("row_scale", [P, T], F32)
        row_shift = sb("row_shift", [P, T], F32)
        rows = arena[:, 0:RING * 2 * D].rearrange("p (k d) -> p k d", k=RING)
        idx = sb("idx", [P, RING], I32)
        sel = sb("sel", [P, RING, P], F16)
        rows_flat = arena[:, 0:RING * 2 * D]
        sel_flat = sel[:, :, :].rearrange("p k n -> p (k n)")
        yself = sb("yself", [P, 2 * D], F16)
        tile_sum = sb("tile_sum", [P, D], F32)
        tile_sum_t = sb("tile_sum_t", [P, KD, P], F32)
        w_sb = sb("w_sb", [P, KD, D], F32)
        bcol = sb("bcol", [P, 3, KD], F32)
        batch_stats = sb("batch_stats", [P, KD, T, 6], F32)
        batch_moments = sb("batch_moments", [P, KD, 2], F32)

        wmx = sb("wmx", [P, 2, NE], F32)
        overall_max = sb("overall_max", [P, 4], F32)
        max_rows = sb("max_rows", [P, 3, P], F32)
        exponent_i = sb("exponent_i", [P, 8], I32)
        exponent_f = sb("exponent_f", [P, 8], F32)
        scale_bits = sb("scale_bits", [P, 8], I32)
        scl = scale_bits[:, :].bitcast(F32)
        scale_w1, scale_w2, scale_h, unscale_1, unscale_2 = (scl[:, i:i + 1] for i in range(5))
        b1_cols_sb = sb("b1_cols_sb", [P, NE * KH], F32)
        bn_a = sb("bn_a", [P, KD], F32)
        bn_b = sb("bn_b", [P, KD], F32)
        bn_v = sb("bn_v", [P, KD], F32)
        gate = sb("gate", [P, KD, EXPERTS], F32)
        ln_scale_plus_1 = sb("ln_scale_plus_1", [P, T], F32)
        ln_shift = sb("ln_shift", [P, T], F32)
        x1_moments = sb("x1_moments", [P, 2, 2], F32)
        x1_stats = sb("x1_stats", [P, 2, 6], F32)
        x1_var = sb("x1_var", [P, 2], F32)
        x1_rstd = sb("x1_rstd", [P, 2], F32)
        x1_shift = sb("x1_shift", [P, 2], F32)
        choice_idx = sb("choice_idx", [P, 2, TOP], I32)
        gather_idx = sb("gather_idx", [P, 2, 2], I32)
        start_f = sb("start_f", [1, EXPERTS + 3], F32)
        start_i = sb("start_i", [1, EXPERTS + 3], I32)
        expert_of_block = sb("expert_of_block", [1, ROUTED_SB], I32)

        big16 = big[:, :].bitcast(F16)

        def views(base, specs):
            at, out_views = 0, []
            for shape, dt in specs:
                size = 1
                for q in shape:
                    size *= q
                width = size if dt == F16 else 2 * size
                v = base[:, at:at + width]
                if dt != F16:
                    v = v.bitcast(dt)
                if len(shape) > 1:
                    names = "abcd"[:len(shape)]
                    v = v.rearrange("p (" + " ".join(names) + ") -> p " + " ".join(names), **dict(zip(names, shape)))
                out_views.append(v)
                at += width
            return out_views

        logits, choice_weight, slot_i, token_of_place = views(raw_weights[:, :, :, :].rearrange("p a b n -> p (a b n)").bitcast(F16), [
            ((T, EXPERTS), F32), ((T, TOP), F32), ((T, TOP), I32), ((RB + 4,), I32)])
        x_again, x1, xn, xn_t, g_tile = views(arena, [((2, D), F32)] * 3 + [((2, KD, P), F32)] * 2)
        xn_row, b2s = views(arena[:, 12288:], [((2, 2 * D), F16), ((SHARED, D), F32)])
        x1b = sel_flat.bitcast(F32).rearrange("p (a d) -> p a d", a=2)
        G = (T, EXPERTS)
        (probs, hot, tmp_a, tmp_b, cum_a, cum_b, rank_s, mask16, rev16, top_v, vec_a, vec_b, place_row, place_block, tval,
         oh_r, oh_b, iota_b, vcol, ebt, iota_sb) = views(big16, [
            (G, F32), ((TOP,) + G, F32), (G, F32), (G, F32), (G, F32), (G, F32), (G, F32), (G, F16), (G, F32), ((TOP, T), F32),
            ((TOP, T), F32), ((TOP, T), F32), ((T, TOP), F32), ((T, TOP), F32), ((T,), F32),
            ((TOP, P), F16), ((TOP, RB), F16), ((RB,), F16), ((TG,), F32), ((ROUTED_SB, EXPERTS), F32), ((ROUTED_SB,), F32)])
        (tot_e, pre_e, pre_e2, blk_e) = views(arena[:, 10240:], [((EXPERTS,), F32), ((EXPERTS,), F32), ((EXPERTS,), F32), ((EXPERTS,), I32)])
        token_of_place_f = views(arena[:, 11264:], [((RB + 4,), F32)])[0]
        expert_weights, b2_rows, gathered_rows, taken_rows, x_hl, hidden_f32, hidden_hi, hidden_lo, result_rows, shared_rows = views(big16, [
            ((2, 4 * WL), F16), ((EXPERTS, D), F32), ((2, 2, 2 * D), F16), ((2, 2 * D), F16), ((2, 2, KD, P), F16),
            ((KH, SB), F32), ((KH, SB), F16), ((KH, SB), F16), ((2, 2, D), F32), ((2, 2, 2 * D), F16)])
        choice_rows, x1r, acc, shared_hidden, shared_hidden_hi, shared_hidden_lo = views(arena, [
            ((2, TOP, D), F32), ((2, D), F32), ((2, D), F32), ((UNITS, SB), F32), ((UNITS, SB), F16), ((UNITS, SB), F16)])
        half_unscale = exponent_f[:, 5:6]

        bank = [ps(f"bank{i}", [P, 512], F32) for i in range(8)]
        deg_ps, bounds_ps = bank[0], bank[1]
        sum_bank = [bank[2], bank[3]]

        def even_slot(slot):
            return nc.s_assert_within(slot, 0, RING - 2, skip_runtime_bounds_check_because="the count of steps is even")

        def cut(b, k, w=P):
            return bank[b][:, 0:k * w].rearrange("p (k n) -> p k n", k=k)

        turned = [[bank[q + 6 * u][:, :].bitcast(F16)[:, 0:D].rearrange("p (k n) -> p k n", k=KD) for u in range(2)] for q in range(2)]
        sum_t_ps, proj_ps, max_ps = cut(4, KD), cut(5, KD), cut(6, 3)

        dst_loaded = sem("dst_loaded")
        src_loaded = sem("src_loaded")
        x_loaded = [sem(f"x_loaded_{i}") for i in range(GRP)]
        gnn_params_loaded = sem("gnn_params_loaded")
        consts_ready = sem("consts_ready")
        vector_chain = sem("vector_chain")
        pool_chain = sem("pool_chain")
        pool_go = sem("pool_go")
        onehots_ready = sem("onehots_ready")
        onehots_used = sem("onehots_used")
        degrees_summed = sem("degrees_summed")
        degrees_kept = sem("degrees_kept")
        dinv_ready = sem("dinv_ready")
        chunk_bounds_ready = sem("chunk_bounds_ready")
        chunk_bounds_turned = sem("chunk_bounds_turned")
        tile_ranges_ready = sem("tile_ranges_ready")
        tile_range_rows_ready = sem("tile_range_rows_ready")
        range_table_ready = sem("range_table_ready")
        row_sums_done = sem("row_sums_done")
        neg_mean_ready = sem("neg_mean_ready")
        row_squares_done = sem("row_squares_done")
        x_variance_ready = sem("x_variance_ready")
        x_rstd_ready = sem("x_rstd_ready")
        row_scales_ready = sem("row_scales_ready")
        z_by_scalar = sem("z_by_scalar")
        z_by_vector = sem("z_by_vector")
        row_high_ready = sem("row_high_ready")
        row_low_ready = sem("row_low_ready")
        row_stored = [sem(f"row_stored_{i}") for i in range(GRP)]
        row_table_complete = sem("row_table_complete")
        selector_ready = sem("selector_ready")
        pack_gathered = [sem(f"pack_gathered_{i}") for i in range(RING // PACK)]
        rows_landed = sem("rows_landed")
        rows_summed = sem("rows_summed")
        own_rows_loaded = sem("own_rows_loaded")
        tile_summed = sem("tile_summed")
        tile_sum_kept = sem("tile_sum_kept")
        tile_sum_turned = sem("tile_sum_turned")
        turned_sum_kept = sem("turned_sum_kept")
        tile_projected = sem("tile_projected")
        projection_kept = sem("projection_kept")
        batch_stats_done = sem("batch_stats_done")
        raw_weights_loaded = [sem(f"raw_weights_loaded_{i}") for i in range(2)]
        weight_maxima_done = sem("weight_maxima_done")
        maxima_ready = sem("maxima_ready")
        maxima_turned = sem("maxima_turned")
        weight_high_ready = sem("weight_high_ready")
        weight_low_ready = sem("weight_low_ready")
        weights_stored = [sem(f"weights_stored_{i}") for i in range(2)]
        b1_loaded = sem("b1_loaded")
        gate_loaded = sem("gate_loaded")
        batch_var_ready = sem("batch_var_ready")
        batch_rstd_ready = sem("batch_rstd_ready")
        bn_coeffs_ready = sem("bn_coeffs_ready")
        residual_may_load = sem("residual_may_load")
        shared_bias_loaded = sem("shared_bias_loaded")
        residual_x_loaded = [sem(f"residual_x_loaded_{i}") for i in range(2)]
        gelu_ready = sem("gelu_ready")
        gelu_turned = sem("gelu_turned")
        scaled_x_ready = sem("scaled_x_ready")
        x1_ready = sem("x1_ready")
        x1_stats_done = sem("x1_stats_done")
        x1_moments_ready = sem("x1_moments_ready")
        x1_var_ready = sem("x1_var_ready")
        x1_rstd_ready = sem("x1_rstd_ready")
        x1_shift_ready = sem("x1_shift_ready")
        biased_x1_ready = sem("biased_x1_ready")
        xn_ready = sem("xn_ready")
        xn_high_ready = sem("xn_high_ready")
        xn_low_ready = sem("xn_low_ready")
        xn_turned = sem("xn_turned")
        turned_xn_kept = sem("turned_xn_kept")
        logits_summed = sem("logits_summed")
        logits_kept = sem("logits_kept")
        x1_stored = [sem(f"x1_stored_{i}") for i in range(2)]
        xn_stored = [sem(f"xn_stored_{i}") for i in range(2)]
        spare_results_filled = sem("spare_results_filled")
        phase_a_stored = sem("phase_a_stored")
        routing_consts_ready = sem("routing_consts_ready")
        logits_shifted = sem("logits_shifted")
        probs_exp_done = sem("probs_exp_done")
        top_shifted = sem("top_shifted")
        top_exp_done = sem("top_exp_done")
        choice_mask_ready = sem("choice_mask_ready")
        ranks_summed = sem("ranks_summed")
        place_onehots_ready = sem("place_onehots_ready")
        place_onehots_used = sem("place_onehots_used")
        tokens_by_place_ready = sem("tokens_by_place_ready")
        b2_loaded = sem("b2_loaded")
        expert_weights_loaded = [sem(f"expert_weights_loaded_{i}") for i in range(2)]
        gather_index_ready = sem("gather_index_ready")
        xrows_gathered = [[sem(f"xrows_gathered_{j}{q}") for q in range(2)] for j in range(2)]
        xrows_taken = sem("xrows_taken")
        xrows_turned = sem("xrows_turned")
        x_parts_ready = sem("x_parts_ready")
        first_layer_summed = sem("first_layer_summed")
        hidden_gelu_done = sem("hidden_gelu_done")
        hidden_high_ready = sem("hidden_high_ready")
        hidden_low_ready = sem("hidden_low_ready")
        second_layer_summed = sem("second_layer_summed")
        results_ready = sem("results_ready")
        results_stored = [sem(f"results_stored_{i}") for i in range(2)]
        shared_rows_loaded = [sem(f"shared_rows_loaded_{i}") for i in range(2)]
        shared_rows_turned = sem("shared_rows_turned")
        shared_x_parts_ready = sem("shared_x_parts_ready")
        shared_first_layer_summed = sem("shared_first_layer_summed")
        shared_gelu_done = sem("shared_gelu_done")
        shared_high_ready = sem("shared_high_ready")
        shared_low_ready = sem("shared_low_ready")
        shared_second_layer_summed = sem("shared_second_layer_summed")
        x1_loaded = [sem(f"x1_loaded_{i}") for i in range(2)]
        base_sum_ready = sem("base_sum_ready")
        choice_index_ready = sem("choice_index_ready")
        choices_gathered = [sem(f"choices_gathered_{i}") for i in range(2)]
        choice_added = sem("choice_added")
        out_stored = [sem(f"out_stored_{i}") for i in range(2)]

        block = ctx.enter_context(nc.Block())

        @block.sync
        def _(sp):
            sp.dma_start(dst_i[:, :], dst_cols).then_inc(dst_loaded, 16)
            sp.dma_start(dr_i[:, :, :], dst_rows.rearrange("(b p) j -> p b j", p=CPART)).then_inc(dst_loaded, 16)
            sp.dma_start(src_i[:, :], src_cols).then_inc(src_loaded, 16)
            xv = x.rearrange("(t p) d -> p t d", p=P)
            for g in range(GRP):
                sp.dma_start(x_all[:, g * GRP:(g + 1) * GRP, :], xv[:, g * GRP:(g + 1) * GRP, :]).then_inc(x_loaded[g], 16)
            sp.dma_start(w_sb[:, :, :], w_t.rearrange("(k p) n -> p k n", p=P)).then_inc(gnn_params_loaded, 16)
            sp.dma_start(bcol[:, 0, :], b_cols).then_inc(gnn_params_loaded, 16)
            sp.dma_start(bcol[:, 1, :], gamma_cols).then_inc(gnn_params_loaded, 16)
            sp.dma_start(bcol[:, 2, :], beta_cols).then_inc(gnn_params_loaded, 16)
            yv = ytab.rearrange("(t p) d -> p t d", p=P)
            with sp.Fori(0, GRP) as g:
                for k in range(GRP):
                    sp.wait_ge(row_low_ready, g * GRP + k + 1)
                    sp.dma_start(yv[:, bass.ds(g * GRP + k, 1), :], yrow[:, k:k + 1, :]).then_inc(row_stored[k], 16)
            for k in range(GRP):
                sp.wait_ge(row_stored[k], 16 * GRP)
            sp.sem_inc(row_table_complete, 1)
            sp.dma_start(b1_cols_sb[:, :], b1_cols).then_inc(b1_loaded, 16)
            sp.dma_start(gate[:, :, :], gate_t.rearrange("(k p) e -> p k e", p=P)).then_inc(gate_loaded, 16)

            def load_raw(e, j):
                sp.dma_start(raw_weights[:, j, 0, :].rearrange("p (k n) -> p k n", k=KD), w1[bass.ds(e, 1)].rearrange("e (k p) n -> p (e k) n", p=P)).then_inc(raw_weights_loaded[j], 16)
                sp.dma_start(raw_weights[:, j, 1, :].rearrange("p (k n) -> p k n", k=KH), w2[bass.ds(e, 1)].rearrange("e (k p) n -> p (e k) n", p=P)).then_inc(raw_weights_loaded[j], 16)

            for j in range(2):
                load_raw(j, j)
            with sp.Fori(1, NE // 2) as i:
                for j in range(2):
                    sp.wait_ge(weight_maxima_done, 2 * i + j - 1)
                    load_raw(2 * i + j, j)
            for j in range(2):
                sp.wait_ge(weight_maxima_done, NE + j - 1)
                load_raw(j, j)
            with sp.Fori(0, NE // 2 - 1) as i:
                for j in range(2):
                    sp.wait_ge(weight_low_ready, 2 * i + j + 1)
                    sp.dma_start(wtab[bass.ds(2 * i + j, 1)].rearrange("e p n -> p (e n)"), weight_parts[:, j, :]).then_inc(weights_stored[j], 16)
                    load_raw(2 * i + j + 2, j)
            for j in range(2):
                sp.wait_ge(weight_low_ready, NE - 1 + j)
                sp.dma_start(wtab[NE - 2 + j], weight_parts[:, j, :]).then_inc(weights_stored[j], 16)

            sp.wait_ge(residual_may_load, 1)
            xt = lambda tab, t: tab[bass.ds(t * P, P), :]
            sp.dma_start(b2s, b2[EXPERTS:NE].unsqueeze(0).to_broadcast([P, SHARED, D])).then_inc(shared_bias_loaded, 16)

            def store_rows(t, j):
                sp.wait_ge(biased_x1_ready, t + 1)
                sp.dma_start(xt(x1tab, t), x1b[:, j, :]).then_inc(x1_stored[j], 16)
                sp.wait_ge(xn_low_ready, t + 1)
                sp.dma_start(xt(xntab, t), xn_row[:, j, :]).then_inc(xn_stored[j], 16)

            for t in range(2):
                sp.dma_start(x_again[:, t, :], xt(x, t)).then_inc(residual_x_loaded[t], 16)
            with sp.Fori(1, T // 2) as h:
                for j in range(2):
                    sp.wait_ge(scaled_x_ready, 2 * h + j - 1)
                    sp.dma_start(x_again[:, j, :], xt(x, 2 * h + j)).then_inc(residual_x_loaded[j], 16)
                    store_rows(2 * h + j - 2, j)
            sp.wait_ge(scaled_x_ready, T - 2)
            sp.dma_start(x_again[:, 0, :], xt(x, T - 1)).then_inc(residual_x_loaded[0], 16)
            for t in range(T - 3, T):
                store_rows(t, t % 2)
            spare = (NP * TOP // SB) * SB
            sp.dma_start(btab[spare:, :].rearrange("(n p) d -> p n d", p=P),
                         w_sb[:, 0:1, :].to_broadcast([P, (ROUTED_SB * SB - spare) // P, D])).then_inc(spare_results_filled, 16)
            sp.wait_ge(spare_results_filled, 16)
            for j in range(2):
                sp.wait_ge(x1_stored[j], 16 * ((T + 1 - j) // 2))
                sp.wait_ge(xn_stored[j], 16 * ((T + 1 - j) // 2))
                sp.wait_ge(weights_stored[j], 16 * (NE // 2))
            sp.sem_inc(phase_a_stored, 1)

            sp.wait_ge(tokens_by_place_ready, 1)
            for j in range(2):
                sp.dma_start(expert_weights[:, j, :], wtab[j]).then_inc(expert_weights_loaded[j], 16)
            sp.dma_start(b2_rows[:, :, :], b2[0:EXPERTS].unsqueeze(0).to_broadcast([P, EXPERTS, D])).then_inc(b2_loaded, 16)

            def load_xs(s, w, nq):
                sp.dma_start(shared_rows[:, w, 0:nq, :], xntab[bass.ds(s * SB, nq * P), :].rearrange("(q p) d -> p q d", q=nq)).then_inc(shared_rows_loaded[w], 16)

            def load_x1(t, q):
                sp.dma_start(x1r[:, q, :], xt(x1tab, t)).then_inc(x1_loaded[q], 16)

            for w in range(2):
                load_xs(w, w, 2)
                load_x1(w, w)
            with sp.Fori(1, NE // 2) as i:
                for j in range(2):
                    done = sp.value_load(start_i[0:1, bass.ds(2 * i + j - 1, 1)], min_val=1, max_val=ROUTED_SB)
                    sp.wait_ge(second_layer_summed, done)
                    sp.dma_start(expert_weights[:, j, :], wtab[bass.ds(2 * i + j, 1)].rearrange("e p n -> p (e n)")).then_inc(expert_weights_loaded[j], 16)

            def store_out(t, q):
                sp.wait_ge(choice_added, TOP * t + TOP)
                sp.dma_start(xt(out, t), acc[:, q, :]).then_inc(out_stored[q], 16)

            def refill(s, w, xs_nq, x1_nq):
                if xs_nq:
                    sp.wait_ge(shared_rows_turned, 2 * s)
                    load_xs(s + 1, w, xs_nq)
                for q in range(x1_nq):
                    sp.wait_ge(base_sum_ready, 2 * s + q + 1)
                    load_x1(2 * s + q, q)
                for q in range(2):
                    store_out(2 * s - 2 + q, q)

            with sp.Fori(1, SHARED_SB // 2) as h:
                for j in range(2):
                    refill(2 * h + j - 1, j, 2, 2)
            refill(SHARED_SB - 2, 0, 1, 2)
            refill(SHARED_SB - 1, 1, 0, 1)
            store_out(T - 1, 0)
            for j in range(2):
                sp.wait_ge(out_stored[j], 16 * ((T + 1 - j) // 2))

        @block.gpsimd
        def _(pool):
            n = [0]

            def link(ins):
                n[0] += 1
                ins.then_inc(pool_chain, 1)
                pool.wait_ge(pool_chain, n[0])

            pool.iota(iota_rep[:, :, :], [[1, P], [0, OH]], base=0, channel_multiplier=0,
                      allow_small_or_imprecise_dtypes=True).then_inc(consts_ready, 1)
            pool.iota(iota16[:, :], [[1, P]], base=0, channel_multiplier=0,
                      allow_small_or_imprecise_dtypes=True).then_inc(consts_ready, 1)
            pool.iota(iota_t[:, :], [[1, T]], base=0, channel_multiplier=0,
                      allow_small_or_imprecise_dtypes=True).then_inc(consts_ready, 1)
            pool.iota(tbase[:, :], [[P, T]], base=0, channel_multiplier=0,
                      allow_small_or_imprecise_dtypes=True).then_inc(consts_ready, 1)
            pool.iota(chunk_id[:, :], [[CPART, CBLK]], base=0, channel_multiplier=1,
                      allow_small_or_imprecise_dtypes=True).then_inc(consts_ready, 1)
            pool.memset(ones[:, :], 1.0).then_inc(consts_ready, 1)
            pool.memset(mhalf[:, :], -0.5).then_inc(consts_ready, 1)
            pool.memset(zero16[:, :], 0.0).then_inc(consts_ready, 1)
            pool.memset(ones16[:, :], 1.0).then_inc(consts_ready, 1)
            pool.wait_ge(consts_ready, 9)
            pool.affine_select(out=ident[:, :], in_=ones[:, :], pattern=[[-1, P]], compare_op=ALU.is_equal,
                               fill=0.0, base=0, channel_multiplier=1).then_inc(consts_ready, 1)
            pool.affine_select(out=upper[:, :], in_=ones[0:T, 0:T], pattern=[[1, T]], compare_op=ALU.is_gt,
                               fill=0.0, base=0, channel_multiplier=-1).then_inc(consts_ready, 1)
            pool.affine_select(out=upper16[:, :], in_=ones16[:, :], pattern=[[1, P]], compare_op=ALU.is_gt,
                               fill=0.0, base=0, channel_multiplier=-1).then_inc(consts_ready, 1)
            pool.wait_ge(consts_ready, 12)
            pool.tensor_copy(ident16[:, :], ident[:, :]).then_inc(consts_ready, 1)
            pool.wait_ge(degrees_kept, 1)
            pool.tensor_tensor(dinv[:, :], deg[:, :], mhalf[:, :], ALU.pow).then_inc(dinv_ready, 1)
            pool.wait_ge(x_variance_ready, 1)
            pool.tensor_tensor(rstd[:, :], x_var[:, :], mhalf[:, :], ALU.pow).then_inc(x_rstd_ready, 1)
            pool.wait_ge(range_table_ready, 1)
            groups = pool.value_load(group_count_i[0:1, 0:1], min_val=1, max_val=T * CPAD // RING)
            pool.wait_ge(row_table_complete, 1)
            pool.sem_inc(rows_landed, CPAD)
            def gathers(g, first):
                for q in range(RING // PACK):
                    pool.wait_ge(selector_ready, CPAD + g * RING + (q + 1) * PACK)
                    pool.sem_inc(pool_go, 1)
                    for k in range(q * PACK, (q + 1) * PACK):
                        pool.indirect_dma_start(rows[:, k, :], None, ytab, bass.IndirectOffsetOnAxis(ap=idx[:, k:k + 1], axis=0)).then_inc(pack_gathered[q], 16)
                    if q >= LAG_PACKS or not first:
                        pool.wait_ge(pack_gathered[(q - LAG_PACKS) % (RING // PACK)], (g + 1 if q >= LAG_PACKS else g) * 16 * PACK)
                        pool.sem_inc(rows_landed, PACK)

            gathers(0, True)
            with pool.Fori(1, groups) as g:
                gathers(g, False)
            for q in range(RING // PACK - LAG_PACKS, RING // PACK):
                pool.wait_ge(pack_gathered[q], groups * 16 * PACK)
                pool.sem_inc(rows_landed, PACK)


            pool.wait_ge(batch_var_ready, 1)
            pool.tensor_tensor(bn_a[:, :], bn_v[:, :], mhalf[:, 0:KD], ALU.pow).then_inc(batch_rstd_ready, 1)

            def rstd2(t, j, steady):
                pool.wait_ge(x1_var_ready, t + 1)
                pool.sem_inc(pool_go, 1)
                pool.tensor_tensor(x1_rstd[:, j:j + 1], x1_var[:, j:j + 1], mhalf[:, 0:1], ALU.pow).then_inc(x1_rstd_ready, 1)
                if steady:
                    pool.wait_ge(x1_stored[j], 8 * (t - j))
                    pool.sem_inc(pool_go, 1)
                pool.tensor_tensor(x1b[:, j, :], x1[:, j, :], b2s[:, 0, :], ALU.add).then_inc(biased_x1_ready, 1)

            pool.wait_ge(shared_bias_loaded, 16)
            link(pool.tensor_tensor(b2s[:, 0, :], b2s[:, 0, :], b2s[:, 1, :], ALU.add))
            link(pool.tensor_scalar(b2s[:, 0, :], b2s[:, 0, :], 1.0 / SHARED, None, ALU.mult))
            for t in range(2):
                rstd2(t, t, False)
            with pool.Fori(1, T // 2) as h:
                for j in range(2):
                    pool.wait_ge(x1_shift_ready, 2 * h + j - 1)
                    pool.sem_inc(pool_go, 1)
                    pool.wait_ge(xn_ready, 2 * h + j - 1)
                    pool.sem_inc(pool_go, 1)
                    rstd2(2 * h + j, j, True)
            pool.wait_ge(xn_ready, T - 2)
            rstd2(T - 1, 0, True)

            pool.wait_ge(logits_kept, T)
            pool.iota(rev16, [[0, T], [-1, EXPERTS]], base=EXPERTS, channel_multiplier=0, allow_small_or_imprecise_dtypes=True).then_inc(routing_consts_ready, 1)
            pool.iota(iota_b, [[1, RB]], base=0, channel_multiplier=0, allow_small_or_imprecise_dtypes=True).then_inc(routing_consts_ready, 1)
            pool.iota(vcol, [[P, TG]], base=1, channel_multiplier=1, allow_small_or_imprecise_dtypes=True).then_inc(routing_consts_ready, 1)
            pool.iota(iota_sb, [[1, ROUTED_SB]], base=0, channel_multiplier=0, allow_small_or_imprecise_dtypes=True).then_inc(routing_consts_ready, 1)
            pool.iota(token_of_place_f, [[P, RB + 4]], base=0, channel_multiplier=1, allow_small_or_imprecise_dtypes=True).then_inc(routing_consts_ready, 1)

            pool.wait_ge(tokens_by_place_ready, 1)
            pool.wait_ge(phase_a_stored, 1)

            def gather(b, j, wait):
                if wait:
                    pool.wait_ge(xrows_taken, 2 * b + 2)
                    pool.sem_inc(pool_go, 1)
                pool.tensor_copy(gather_idx[:, j, :], token_of_place[:, bass.ds(2 * b, 2)]).then_inc(gather_index_ready, 1)
                pool.wait_ge(gather_index_ready, b + 1)
                pool.sem_inc(pool_go, 1)
                for q in range(2):
                    pool.indirect_dma_start(gathered_rows[:, j, q, :], None, xntab, bass.IndirectOffsetOnAxis(ap=gather_idx[:, j, q:q + 1], axis=0)).then_inc(xrows_gathered[j][q], 16)

            pairs = pool.value_load(start_i[0:1, EXPERTS + 1:EXPERTS + 2], min_val=EXPERTS // 2, max_val=ROUTED_SB // 2)
            gather(0, 0, False)
            gather(1, 1, False)
            with pool.Fori(1, pairs) as h:
                for j in range(2):
                    gather(2 * h + j, j, True)
            for j in range(2):
                gather(pairs * 2 + j, j, True)
            for j in range(2):
                pool.wait_ge(results_stored[j], pairs * 16)
            pool.sem_inc(pool_go, 1)

            def gather4(t, j, wait):
                if wait:
                    pool.wait_ge(choices_gathered[j], 32 * (t - 2 - j) + 64)
                    pool.sem_inc(pool_go, 1)
                pool.tensor_copy(choice_idx[:, j, :], slot_i[:, bass.ds(t, 1), :].rearrange("p a k -> p (a k)")).then_inc(choice_index_ready, 1)
                pool.wait_ge(choice_index_ready, t + 1)
                pool.sem_inc(pool_go, 1)
                for k in range(TOP):
                    if wait:
                        pool.wait_ge(choice_added, TOP * (t - 2) + k + 1)
                        pool.sem_inc(pool_go, 1)
                    pool.indirect_dma_start(choice_rows[:, j, k, :], None, btab, bass.IndirectOffsetOnAxis(ap=choice_idx[:, j, k:k + 1], axis=0)).then_inc(choices_gathered[j], 16)

            for t in range(2):
                gather4(t, t, False)
            with pool.Fori(1, T // 2) as h:
                for j in range(2):
                    gather4(2 * h + j, j, True)
            gather4(T - 1, 0, True)

        @block.vector
        def _(dve):
            n = [0]

            def link(ins):
                n[0] += 1
                ins.then_inc(vector_chain, 1)
                dve.wait_ge(vector_chain, n[0])

            dve.wait_ge(dst_loaded, 32)
            link(nc.vector.tensor_copy(dst_f[:, :], dst_i[:, :]))
            link(nc.vector.tensor_scalar(tmp_i[:, :], dst_i[:, :], 7, None, ALU.logical_shift_right))
            link(nc.vector.tensor_copy(dst_h[:, :], tmp_i[:, :]))
            link(nc.vector.tensor_scalar(tmp_i[:, :], dst_i[:, :], P - 1, None, ALU.bitwise_and))
            link(nc.vector.tensor_copy(dst_l[:, :], tmp_i[:, :]))
            dve.wait_ge(consts_ready, 9)

            def onehots(i, k):
                c = bass.ds(i * 2 * OH + k * OH, OH)
                nc.vector.tensor_tensor(oh_l[:, k, :, :], iota_rep[:, :, :],
                                        dst_l[:, c].unsqueeze(1).to_broadcast([P, P, OH]), ALU.is_equal).then_inc(onehots_ready, 1)
                nc.vector.tensor_tensor(oh_h[:, k, :, :], iota_rep[:, 0:T, :],
                                        dst_h[:, c].unsqueeze(1).to_broadcast([P, T, OH]), ALU.is_equal).then_inc(onehots_ready, 1)

            for k in range(2):
                onehots(0, k)
            with dve.Fori(1, NB // 2) as i:
                for k in range(2):
                    dve.wait_ge(onehots_used, 2 * i + k - 1)
                    onehots(i, k)
            dve.wait_ge(degrees_summed, 1)
            nc.vector.tensor_copy(deg[:, :], deg_ps[:, 0:T]).then_inc(degrees_kept, 1)
            dve.wait_ge(row_squares_done, T)
            nc.vector.tensor_scalar(x_var[:, :], ssq[:, :], 1.0 / D, EPS, ALU.mult, ALU.add).then_inc(x_variance_ready, 1)
            dve.wait_ge(dinv_ready, 1)
            dve.wait_ge(x_rstd_ready, 1)
            link(nc.vector.tensor_scalar(dinv_ys[:, :], dinv[:, :], 1.0 / YS, None, ALU.mult))
            link(nc.vector.scalar_tensor_tensor(row_scale[:, :], rstd[:, :], YS, dinv[:, :], ALU.mult, ALU.mult))
            nc.vector.tensor_tensor(row_shift[:, :], nmean[:, :], row_scale[:, :], ALU.mult).then_inc(row_scales_ready, 1)
            dve.wait_ge(row_scales_ready, 1)
            link(nc.vector.tensor_scalar(dr_i[:, :, :], dr_i[:, :, :], 7, None, ALU.logical_shift_right))
            link(nc.vector.tensor_reduce(chunk_first[:, :], dr_i[:, :, :], AX.X, ALU.min))
            link(nc.vector.tensor_reduce(chunk_last[:, :], dr_i[:, :, :], AX.X, ALU.max))
            tt = iota_t[0:CPART, :].unsqueeze(2).to_broadcast([CPART, T, CBLK])
            bc = lambda a: a[:, :].unsqueeze(1).to_broadcast([CPART, T, CBLK])
            link(nc.vector.tensor_tensor(reach[:, 0], tt, bc(chunk_first), ALU.is_ge))
            link(nc.vector.tensor_tensor(reach[:, 1], bc(chunk_last), tt, ALU.is_ge))
            link(nc.vector.tensor_tensor(reach[:, 0], reach[:, 0], reach[:, 1], ALU.mult))
            link(nc.vector.tensor_scalar(chunk_first[:, :], chunk_id[:, :], -1.0, float(BIG), ALU.mult, ALU.add))
            link(nc.vector.tensor_scalar(chunk_last[:, :], chunk_id[:, :], 1.0, None, ALU.add))
            link(nc.vector.tensor_tensor(reach[:, 2], reach[:, 0], bc(chunk_first), ALU.mult))
            link(nc.vector.tensor_tensor(reach[:, 3], reach[:, 0], bc(chunk_last), ALU.mult))
            link(nc.vector.tensor_reduce(bounds[:, 0, :], reach[:, 2], AX.X, ALU.max))
            nc.vector.tensor_reduce(bounds[:, 1, :], reach[:, 3], AX.X, ALU.max).then_inc(chunk_bounds_ready, 1)
            dve.wait_ge(chunk_bounds_turned, 1)
            rt = bounds_ps[0:T, 0:2 * CPART].rearrange("t (a c) -> t a c", a=2)
            link(nc.vector.tensor_reduce(range_col[:, 0:2], rt, AX.X, ALU.max))
            link(nc.vector.tensor_scalar(range_col[:, 2:3], range_col[:, 0:1], -1.0, float(BIG), ALU.mult, ALU.add))
            link(nc.vector.tensor_scalar(range_col[:, 2:3], range_col[:, 2:3], float(CHUNKS - 1), None, ALU.min))
            link(nc.vector.tensor_scalar(range_col[:, 3:4], range_col[:, 2:3], 1.0, None, ALU.add))
            link(nc.vector.tensor_tensor(range_col[:, 3:4], range_col[:, 3:4], range_col[:, 1:2], ALU.max))
            link(nc.vector.scalar_tensor_tensor(range_col[:, 4:5], range_col[:, 3:4], 1.0, range_col[:, 2:3], ALU.add, ALU.subtract))
            link(nc.vector.tensor_copy(range_col_i[:, 0:1], range_col[:, 4:5]))
            link(nc.vector.tensor_scalar(range_col_i[:, 1:2], range_col_i[:, 0:1], 1, 1, ALU.logical_shift_right, ALU.logical_shift_left))
            link(nc.vector.tensor_copy(range_col[:, 4:5], range_col_i[:, 1:2]))
            nc.vector.tensor_tensor(range_col[:, 3:4], range_col[:, 2:3], range_col[:, 4:5], ALU.add).then_inc(tile_ranges_ready, 1)
            dve.wait_ge(tile_range_rows_ready, 1)
            link(nc.vector.tensor_copy(range_row[:, 0:3, :], bounds_ps[0:1, 256:256 + 3 * T].rearrange("o (a t) -> o a t", a=3)))
            link(nc.vector.tensor_copy(step_count[:, 0:1], bounds_ps[0:1, 256 + 3 * T:257 + 3 * T]))
            link(nc.vector.tensor_tensor(range_row[:, 2, :], range_row[:, 2, :], range_row[:, 0, :], ALU.subtract))
            link(nc.vector.tensor_scalar(range_row[:, 2, :], range_row[:, 2, :], float(CPAD), None, ALU.add))
            link(nc.vector.tensor_scalar(step_count[:, 1:2], step_count[:, 0:1], float(RING - 1), None, ALU.add))
            link(nc.vector.tensor_copy(group_count_i[:, 1:2], step_count[:, 1:2]))
            link(nc.vector.tensor_scalar(group_count_i[:, 0:1], group_count_i[:, 1:2], RING.bit_length() - 1, None, ALU.logical_shift_right))
            link(nc.vector.tensor_copy(step_count[:, 2:3], group_count_i[:, 0:1]))
            link(nc.vector.tensor_scalar(step_count[:, 3:4], step_count[:, 2:3], float(RING), step_count[:, 0:1], ALU.mult, ALU.subtract))
            link(nc.vector.tensor_tensor(range_row[:, 1, T - 1:T], range_row[:, 1, T - 1:T], step_count[:, 3:4], ALU.add))
            link(nc.vector.tensor_copy(tab[:, :, :], range_row[:, 0:3, :]))
            dve.sem_inc(range_table_ready, 1)
            def rows_lo(g):
                for k in range(Z_ACT, GRP):
                    t = g * GRP + k
                    nc.vector.tensor_scalar(z[:, k, :].unsqueeze(1), x_all[:, bass.ds(t, 1), :], row_scale[:, bass.ds(t, 1)], row_shift[:, bass.ds(t, 1)], ALU.mult, ALU.add).then_inc(z_by_vector, 1)
                for k in range(GRP):
                    dve.wait_ge(row_high_ready, g * GRP + k + 1)
                    if k < Z_ACT:
                        dve.wait_ge(z_by_scalar, g * Z_ACT + k + 1)
                    else:
                        dve.wait_ge(z_by_vector, g * (GRP - Z_ACT) + k - Z_ACT + 1)
                    nc.vector.tensor_tensor(yrow[:, k, D:2 * D], z[:, k, :], yrow[:, k, 0:D], ALU.subtract).then_inc(row_low_ready, 1)

            rows_lo(0)
            with dve.Fori(1, GRP) as g:
                dve.wait_ge(row_low_ready, g * GRP)
                rows_lo(g)

            dve.wait_ge(src_loaded, 16)
            dve.sem_inc(selector_ready, CPAD)

            def tile(t, stats):
                lo = dve.value_load(tab[0:1, 0, bass.ds(t, 1)], min_val=0, max_val=CPAD - 2)
                hi = dve.value_load(tab[0:1, 1, bass.ds(t, 1)], min_val=0, max_val=CPAD - 2)
                off = dve.value_load(tab[0:1, 2, bass.ds(t, 1)], min_val=0, max_val=T * CPAD + CPAD)
                with dve.Fori(lo, hi, 2) as c:
                    s = dve.snap(c + off)
                    slot = even_slot(dve.snap(s % RING))
                    dve.wait_ge(rows_summed, s + 2)
                    nc.vector.tensor_copy(idx[:, bass.ds(slot, 2)], src_i[:, bass.ds(c, 2)])
                    for q in range(2):
                        nc.vector.tensor_scalar(sel[:, bass.ds(slot + q, 1), :], iota16[:, :].unsqueeze(1), tbase[:, bass.ds(t, 1)],
                                                dst_f[:, bass.ds(c + q, 1)], ALU.add, ALU.is_equal).then_inc(selector_ready, 1)
                if stats:
                    dve.wait_ge(projection_kept, t - 1)
                    for m in range(KD):
                        nc.vector.bn_stats(batch_stats[:, m, bass.ds(t - 2, 1), :], h_t[:, m, bass.ds((t - 2) * P, P)].unsqueeze(1)).then_inc(batch_stats_done, 1)

            def weight_max(e, j):
                dve.wait_ge(raw_weights_loaded[j], 16 * (e - j) + 32)
                nc.vector.tensor_reduce(wmx[:, 0, bass.ds(e, 1)], raw_weights[:, j, 0, :], AX.X, ALU.max, apply_absolute_value=True)
                nc.vector.tensor_reduce(wmx[:, 1, bass.ds(e, 1)], raw_weights[:, j, 1, :], AX.X, ALU.max, apply_absolute_value=True).then_inc(weight_maxima_done, 1)

            def weight_split(e, j, wait):
                dve.wait_ge(raw_weights_loaded[j], 16 * (e - j) + 32 + 16 * NE)
                if wait:
                    dve.wait_ge(weights_stored[j], 8 * (e - j))
                for w in range(2):
                    hi = weight_parts[:, j, 2 * w * WL:(2 * w + 1) * WL]
                    lo = weight_parts[:, j, (2 * w + 1) * WL:(2 * w + 2) * WL]
                    nc.vector.tensor_scalar(hi, raw_weights[:, j, w, :], scl[:, w:w + 1], None, ALU.mult).then_inc(weight_high_ready, 1)
                    dve.wait_ge(weight_high_ready, 2 * e + w + 1)
                    last = nc.vector.scalar_tensor_tensor(lo, raw_weights[:, j, w, :], scl[:, w:w + 1], hi, ALU.mult, ALU.subtract)
                last.then_inc(weight_low_ready, 1)

            MAX_TO = MAX_FROM + NE
            tile(0, False)
            tile(1, False)
            with dve.Fori(0, NE // 2) as i:
                for j in range(2):
                    tile(2 * i + j + MAX_FROM, True)
                    weight_max(2 * i + j, j)
            dve.wait_ge(weight_maxima_done, NE)
            dve.wait_ge(b1_loaded, 16)
            link(nc.vector.tensor_reduce(overall_max[:, 0:2], wmx[:, :, :], AX.X, ALU.max))
            link(nc.vector.tensor_reduce(overall_max[:, 2:3], b1_cols_sb[:, :], AX.X, ALU.max, apply_absolute_value=True))
            nc.vector.tensor_copy(max_rows[:, :, :], overall_max[:, 0:3].unsqueeze(2).to_broadcast([P, 3, P])).then_inc(maxima_ready, 1)
            with dve.Fori(MAX_TO, SPLIT_FROM) as t:
                tile(t, True)
            dve.wait_ge(maxima_turned, 1)
            link(nc.vector.tensor_reduce(overall_max[:, 0:3], max_ps, AX.X, ALU.max))
            link(nc.vector.scalar_tensor_tensor(overall_max[:, 2:3], overall_max[:, 0:1], float(D), overall_max[:, 2:3], ALU.mult, ALU.add))
            link(nc.vector.tensor_scalar(exponent_i[:, 0:3], overall_max[:, 0:3].bitcast(I32), 23, None, ALU.logical_shift_right))
            link(nc.vector.tensor_copy(exponent_f[:, 0:3], exponent_i[:, 0:3]))
            link(nc.vector.tensor_scalar(exponent_f[:, 0:3], exponent_f[:, 0:3], 97.0, None, ALU.max))
            link(nc.vector.tensor_scalar(exponent_f[:, 0:3], exponent_f[:, 0:3], -1.0, 268.0, ALU.mult, ALU.add))
            link(nc.vector.tensor_scalar(exponent_f[:, 3:4], exponent_f[:, 0:1], -1.0, 244.0, ALU.mult, ALU.add))
            link(nc.vector.tensor_tensor(exponent_f[:, 4:5], exponent_f[:, 1:2], exponent_f[:, 2:3], ALU.add))
            link(nc.vector.tensor_scalar(exponent_f[:, 4:5], exponent_f[:, 4:5], -1.0, 381.0, ALU.mult, ALU.add))
            link(nc.vector.tensor_copy(exponent_i[:, 0:5], exponent_f[:, 0:5]))
            link(nc.vector.tensor_scalar(scale_bits[:, 0:5], exponent_i[:, 0:5], 23, None, ALU.logical_shift_left))
            for j in range(2):
                tile(j + SPLIT_FROM, True)
                weight_split(j, j, False)
            with dve.Fori(1, NE // 2) as i:
                for j in range(2):
                    tile(2 * i + j + SPLIT_FROM, True)
                    weight_split(2 * i + j, j, True)
            for t in range(SPLIT_FROM + NE, T):
                tile(t, True)
            dve.wait_ge(projection_kept, T)
            for m in range(KD):
                nc.vector.bn_stats(batch_stats[:, m, T - 2, :], h_t[:, m, (T - 2) * P:(T - 1) * P]).then_inc(batch_stats_done, 1)
            for m in range(KD):
                nc.vector.bn_stats(batch_stats[:, m, T - 1, :], h_t[:, m, (T - 1) * P:(T - 1) * P + LAST]).then_inc(batch_stats_done, 1)
            dve.wait_ge(batch_stats_done, KD * T)
            for m in range(KD):
                link(nc.vector.bn_aggr(batch_moments[:, m, :], batch_stats[:, m, :, :].rearrange("p t s -> p (t s)")))
            nc.vector.tensor_scalar(bn_v[:, :], batch_moments[:, :, 1], EPS, None, ALU.add).then_inc(batch_var_ready, 1)
            dve.wait_ge(batch_rstd_ready, 1)
            link(nc.vector.tensor_tensor(bn_a[:, :], bn_a[:, :], bcol[:, 1, :], ALU.mult))
            link(nc.vector.tensor_tensor(bn_b[:, :], batch_moments[:, :, 0], bn_a[:, :], ALU.mult))
            link(nc.vector.tensor_tensor(bn_b[:, :], bcol[:, 2, :], bn_b[:, :], ALU.subtract))
            link(nc.vector.tensor_scalar(ln_scale_plus_1[:, :], rstd[:, :], 1.0, None, ALU.add))
            link(nc.vector.tensor_tensor(ln_shift[:, :], nmean[:, :], rstd[:, :], ALU.mult))
            dve.sem_inc(bn_coeffs_ready, 1)
            dve.sem_inc(residual_may_load, 1)

            def residual(t, j, steady):
                dve.wait_ge(residual_x_loaded[j], 8 * (t - j) + 16)
                if steady:
                    dve.wait_ge(xn_ready, t - 1)
                    dve.wait_ge(biased_x1_ready, t - 1)
                nc.vector.tensor_scalar(x1[:, j, :], x_again[:, j, :], ln_scale_plus_1[:, bass.ds(t, 1)], ln_shift[:, bass.ds(t, 1)], ALU.mult, ALU.add).then_inc(scaled_x_ready, 1)
                dve.wait_ge(scaled_x_ready, t + 1)
                dve.wait_ge(gelu_turned, t + 1)
                nc.vector.tensor_tensor(x1[:, j, :], bank[j][:, :], x1[:, j, :], ALU.add).then_inc(x1_ready, 1)
                dve.wait_ge(x1_ready, t + 1)
                nc.vector.bn_stats(x1_stats[:, j, :], x1[:, j, :]).then_inc(x1_stats_done, 1)
                dve.wait_ge(x1_stats_done, t + 1)
                dve.sem_inc(pool_go, 1)
                nc.vector.bn_aggr(x1_moments[:, j, :], x1_stats[:, j, :]).then_inc(x1_moments_ready, 1)
                dve.wait_ge(x1_moments_ready, t + 1)
                nc.vector.tensor_scalar(x1_var[:, j:j + 1], x1_moments[:, j, 1:2], EPS, None, ALU.add).then_inc(x1_var_ready, 1)

            def shift(t, j):
                dve.wait_ge(x1_rstd_ready, t + 1)
                nc.vector.scalar_tensor_tensor(x1_shift[:, j:j + 1], x1_moments[:, j, 0:1], -1.0, x1_rstd[:, j:j + 1], ALU.mult, ALU.mult).then_inc(x1_shift_ready, 1)

            def low_row(t, j):
                dve.wait_ge(xn_high_ready, t + 1)
                nc.vector.scalar_tensor_tensor(xn_row[:, j, D:2 * D], xn[:, j, :], YS, xn_row[:, j, 0:D], ALU.mult, ALU.subtract).then_inc(xn_low_ready, 1)

            def keep_logits(t, j):
                dve.wait_ge(logits_summed, t + 1)
                nc.vector.tensor_copy(logits[:, bass.ds(t, 1), :], bank[4 + j][:, 0:EXPERTS].unsqueeze(1)).then_inc(logits_kept, 1)

            residual(0, 0, False)
            shift(0, 0)
            residual(1, 1, False)
            low_row(0, 0)
            shift(1, 1)
            residual(2, 0, True)
            low_row(1, 1)
            shift(2, 0)
            residual(3, 1, True)
            keep_logits(0, 0)
            low_row(2, 0)
            shift(3, 1)
            with dve.Fori(2, T // 2) as h:
                for j in range(2):
                    residual(2 * h + j, j, True)
                    keep_logits(2 * h + j - 3, 1 - j)
                    low_row(2 * h + j - 1, 1 - j)
                    shift(2 * h + j, j)
            residual(T - 1, 0, True)
            low_row(T - 2, 1)
            shift(T - 1, 0)
            low_row(T - 1, 0)
            for t in range(T - 4, T):
                keep_logits(t, t % 2)

            V = nc.vector
            full = [P, T, EXPERTS]
            over = lambda a: a.unsqueeze(2).to_broadcast(full)
            dve.wait_ge(logits_kept, T)
            dve.wait_ge(routing_consts_ready, 5)
            link(V.tensor_reduce(vec_a[:, 0, :], logits, AX.X, ALU.max))
            V.tensor_tensor(probs, logits, over(vec_a[:, 0, :]), ALU.subtract).then_inc(logits_shifted, 1)
            dve.wait_ge(probs_exp_done, 1)
            link(V.tensor_reduce(vec_a[:, 0, :], probs, AX.X, ALU.add))
            link(V.reciprocal(vec_a[:, 0, :], vec_a[:, 0, :]))
            link(V.tensor_tensor(probs, probs, over(vec_a[:, 0, :]), ALU.mult))
            for k in range(TOP):
                link(V.tensor_reduce(top_v[:, k, :], probs, AX.X, ALU.max))
                link(V.tensor_tensor(tmp_a, probs, over(top_v[:, k, :]), ALU.is_equal))
                link(V.tensor_tensor(tmp_a, tmp_a, rev16, ALU.mult))
                link(V.tensor_reduce(vec_b[:, 0, :], tmp_a, AX.X, ALU.max))
                link(V.tensor_tensor(hot[:, k], rev16, over(vec_b[:, 0, :]), ALU.is_equal))
                link(V.scalar_tensor_tensor(probs, hot[:, k], -2.0, probs, ALU.mult, ALU.add))
            link(V.tensor_tensor(tmp_a, hot[:, 0], hot[:, 1], ALU.add))
            link(V.tensor_tensor(tmp_b, hot[:, 2], hot[:, 3], ALU.add))
            V.tensor_tensor(mask16, tmp_a, tmp_b, ALU.add).then_inc(choice_mask_ready, 1)
            V.tensor_tensor(vec_a, top_v, top_v[:, 0:1, :].to_broadcast([P, TOP, T]), ALU.subtract).then_inc(top_shifted, 1)
            dve.wait_ge(ranks_summed, 1)
            HG = T * EXPERTS // 2
            flat = lambda a: a.rearrange("p t e -> p (t e)")
            for h in range(2):
                link(V.tensor_copy(flat(rank_s)[:, h * HG:(h + 1) * HG], bank[h][:, 0:HG]))
                link(V.tensor_copy(flat(cum_a)[:, h * HG:(h + 1) * HG], bank[2 + h][:, 0:HG]))
            src_c, dst_c, step = cum_a, cum_b, 1
            while step < T:
                link(V.tensor_copy(dst_c[:, 0:step, :], src_c[:, 0:step, :]))
                link(V.tensor_tensor(dst_c[:, step:T, :], src_c[:, step:T, :], src_c[:, 0:T - step, :], ALU.add))
                src_c, dst_c, step = dst_c, src_c, 2 * step
            link(V.tensor_tensor(flat(rank_s)[:, EXPERTS:], flat(rank_s)[:, EXPERTS:], flat(src_c)[:, 0:(T - 1) * EXPERTS], ALU.add))
            link(V.tensor_scalar(tot_e, src_c[:, T - 1, :], float(SB - 1), None, ALU.add))
            link(V.tensor_copy(blk_e, tot_e))
            link(V.tensor_scalar(blk_e, blk_e, 8, None, ALU.logical_shift_right))
            link(V.tensor_copy(tot_e, blk_e))
            link(V.tensor_scalar(pre_e, tot_e, 1.0, None, ALU.max))
            link(V.tensor_copy(tot_e, pre_e))
            a_e, b_e, step = pre_e, pre_e2, 1
            while step < EXPERTS:
                link(V.tensor_copy(b_e[:, 0:step], a_e[:, 0:step]))
                link(V.tensor_tensor(b_e[:, step:], a_e[:, step:], a_e[:, 0:EXPERTS - step], ALU.add))
                a_e, b_e, step = b_e, a_e, 2 * step
            link(V.tensor_tensor(b_e, a_e, tot_e, ALU.subtract))
            link(V.tensor_copy(start_f[:, 0:EXPERTS], b_e[0:1, :]))
            link(V.tensor_scalar(start_f[:, EXPERTS:EXPERTS + 2], a_e[0:1, EXPERTS - 1:EXPERTS].to_broadcast([1, 2]), 1.0, None, ALU.add))
            link(V.tensor_scalar(start_f[:, EXPERTS + 2:EXPERTS + 3], a_e[0:1, EXPERTS - 1:EXPERTS], 1.0, None, ALU.subtract))
            link(V.tensor_copy(start_i[:, :], start_f[:, :]))
            link(V.tensor_scalar(start_i[:, EXPERTS:EXPERTS + 3], start_i[:, EXPERTS:EXPERTS + 3], 1, None, ALU.logical_shift_right))
            link(V.tensor_scalar(start_i[:, EXPERTS:EXPERTS + 1], start_i[:, EXPERTS:EXPERTS + 1], 1, None, ALU.logical_shift_left))
            link(V.tensor_tensor(ebt[0:1], iota_sb[0:1, :].unsqueeze(2).to_broadcast([1, ROUTED_SB, EXPERTS]),
                                 start_f[:, 0:EXPERTS].unsqueeze(1).to_broadcast([1, ROUTED_SB, EXPERTS]), ALU.is_ge))
            link(V.tensor_reduce(iota_sb[0:1, :], ebt[0:1], AX.X, ALU.add))
            link(V.tensor_scalar(expert_of_block[:, :], iota_sb[0:1, :], 1.0, None, ALU.subtract))
            link(V.scalar_tensor_tensor(rank_s, b_e.unsqueeze(1).to_broadcast(full), float(SB), rank_s, ALU.mult, ALU.add))
            for k in range(TOP):
                link(V.tensor_tensor(tmp_a, hot[:, k], rank_s, ALU.mult))
                link(V.tensor_reduce(place_row[:, :, k], tmp_a, AX.X, ALU.add))
            link(V.tensor_copy(slot_i, place_row))
            ti = tmp_b.rearrange("p t e -> p (t e)")[:, 0:T * TOP].bitcast(I32).rearrange("p (t k) -> p t k", k=TOP)
            link(V.tensor_scalar(ti, slot_i, 7, None, ALU.logical_shift_right))
            link(V.tensor_copy(place_block, ti))
            link(V.tensor_scalar(ti, slot_i, P - 1, None, ALU.bitwise_and))
            link(V.tensor_copy(place_row, ti))
            dve.wait_ge(top_exp_done, 1)
            link(V.tensor_tensor(vec_b[:, 0, :], vec_a[:, 0, :], vec_a[:, 1, :], ALU.add))
            link(V.tensor_tensor(vec_b[:, 1, :], vec_a[:, 2, :], vec_a[:, 3, :], ALU.add))
            link(V.tensor_tensor(vec_b[:, 0, :], vec_b[:, 0, :], vec_b[:, 1, :], ALU.add))
            link(V.reciprocal(vec_b[:, 0, :], vec_b[:, 0, :]))
            link(V.tensor_tensor(choice_weight, vec_a.rearrange("p k t -> p t k"), vec_b[:, 0, :].unsqueeze(2).to_broadcast([P, T, TOP]), ALU.mult))

            def places(t, g, wait):
                for k in range(TOP):
                    if wait:
                        dve.wait_ge(place_onehots_used, t * TOP + k + 1 - TOP)
                    nc.vector.tensor_scalar(oh_r[:, k, :], iota16[:, :], place_row[:, bass.ds(t, 1), k:k + 1].rearrange("p a k -> p (a k)"), None, ALU.is_equal)
                    nc.vector.tensor_scalar(oh_b[:, k, :], iota_b, place_block[:, bass.ds(t, 1), k:k + 1].rearrange("p a k -> p (a k)"),
                                            vcol[:, bass.ds(t - g * TG, 1)], ALU.is_equal, ALU.mult).then_inc(place_onehots_ready, 1)

            places(0, 0, False)
            for g in range(GROUPS):
                with dve.Fori(max(1, g * TG), min(T, (g + 1) * TG)) as t:
                    places(t, g, True)
            dve.wait_ge(place_onehots_used, T * TOP + 1)
            grp_ps = [bank[4 + g // 2][:, g % 2 * RB:(g % 2 + 1) * RB] for g in range(GROUPS)]
            tok_v, tok_g = token_of_place_f[:, 0:RB], tmp_a.rearrange("p t e -> p (t e)")[:, 0:RB]
            link(V.tensor_scalar(tok_v, grp_ps[0], 1.0, None, ALU.subtract))
            for g in range(1, GROUPS):
                link(V.tensor_tensor(tok_v, grp_ps[g], tok_v, ALU.add))
                link(V.tensor_scalar(tok_g, grp_ps[g], 0.0, float(g * TG * P), ALU.is_gt, ALU.mult))
                link(V.tensor_tensor(tok_v, tok_v, tok_g, ALU.add))
            link(V.tensor_scalar(token_of_place_f, token_of_place_f, 0.0, float(NP - 1), ALU.max, ALU.min))
            link(V.tensor_copy(token_of_place, token_of_place_f))
            dve.sem_inc(tokens_by_place_ready, 1)

            def take_rows(b, j, q, wait=True):
                dve.wait_ge(xrows_gathered[j][q], 8 * (b - j) + 16)
                if wait:
                    dve.wait_ge(xrows_turned, 2 * b + q)
                nc.vector.tensor_copy(taken_rows[:, q, :], gathered_rows[:, j, q, :]).then_inc(xrows_taken, 1)

            def low_x(b, q):
                dve.wait_ge(xrows_turned, 2 * b + q + 2)
                if q == 0:
                    dve.wait_ge(first_layer_summed, KH * b + 1)
                nc.vector.tensor_copy(x_hl[:, q, 1], turned[q][1]).then_inc(x_parts_ready, 1)

            def hidden(b, m):
                dve.wait_ge(hidden_high_ready, 2 * b + m + 1)
                nc.vector.scalar_tensor_tensor(hidden_lo[:, m, :], hidden_f32[:, m, :], scale_h, hidden_hi[:, m, :], ALU.mult, ALU.subtract).then_inc(hidden_low_ready, 1)

            def results(b, j, wait):
                e = dve.value_load(expert_of_block[0:1, bass.ds(b, 1)], min_val=0, max_val=EXPERTS - 1)
                dve.wait_ge(second_layer_summed, b + 1)
                if wait:
                    dve.wait_ge(results_stored[j], 8 * (b - j))
                else:
                    dve.wait_ge(b2_loaded, 16)
                for q in range(2):
                    nc.vector.scalar_tensor_tensor(result_rows[:, j, q, :].unsqueeze(1), bank[4 + q][:, :].unsqueeze(1), unscale_2, b2_rows[:, bass.ds(e, 1), :], ALU.mult, ALU.add).then_inc(results_ready, 1)

            dve.sem_inc(first_layer_summed, 1)
            link(V.tensor_scalar(half_unscale, unscale_2, 1.0 / SHARED, None, ALU.mult))
            dve.sem_inc(xrows_taken, 4)
            def step(b, j, wait):
                for m in range(KH):
                    hidden(b, m)
                    low_x(b + 1, m)
                for q in range(2):
                    take_rows(b + 2, j, q)
                results(b, j, wait)

            for q in range(2):
                take_rows(0, 0, q, False)
            for q in range(2):
                low_x(0, q)
            for q in range(2):
                take_rows(1, 1, q)
            for b in range(2):
                step(b, b, False)
            pairs = dve.value_load(start_i[0:1, EXPERTS + 1:EXPERTS + 2], min_val=EXPERTS // 2, max_val=ROUTED_SB // 2)
            with dve.Fori(1, pairs) as h:
                for j in range(2):
                    step(2 * h + j, j, True)

            def low_s(s, nq):
                for q in range(nq):
                    dve.wait_ge(shared_rows_turned, 2 * s + q + 1)
                    nc.vector.tensor_copy(x_hl[:, q, 1], turned[q][1]).then_inc(shared_x_parts_ready, 1)

            def hidden_s(s, units, nq):
                for u in units:
                    dve.wait_ge(shared_high_ready, UNITS * s + u + 1)
                    nc.vector.scalar_tensor_tensor(shared_hidden_lo[:, u, 0:nq * P], shared_hidden[:, u, 0:nq * P], scale_h, shared_hidden_hi[:, u, 0:nq * P], ALU.mult, ALU.subtract).then_inc(shared_low_ready, 1)

            def base(s, nq, wait):
                dve.wait_ge(shared_second_layer_summed, s + 1)
                for q in range(nq):
                    dve.wait_ge(x1_loaded[q], 16 * s + 16)
                    if wait:
                        dve.wait_ge(out_stored[q], 16 * s)
                    V.scalar_tensor_tensor(acc[:, q, :], bank[4 + q][:, :], half_unscale, x1r[:, q, :], ALU.mult, ALU.add).then_inc(base_sum_ready, 1)

            def choices(s, q):
                t = 2 * s + q
                dve.wait_ge(choices_gathered[q], 64 * s + 64)
                dve.wait_ge(base_sum_ready, t + 3)
                for k in range(TOP):
                    if k:
                        dve.wait_ge(choice_added, TOP * t + k)
                    V.scalar_tensor_tensor(acc[:, q, :], choice_rows[:, q, k, :], choice_weight[:, bass.ds(t, 1), k:k + 1].rearrange("p a k -> p (a k)"), acc[:, q, :],
                                           ALU.mult, ALU.add).then_inc(choice_added, 1)

            def step_s(s, nq, next_nq, wait):
                base(s - 1, 2, wait)
                choices(s - 1, 0)
                hidden_s(s, range(0, KH), nq)
                choices(s - 1, 1)
                hidden_s(s, range(KH, UNITS), nq)
                low_s(s + 1, next_nq)

            low_s(0, 2)
            hidden_s(0, range(UNITS), 2)
            low_s(1, 2)
            step_s(1, 2, 2, False)
            with dve.Fori(2, SHARED_SB - 2) as s:
                step_s(s, 2, 2, True)
            step_s(SHARED_SB - 2, 2, 1, True)
            step_s(SHARED_SB - 1, 1, 0, True)
            base(SHARED_SB - 1, 1, True)
            choices(SHARED_SB - 1, 0)

        @block.scalar
        def _(act):
            def x_row(t):
                return x_all[:, bass.ds(t, 1), :].rearrange("p a d -> p (a d)")

            def row_sums(func, sums, counted, bias=None, loads=None):
                for g in range(GRP):
                    if loads:
                        act.wait_ge(loads[g], 16)
                    if g >= 2:
                        act.wait_ge(counted, (g - 1) * GRP)
                    with act.Fori(g * GRP, (g + 1) * GRP) as t:
                        b = 0.0 if bias is None else bias[:, bass.ds(t, 1)]
                        nc.scalar.activation(spare_rows[:, bass.ds(t - g * GRP + g % 2 * GRP, 1), :].rearrange("p a d -> p (a d)"), x_row(t), func, bias=b,
                                             accum_out=sums[:, bass.ds(t, 1)]).then_inc(counted, 1)

            row_sums(ACT.Identity, sum_x, row_sums_done, loads=x_loaded)
            act.wait_ge(row_sums_done, T)
            nc.scalar.activation(nmean[:, :], sum_x[:, :], ACT.Copy, scale=-1.0 / D).then_inc(neg_mean_ready, 1)
            act.wait_ge(neg_mean_ready, 1)
            row_sums(ACT.Square, ssq, row_squares_done, bias=nmean)

            act.wait_ge(row_scales_ready, 1)

            def rows_hi(g, k):
                t = g * GRP + k
                row = x_all[:, bass.ds(t, 1), :].rearrange("p a d -> p (a d)")
                nc.scalar.activation(yrow[:, k, 0:D], row, ACT.Identity, bias=row_shift[:, bass.ds(t, 1)], scale=row_scale[:, bass.ds(t, 1)]).then_inc(row_high_ready, 1)
                if k < Z_ACT:
                    nc.scalar.activation(z[:, k, :], row, ACT.Identity, bias=row_shift[:, bass.ds(t, 1)], scale=row_scale[:, bass.ds(t, 1)]).then_inc(z_by_scalar, 1)

            for k in range(GRP):
                rows_hi(0, k)
            with act.Fori(1, GRP) as g:
                for k in range(GRP):
                    act.wait_ge(row_stored[k], g * 16)
                    act.wait_ge(row_low_ready, g * GRP + k + 1 - GRP)
                    rows_hi(g, k)
            act.wait_ge(gnn_params_loaded, 64)

            yv = ytab.rearrange("(t p) d -> p t d", p=P)
            act.wait_ge(row_table_complete, 1)
            act.dma_start(yself[:, :], yv[:, 0:1, :]).then_inc(own_rows_loaded, 16)

            def finish_tile(t, par, more=True):
                act.wait_ge(tile_summed, t + 2)
                if more:
                    act.dma_start(yself[:, :], yv[:, bass.ds(t + 1, 1), :]).then_inc(own_rows_loaded, 16)
                act.wait_ge(tile_sum_turned, t + 1)
                nc.scalar.activation(tile_sum[:, :], sum_bank[par][:, :], ACT.Copy, scale=dinv_ys[:, bass.ds(t, 1)]).then_inc(tile_sum_kept, 1)
                act.wait_ge(tile_sum_turned, t + 2)
                nc.scalar.activation(tile_sum_t[:, :, :], sum_t_ps[:, :, :], ACT.Copy).then_inc(turned_sum_kept, 1)
                act.wait_ge(tile_projected, t + 1)
                for m in range(KD):
                    ins = nc.scalar.activation(h_t[:, m, bass.ds(t * P, P)], proj_ps[:, m, :], ACT.Identity, bias=bcol[:, 0, m:m + 1])
                ins.then_inc(projection_kept, 1)

            finish_tile(0, 0)
            with act.Fori(0, T // 2 - 1) as h:
                finish_tile(2 * h + 1, 1)
                finish_tile(2 * h + 2, 0)
            finish_tile(T - 2, 1)
            finish_tile(T - 1, 0, more=False)

            act.wait_ge(bn_coeffs_ready, 1)
            def gelu_tile(t, j, steady):
                if steady:
                    act.wait_ge(gelu_turned, t - 1)
                for m in range(KD):
                    last = nc.scalar.activation(g_tile[:, j, m, :], h_t[:, m, bass.ds(t * P, P)], ACT.Gelu, bias=bn_b[:, m:m + 1], scale=bn_a[:, m:m + 1])
                last.then_inc(gelu_ready, 1)

            def norm_row(t, j, steady):
                act.wait_ge(x1_shift_ready, t + 1)
                if steady:
                    act.wait_ge(xn_turned, t - 1)
                    act.wait_ge(xn_low_ready, t - 1)
                nc.scalar.activation(xn[:, j, :], x1[:, j, :], ACT.Identity, bias=x1_shift[:, j:j + 1], scale=x1_rstd[:, j:j + 1]).then_inc(xn_ready, 1)
                if steady:
                    act.wait_ge(xn_stored[j], 8 * (t - j))
                act.wait_ge(xn_ready, t + 1)
                nc.scalar.activation(xn_row[:, j, 0:D], xn[:, j, :], ACT.Copy, scale=YS).then_inc(xn_high_ready, 1)

            def keep_turned(t, j, steady):
                act.wait_ge(xn_turned, t + 1)
                if steady:
                    act.wait_ge(logits_summed, t - 1)
                nc.scalar.activation(xn_t[:, j], cut(2 + j, KD), ACT.Copy).then_inc(turned_xn_kept, 1)

            gelu_tile(0, 0, False)
            gelu_tile(1, 1, False)
            norm_row(0, 0, False)
            gelu_tile(2, 0, True)
            norm_row(1, 1, False)
            keep_turned(0, 0, False)
            gelu_tile(3, 1, True)
            norm_row(2, 0, True)
            keep_turned(1, 1, False)
            with act.Fori(2, T // 2) as h:
                for j in range(2):
                    gelu_tile(2 * h + j, j, True)
                    norm_row(2 * h + j - 1, 1 - j, True)
                    keep_turned(2 * h + j - 2, j, True)
            gelu_tile(T - 1, 0, True)
            norm_row(T - 2, 1, True)
            keep_turned(T - 3, 0, True)
            norm_row(T - 1, 0, True)
            keep_turned(T - 2, 1, True)
            keep_turned(T - 1, 0, True)

            act.wait_ge(logits_shifted, 1)
            nc.scalar.activation(probs, probs, ACT.Exp).then_inc(probs_exp_done, 1)
            act.wait_ge(top_shifted, 1)
            nc.scalar.activation(vec_a, vec_a, ACT.Exp).then_inc(top_exp_done, 1)

            def high_x(b):
                for q in range(2):
                    act.wait_ge(xrows_turned, 2 * b + q + 2)
                    if q == 0:
                        act.wait_ge(first_layer_summed, KH * b + 1)
                    nc.scalar.activation(x_hl[:, q, 0], turned[q][0], ACT.Copy).then_inc(x_parts_ready, 1)

            def store_y(b, j):
                act.wait_ge(results_ready, 2 * b + 4)
                act.dma_start(btab[bass.ds(b * SB, SB), :].rearrange("(q p) d -> p q d", q=2), result_rows[:, j, :, :]).then_inc(results_stored[j], 16)

            def gelu(b, j, first=False):
                e = act.value_load(expert_of_block[0:1, bass.ds(b, 1)], min_val=0, max_val=EXPERTS - 1)
                for m in range(KH):
                    act.wait_ge(first_layer_summed, 2 * b + m + 2)
                    if not first:
                        act.wait_ge(hidden_low_ready, 2 * b + m - 1)
                    nc.scalar.activation(hidden_f32[:, m, :], bank[2 + m][:, 0:SB], ACT.Gelu, bias=b1_cols_sb[:, bass.ds(e * KH + m, 1)], scale=unscale_1).then_inc(hidden_gelu_done, 1)
                    act.wait_ge(hidden_gelu_done, 2 * b + m + 3)
                    if m == 0 and not first:
                        act.wait_ge(second_layer_summed, b)
                    nc.scalar.activation(hidden_hi[:, m, :], hidden_f32[:, m, :], ACT.Copy, scale=scale_h).then_inc(hidden_high_ready, 1)
                    if m == 0 and not first:
                        store_y(b - 1, 1 - j)

            act.sem_inc(hidden_gelu_done, 2)
            act.wait_ge(tokens_by_place_ready, 1)
            high_x(0)
            gelu(0, 0, first=True)
            high_x(1)
            gelu(1, 1)
            high_x(2)
            pairs = act.value_load(start_i[0:1, EXPERTS + 1:EXPERTS + 2], min_val=EXPERTS // 2, max_val=ROUTED_SB // 2)
            with act.Fori(1, pairs) as h:
                for j in range(2):
                    gelu(2 * h + j, j)
                    high_x(2 * h + j + 1)
            last_pair = act.value_load(start_i[0:1, EXPERTS + 2:EXPERTS + 3], min_val=EXPERTS // 2 - 1, max_val=ROUTED_SB // 2 - 1)
            store_y(last_pair * 2 + 1, 1)

            def high_s(s, nq):
                for q in range(nq):
                    act.wait_ge(shared_rows_turned, 2 * s + q + 1)
                    nc.scalar.activation(x_hl[:, q, 0], turned[q][0], ACT.Copy).then_inc(shared_x_parts_ready, 1)

            def gelu_s(s, nq, wait=True):
                for u in range(UNITS):
                    act.wait_ge(shared_first_layer_summed, UNITS * s + u + 1)
                    nc.scalar.activation(shared_hidden[:, u, 0:nq * P], bank[2 + u % 2][:, 0:nq * P], ACT.Gelu,
                                         bias=b1_cols_sb[:, EXPERTS * KH + u:EXPERTS * KH + u + 1], scale=unscale_1).then_inc(shared_gelu_done, 1)
                    act.wait_ge(shared_gelu_done, UNITS * s + u + 3)
                    if u == 0 and wait:
                        act.wait_ge(shared_second_layer_summed, s)
                    nc.scalar.activation(shared_hidden_hi[:, u, 0:nq * P], shared_hidden[:, u, 0:nq * P], ACT.Copy, scale=scale_h).then_inc(shared_high_ready, 1)

            act.sem_inc(shared_gelu_done, 2)
            high_s(0, 2)
            gelu_s(0, 2, False)
            high_s(1, 2)
            with act.Fori(1, SHARED_SB - 2) as s:
                gelu_s(s, 2)
                high_s(s + 1, 2)
            gelu_s(SHARED_SB - 2, 2)
            high_s(SHARED_SB - 1, 1)
            gelu_s(SHARED_SB - 1, 1)

        @block.tensor
        def _(pe):
            pe.wait_ge(consts_ready, 13)
            nc.tensor.matmul(deg_ps[:, 0:T], ones[0:1, 0:P], ones[0:1, 0:T], start=True, stop=False)
            with pe.Fori(0, NB // 2) as i:
                for k in range(2):
                    pe.wait_ge(onehots_ready, 4 * i + 2 * k + 2)
                    for c in range(OH):
                        mm = nc.tensor.matmul(deg_ps[:, 0:T], oh_l[:, k, :, c], oh_h[:, k, :, c], start=False, stop=False)
                    mm.then_inc(onehots_used, 1)
            nc.tensor.matmul(deg_ps[:, 0:T], zero16[:, 0:P], zero16[:, 0:T], start=False, stop=True).then_inc(degrees_summed, 1)
            pe.wait_ge(chunk_bounds_ready, 1)
            for a in range(2):
                mm = nc.tensor.transpose(bounds_ps[0:T, a * CPART:(a + 1) * CPART], bounds[:, a, :], ident[0:CPART, 0:CPART])
            mm.then_inc(chunk_bounds_turned, 1)
            pe.wait_ge(tile_ranges_ready, 1)
            nc.tensor.matmul(bounds_ps[0:1, 256:256 + T], range_col[:, 2:3], ident[0:T, 0:T], start=True, stop=True)
            nc.tensor.matmul(bounds_ps[0:1, 256 + T:256 + 2 * T], range_col[:, 3:4], ident[0:T, 0:T], start=True, stop=True)
            nc.tensor.matmul(bounds_ps[0:1, 256 + 2 * T:256 + 3 * T], range_col[:, 4:5], upper[:, :], start=True, stop=True)
            nc.tensor.matmul(bounds_ps[0:1, 256 + 3 * T:257 + 3 * T], range_col[:, 4:5], ones[0:T, 0:1], start=True, stop=True).then_inc(tile_range_rows_ready, 1)

            pe.wait_ge(range_table_ready, 1)
            pe.wait_ge(row_table_complete, 1)
            pe.wait_ge(gnn_params_loaded, 64)
            pe.sem_inc(tile_summed, 1)
            pe.sem_inc(rows_summed, RING + CPAD)

            def gather_sum(t, par):
                lo = pe.value_load(tab[0:1, 0, bass.ds(t, 1)], min_val=0, max_val=CPAD - 2)
                hi = pe.value_load(tab[0:1, 1, bass.ds(t, 1)], min_val=0, max_val=CPAD - 2)
                off = pe.value_load(tab[0:1, 2, bass.ds(t, 1)], min_val=0, max_val=T * CPAD + CPAD)
                pe.wait_ge(tile_sum_kept, t + 1)
                nc.tensor.matmul(sum_bank[par][:, :], zero16[:, 0:P], zero16[:, 0:D], start=True, stop=False)
                with pe.Fori(lo, hi, 2) as c:
                    s = pe.snap(c + off)
                    pe.wait_ge(rows_landed, s + 2)
                    slot = even_slot(pe.snap(s % RING))
                    for q in range(2):
                        w = sel_flat[:, bass.ds(slot * P + q * P, P)]
                        for part in range(2):
                            mm = nc.tensor.matmul(sum_bank[par][:, :], w, rows_flat[:, bass.ds(slot * (2 * D) + (2 * q + part) * D, D)], start=False, stop=False)
                        mm.then_inc(rows_summed, 1)
                pe.wait_ge(own_rows_loaded, 16 * t + 16)
                nc.tensor.matmul(sum_bank[par][:, :], ident16[:, :], yself[:, 0:D], start=False, stop=False)
                nc.tensor.matmul(sum_bank[par][:, :], ident16[:, :], yself[:, D:2 * D], start=False, stop=True).then_inc(tile_summed, 1)

            def turn(t):
                pe.wait_ge(tile_sum_kept, t + 3)
                for k in range(KD):
                    mm = nc.tensor.transpose(sum_t_ps[:, k, :], tile_sum[:, k * P:(k + 1) * P], ident[:, :])
                mm.then_inc(tile_sum_turned, 1)

            def project(t):
                pe.wait_ge(turned_sum_kept, t + 1)
                for m in range(KD):
                    for k in range(KD):
                        mm = nc.tensor.matmul(proj_ps[:, m, :], w_sb[:, k, m * P:(m + 1) * P], tile_sum_t[:, k, :], start=(k == 0), stop=(k == KD - 1))
                mm.then_inc(tile_projected, 1)

            pe.sem_inc(tile_sum_kept, 2)
            pe.sem_inc(tile_sum_turned, 1)
            gather_sum(0, 0)
            def pair(h):
                for j in range(2):
                    gather_sum(2 * h + j + 1, (j + 1) % 2)
                    turn(2 * h + j)
                    project(2 * h + j)

            with pe.Fori(0, (MAX_FROM + NE) // 2) as h:
                pair(h)
            pe.wait_ge(maxima_ready, 1)
            for q in range(3):
                mm = nc.tensor.transpose(max_ps[:, q, :], max_rows[:, q, :], ident[:, :])
            mm.then_inc(maxima_turned, 1)
            with pe.Fori((MAX_FROM + NE) // 2, T // 2) as h:
                pair(h)
            turn(T - 1)
            project(T - 1)

            pe.wait_ge(gate_loaded, 16)

            def turn_gelu(t, j, steady):
                pe.wait_ge(gelu_ready, t + 1)
                if steady:
                    pe.wait_ge(x1_ready, t - 1)
                for m in range(KD):
                    mm = nc.tensor.transpose(bank[j][:, m * P:(m + 1) * P], g_tile[:, j, m, :], ident[:, :])
                mm.then_inc(gelu_turned, 1)

            def turn_norm(t, j, steady):
                pe.wait_ge(xn_ready, t + 1)
                if steady:
                    pe.wait_ge(turned_xn_kept, t - 1)
                for m in range(KD):
                    mm = nc.tensor.transpose(bank[2 + j][:, m * P:(m + 1) * P], xn[:, j, m * P:(m + 1) * P], ident[:, :])
                mm.then_inc(xn_turned, 1)

            def gate_logits(t, j, steady):
                pe.wait_ge(turned_xn_kept, t + 1)
                if steady:
                    pe.wait_ge(logits_kept, t - 1)
                for m in range(KD):
                    mm = nc.tensor.matmul(bank[4 + j][:, 0:EXPERTS], xn_t[:, j, m, :], gate[:, m, :], start=(m == 0), stop=(m == KD - 1))
                mm.then_inc(logits_summed, 1)

            turn_gelu(0, 0, False)
            turn_gelu(1, 1, False)
            turn_norm(0, 0, False)
            turn_gelu(2, 0, True)
            turn_norm(1, 1, False)
            gate_logits(0, 0, False)
            turn_gelu(3, 1, True)
            turn_norm(2, 0, True)
            gate_logits(1, 1, False)
            with pe.Fori(2, T // 2) as h:
                for j in range(2):
                    turn_gelu(2 * h + j, j, True)
                    turn_norm(2 * h + j - 1, 1 - j, True)
                    gate_logits(2 * h + j - 2, j, True)
            turn_gelu(T - 1, 0, True)
            turn_norm(T - 2, 1, True)
            gate_logits(T - 3, 0, True)
            turn_norm(T - 1, 0, True)
            gate_logits(T - 2, 1, True)
            gate_logits(T - 1, 0, True)

            pe.wait_ge(choice_mask_ready, 1)
            mflat = mask16.rearrange("p t e -> p (t e)")
            HG = T * EXPERTS // 2
            for h in range(2):
                nc.tensor.matmul(bank[h][:, 0:HG], upper16[:, :], mflat[:, h * HG:(h + 1) * HG], start=True, stop=True)
                mm = nc.tensor.matmul(bank[2 + h][:, 0:HG], ones16[:, :], mflat[:, h * HG:(h + 1) * HG], start=True, stop=True)
            mm.then_inc(ranks_summed, 1)
            for c in range(2):
                nc.tensor.matmul(bank[4 + c][:, 0:2 * RB], zero16[:, 0:P], zero16[:, 0:2 * RB], start=True, stop=False)
            for g in range(GROUPS):
                o = bank[4 + g // 2][:, g % 2 * RB:(g % 2 + 1) * RB]
                with pe.Fori(g * TG, min(T, (g + 1) * TG)) as t:
                    for k in range(TOP):
                        pe.wait_ge(place_onehots_ready, t * TOP + k + 1)
                        nc.tensor.matmul(o, oh_r[:, k, :], oh_b[:, k, :], start=False, stop=False).then_inc(place_onehots_used, 1)
            for c in range(2):
                mm = nc.tensor.matmul(bank[4 + c][:, 0:2 * RB], zero16[:, 0:P], zero16[:, 0:2 * RB], start=False, stop=True)
            mm.then_inc(place_onehots_used, 1)

            def turn(dst, src):
                for u in range(2):
                    for m in range(KD):
                        mm = nc.tensor.transpose(dst[u][:, m, :], src[:, u * D + m * P:u * D + (m + 1) * P], ident16[:, :])
                return mm

            def turn_rows(b, q):
                turn(turned[q], taken_rows[:, q, :]).then_inc(xrows_turned, 1)

            def halves(w):
                return (expert_weights[:, w, 0:2 * WL].rearrange("p (s k n) -> p s k n", s=2, k=KD),
                        expert_weights[:, w, 2 * WL:4 * WL].rearrange("p (s k n) -> p s k n", s=2, k=KH))

            def first_layer(o, w1_parts, m, nq):
                for k in range(KD):
                    for u, v in ((0, 0), (0, 1), (1, 0)):
                        mm = nc.tensor.matmul(o, w1_parts[:, u, k, m * P:(m + 1) * P], x_hl[:, 0:nq, v, k, :], start=(k == 0 and u == 0 and v == 0),
                                              stop=(k == KD - 1 and u == 1))
                return mm

            def superblock(b, w):
                W1, W2 = halves(w)
                pe.wait_ge(x_parts_ready, 4 * b + 4)
                for m in range(KH):
                    first_layer(bank[2 + m][:, 0:SB].rearrange("p (q n) -> p q n", q=2), W1, m, 2).then_inc(first_layer_summed, 1)
                pe.wait_ge(xrows_taken, 2 * b + 8)
                for q in range(2):
                    turn_rows(b + 1, q)
                for m in range(KH):
                    pe.wait_ge(hidden_low_ready, 2 * b + m + 1)
                    for q in range(2):
                        for u, v in ((0, hidden_hi), (0, hidden_lo), (1, hidden_hi)):
                            mm = nc.tensor.matmul(bank[4 + q][:, :], v[:, m, q * P:(q + 1) * P], W2[:, u, m, :], start=(m == 0 and u == 0 and v is hidden_hi),
                                                  stop=(m == KH - 1 and u == 1))
                mm.then_inc(second_layer_summed, 1)

            pe.wait_ge(tokens_by_place_ready, 1)
            pe.sem_inc(results_ready, 2)
            pe.sem_inc(xrows_turned, 1)
            pe.wait_ge(xrows_taken, 6)
            for q in range(2):
                turn_rows(0, q)
            with pe.Fori(0, EXPERTS // 2) as i:
                for w in range(2):
                    pe.wait_ge(expert_weights_loaded[w], 16 * i + 16)
                    pe.sem_inc(pool_go, 1)
                    b_from = pe.value_load(start_i[0:1, bass.ds(2 * i + w, 1)], min_val=0, max_val=ROUTED_SB)
                    b_to = pe.value_load(start_i[0:1, bass.ds(2 * i + w + 1, 1)], min_val=1, max_val=ROUTED_SB)
                    with pe.Fori(b_from, b_to) as b:
                        superblock(b, w)

            def turn_s(s, w, q):
                turn(turned[q], shared_rows[:, w, q, :]).then_inc(shared_rows_turned, 1)

            def shared_block(s, w, nq, next_nq):
                pe.wait_ge(shared_x_parts_ready, 4 * s + 2 * nq)
                for u in range(UNITS):
                    if u >= 2:
                        pe.wait_ge(shared_gelu_done, UNITS * s + u + 1)
                    o = bank[2 + u % 2][:, 0:nq * P].rearrange("p (q n) -> p q n", q=nq)
                    first_layer(o, halves(u // KH)[0], u % KH, nq).then_inc(shared_first_layer_summed, 1)
                if next_nq:
                    pe.wait_ge(shared_rows_loaded[1 - w], 8 * (s + 1 - (1 - w)) + 16)
                    for q in range(next_nq):
                        turn_s(s + 1, 1 - w, q)
                for u in range(UNITS):
                    W2 = halves(u // KH)[1]
                    pe.wait_ge(shared_low_ready, UNITS * s + u + 1)
                    for q in range(nq):
                        for part, v in ((0, shared_hidden_hi), (0, shared_hidden_lo), (1, shared_hidden_hi)):
                            mm = nc.tensor.matmul(bank[4 + q][:, :], v[:, u, q * P:(q + 1) * P], W2[:, part, u % KH, :], start=(u == 0 and part == 0 and v is shared_hidden_hi),
                                                  stop=(u == UNITS - 1 and part == 1))
                mm.then_inc(shared_second_layer_summed, 1)

            pe.sem_inc(pool_go, 1)
            blocks = pe.value_load(start_i[0:1, EXPERTS:EXPERTS + 1], min_val=EXPERTS, max_val=ROUTED_SB)
            pe.wait_ge(x_parts_ready, blocks * 4 + 4)
            pe.wait_ge(hidden_gelu_done, blocks * KH + 2)
            pe.wait_ge(results_ready, blocks * 2 + 2)
            for w in range(2):
                pe.wait_ge(expert_weights_loaded[w], 16 * (NE // 2))
            pe.sem_inc(base_sum_ready, 2)
            pe.wait_ge(shared_rows_loaded[0], 16)
            for q in range(2):
                turn_s(0, 0, q)
            with pe.Fori(0, SHARED_SB // 2 - 1) as h:
                for w in range(2):
                    shared_block(2 * h + w, w, 2, 2)
            shared_block(SHARED_SB - 3, 0, 2, 2)
            shared_block(SHARED_SB - 2, 1, 2, 1)
            shared_block(SHARED_SB - 1, 0, 1, 0)


def kernel(x, src, dst, L0_gnn_W, L0_gnn_b, L0_gnn_gamma, L0_gnn_beta, L0_ffn_gate_w, L0_ffn_re_w1, L0_ffn_re_b1, L0_ffn_re_w2, L0_ffn_re_b2, L0_ffn_se_w1, L0_ffn_se_b1, L0_ffn_se_w2, L0_ffn_se_b2):
    import numpy as np
    import concourse.bacc as bacc
    from concourse.bass_utils import run_bass_kernel_spmd

    nc = bacc.Bacc("TRN2", target_bir_lowering=False, num_devices=1)
    edges = CPAD * P - EDGES
    dst_rows = np.pad(np.asarray(dst), (0, edges), constant_values=NP).reshape(CPAD, P)
    src_rows = np.pad(np.asarray(src), (0, edges)).reshape(CPAD, P)
    laid = {
        "x": np.pad(np.asarray(x), ((0, NP - N), (0, 0))),
        "src_cols": src_rows.T, "dst_cols": dst_rows.T, "dst_rows": dst_rows,
        "w_t": np.asarray(L0_gnn_W).T,
        "b_cols": np.asarray(L0_gnn_b).reshape(KD, P).T,
        "gamma_cols": np.asarray(L0_gnn_gamma).reshape(KD, P).T,
        "beta_cols": np.asarray(L0_gnn_beta).reshape(KD, P).T,
        "gate_t": np.asarray(L0_ffn_gate_w).T,
        "w1": np.concatenate([np.asarray(L0_ffn_re_w1), np.asarray(L0_ffn_se_w1)]),
        "b1_cols": np.concatenate([np.asarray(L0_ffn_re_b1), np.asarray(L0_ffn_se_b1)]).reshape(NE * KH, P).T,
        "w2": np.concatenate([np.asarray(L0_ffn_re_w2), np.asarray(L0_ffn_se_w2)]),
        "b2": np.concatenate([np.asarray(L0_ffn_re_b2), np.asarray(L0_ffn_se_b2)]),
    }
    arrays, args = {}, []
    for name, a in laid.items():
        a = np.ascontiguousarray(a)
        arrays[f"in_{name}"] = a
        args.append(nc.dram_tensor(f"in_{name}", a.shape, mybir.dt.from_np(a.dtype), kind="ExternalInput").ap())
    args.append(nc.dram_tensor("out_x", (NP, D), F32, kind="ExternalOutput").ap())
    gnn_ffn(nc, *args)
    r = run_bass_kernel_spmd(nc, [arrays], core_ids=[0])
    return r.results[0]["out_x"][:N]
```
